# Optimizing a Trainium2 kernel written in Bass

```python
import numpy as np
import jax
import jax.numpy as jnp

def _softmax(x, axis=-1):
    return jax.nn.softmax(x, axis=axis)

def _gelu(x):
    return jax.nn.gelu(x, approximate=True)

def _silu(x):
    return jax.nn.silu(x)

def _sigmoid(x):
    return jax.nn.sigmoid(x)

def _layernorm(x, axis=-1, eps=1e-05):
    m = jnp.mean(x, axis=axis, keepdims=True)
    v = jnp.var(x, axis=axis, keepdims=True)
    return (x - m) / jnp.sqrt(v + eps)

def _scatter_add(tgt, idx, src, axis=0):
    return tgt.at[idx].add(src)

def _segment_sum(src, seg, n):
    return jax.ops.segment_sum(src, seg, n)
kernel_name = 'mk_metaformer_d4_conv_nchw512_r4_8f98a1'

def setup_inputs(seed: int=0):
    np.random.seed(seed)
    _w = jnp.asarray

    def _rec_inputs():
        import jax
        import jax.numpy as jnp
        _gk = jax.random.key(seed)
        x = -0.0006537 + 1.001 * jax.random.normal(jax.random.fold_in(_gk, 1), (2, 128, 48, 48), jnp.float32)
        return x
    x = _rec_inputs()

    def _L0_conv_setup():
        import jax, jax.numpy as jnp
        import numpy as np
        D_MODEL = 128
        D_HEAD = 16
        N_HEADS = D_MODEL // D_HEAD
        KS = 7
        GROUPS = 16
        GN_EPS = 1e-05
        COS_EPS = 1e-06

        def conv3x3(x, w, b):
            y = jax.lax.conv_general_dilated(x, w, window_strides=(1, 1), padding='SAME', dimension_numbers=('NCHW', 'OIHW', 'NCHW'))
            return y + b[None, :, None, None]

        def group_norm(x, gamma, beta):
            B, C, H, W = x.shape
            xr = x.reshape(B, GROUPS, -1)
            mean = jnp.mean(xr, axis=-1, keepdims=True)
            var = jnp.var(xr, axis=-1, keepdims=True)
            xn = ((xr - mean) * jax.lax.rsqrt(var + GN_EPS)).reshape(B, C, H, W)
            return xn * gamma[None, :, None, None] + beta[None, :, None, None]

        def cosine_scale(t, scale_h):
            s = scale_h.astype(jnp.float32)[None, None, None, :, None]
            ssq = jnp.sum(t.astype(jnp.float32) ** 2, axis=-1, keepdims=True)
            return t * (jnp.sqrt(s) * jax.lax.rsqrt(ssq + COS_EPS)).astype(t.dtype)

        def na2d(q, k, v, ks):
            B, H, W, nh, dh = q.shape
            ih = jnp.clip(jnp.arange(H) - ks // 2, 0, H - ks)[:, None] + jnp.arange(ks)[None, :]
            iw = jnp.clip(jnp.arange(W) - ks // 2, 0, W - ks)[:, None] + jnp.arange(ks)[None, :]
            kw = k[:, ih][:, :, :, iw]
            vw = v[:, ih][:, :, :, iw]
            logits = jnp.einsum('bxynd,bxiyjnd->bxynij', q, kw)
            a = jax.nn.softmax(logits.reshape(B, H, W, nh, ks * ks), axis=-1)
            a = a.reshape(B, H, W, nh, ks, ks).astype(v.dtype)
            return jnp.einsum('bxynij,bxiyjnd->bxynd', a, vw)
        key = jax.random.key(seed)
        ks = jax.random.split(key, 3)
        x = jax.random.normal(ks[0], (2, D_MODEL, 48, 48), dtype=jnp.float32)
        qkv_w = jax.random.normal(ks[1], (3 * D_MODEL, D_MODEL, 3, 3), dtype=jnp.float32) * 0.02
        out_w = jax.random.normal(ks[2], (D_MODEL, D_MODEL, 3, 3), dtype=jnp.float32) * 0.02
        return {'x': x, 'gn_w': jnp.ones((D_MODEL,), jnp.float32), 'gn_b': jnp.zeros((D_MODEL,), jnp.float32), 'qkv_w': qkv_w, 'qkv_b': jnp.zeros((3 * D_MODEL,), jnp.float32), 'scale': jnp.full((N_HEADS,), 10.0, jnp.float32), 'out_w': out_w, 'out_b': jnp.zeros((D_MODEL,), jnp.float32)}
    _L0_conv_all = _L0_conv_setup()
    _L0_conv_in = {k: v for k, v in _L0_conv_all.items() if k in ('gn_w', 'gn_b', 'qkv_w', 'qkv_b', 'scale', 'out_w', 'out_b')}
    del _L0_conv_all

    def _L0_ffn_setup():
        import jax, jax.numpy as jnp
        import numpy as np
        NUM_EXPERTS = 8
        TOP_K = 2
        LN_EPS = 1e-05

        def _layernorm(x, g, b):
            mu = jnp.mean(x, axis=-1, keepdims=True)
            var = jnp.mean(jnp.square(x - mu), axis=-1, keepdims=True)
            return (x - mu) * jax.lax.rsqrt(var + LN_EPS) * g + b
        key = jax.random.key(seed)
        ks = jax.random.split(key, 8)
        B, S, D, F, E = (8, 1024, 128, 512, NUM_EXPERTS)
        return {'x': jax.random.normal(ks[0], (B, S, D), dtype=jnp.float32), 'gate_w': jax.random.normal(ks[1], (D, E), dtype=jnp.float32) * 0.02, 'w1': jax.random.normal(ks[2], (E, D, F), dtype=jnp.float32) * 0.02, 'b1': jnp.zeros((E, F), dtype=jnp.float32), 'w2': jax.random.normal(ks[3], (E, F, D), dtype=jnp.float32) * 0.02, 'b2': jnp.zeros((E, D), dtype=jnp.float32), 'ln_g': jnp.ones((D,), dtype=jnp.float32), 'ln_b': jnp.zeros((D,), dtype=jnp.float32)}
    _L0_ffn_all = _L0_ffn_setup()
    _L0_ffn_in = {k: v for k, v in _L0_ffn_all.items() if k in ('gate_w', 'w1', 'b1', 'w2', 'b2', 'ln_g', 'ln_b')}
    del _L0_ffn_all

    def _L1_conv_setup():
        import jax, jax.numpy as jnp
        import numpy as np
        C = 128
        CQK = C // 8
        key = jax.random.key(seed)
        ks = jax.random.split(key, 7)
        B, H, W = (4, 16, 16)
        x = jax.random.normal(ks[0], (B, C, H, W), dtype=jnp.float32)
        s = 1.0 / np.sqrt(C)
        Wq = jax.random.uniform(ks[1], (CQK, C), jnp.float32, -s, s)
        bq = jax.random.uniform(ks[2], (CQK,), jnp.float32, -s, s)
        Wk = jax.random.uniform(ks[3], (CQK, C), jnp.float32, -s, s)
        bk = jax.random.uniform(ks[4], (CQK,), jnp.float32, -s, s)
        Wv = jax.random.uniform(ks[5], (C, C), jnp.float32, -s, s)
        bv = jax.random.uniform(ks[6], (C,), jnp.float32, -s, s)
        return {'x': x, 'Wq': Wq, 'bq': bq, 'Wk': Wk, 'bk': bk, 'Wv': Wv, 'bv': bv}
    _L1_conv_all = _L1_conv_setup()
    _L1_conv_in = {k: v for k, v in _L1_conv_all.items() if k in ('Wq', 'bq', 'Wk', 'bk', 'Wv', 'bv')}
    del _L1_conv_all

    def _L1_ffn_setup():
        import jax, jax.numpy as jnp
        import numpy as np
        E, D, H = (8, 128, 512)
        B, N = (8, 128)
        key = jax.random.key(seed)
        ks = jax.random.split(key, 4)

        def init(k, shape, fan_in):
            return jax.random.normal(k, shape, jnp.float32) * (1.0 / np.sqrt(fan_in))
        return {'x': jax.random.normal(ks[0], (B, N, D), jnp.float32), 'Wr': init(ks[1], (D, E), D), 'br': jnp.zeros((E,), jnp.float32), 'W1': init(ks[2], (E, D, H), D), 'b1': jnp.zeros((E, H), jnp.float32), 'W2': init(ks[3], (E, H, D), H), 'b2': jnp.zeros((E, D), jnp.float32)}
    _L1_ffn_all = _L1_ffn_setup()
    _L1_ffn_in = {k: v for k, v in _L1_ffn_all.items() if k in ('Wr', 'br', 'W1', 'b1', 'W2', 'b2')}
    del _L1_ffn_all

    def _L2_conv_setup():
        import jax, jax.numpy as jnp
        from jax import lax
        import numpy as np
        key = jax.random.key(seed)
        ks = jax.random.split(key, 16)
        N, C, H, W = (16, 128, 16, 16)
        Cm, planes, k = (32, 128, 5)
        s = 0.05
        return {'x': jax.random.normal(ks[0], (N, C, H, W), jnp.float32), 'conv_w': jax.random.normal(ks[1], (Cm, C, 1, 1), jnp.float32) * s, 'conv_b': jax.random.normal(ks[2], (Cm,), jnp.float32) * s, 'conv_k_w': jax.random.normal(ks[3], (1, 2, 1, 1), jnp.float32) * s, 'conv_k_b': jax.random.normal(ks[4], (1,), jnp.float32) * s, 'conv_k2_w': jax.random.normal(ks[5], (1, 2, 1, 1), jnp.float32) * s, 'conv_k2_b': jax.random.normal(ks[6], (1,), jnp.float32) * s, 'conv_kernel_w': jax.random.normal(ks[7], (k * k, 1, 1, 1), jnp.float32) * s, 'conv_kernel_b': jax.random.normal(ks[8], (k * k,), jnp.float32) * s, 'conv_kernel2_w': jax.random.normal(ks[9], (9, 1, 1, 1), jnp.float32) * s, 'conv_kernel2_b': jax.random.normal(ks[10], (9,), jnp.float32) * s, 'adap_bias': jax.random.normal(ks[11], (Cm,), jnp.float32) * s, 'atrous_bias': jax.random.normal(ks[12], (Cm,), jnp.float32) * s, 'fuse_w': jax.random.normal(ks[13], (planes, 2 * Cm, 1, 1), jnp.float32) * s, 'fuse_b': jax.random.normal(ks[14], (planes,), jnp.float32) * s}
    _L2_conv_all = _L2_conv_setup()
    _L2_conv_in = {k: v for k, v in _L2_conv_all.items() if k in ('conv_w', 'conv_b', 'conv_k_w', 'conv_k_b', 'conv_k2_w', 'conv_k2_b', 'conv_kernel_w', 'conv_kernel_b', 'conv_kernel2_w', 'conv_kernel2_b', 'adap_bias', 'atrous_bias', 'fuse_w', 'fuse_b')}
    del _L2_conv_all

    def _L2_ffn_setup():
        import jax, jax.numpy as jnp
        import numpy as np
        IN_FEATURES = 128
        FEATURES = 128
        BATCH, SEQ = (8, 2048)

        def _ste(x_orig, y_proc):
            return x_orig + jax.lax.stop_gradient(y_proc - x_orig)
        key = jax.random.key(seed)
        kx, kw = jax.random.split(key)
        x = jax.random.normal(kx, (BATCH, SEQ, IN_FEATURES), dtype=jnp.float32)
        weight = jax.random.normal(kw, (IN_FEATURES, FEATURES), dtype=jnp.float32) / np.sqrt(IN_FEATURES)
        bias = jnp.zeros((FEATURES,), dtype=jnp.float32)
        return {'x': x, 'weight': weight, 'bias': bias}
    _L2_ffn_all = _L2_ffn_setup()
    _L2_ffn_in = {k: v for k, v in _L2_ffn_all.items() if k in ('weight', 'bias')}
    del _L2_ffn_all

    def _L3_conv_setup():
        import jax, jax.numpy as jnp
        import numpy as np
        from jax import lax
        EPS = 1e-05
        DW_THRESH = 4.0
        PW_THRESH = 0.001
        C_IN = 128
        C_OUT = 128

        def _bn(x, g, b, m, v):
            inv = g * lax.rsqrt(v + EPS)
            return x * inv[None, :, None, None] + (b - m * inv)[None, :, None, None]

        def _prune(x, thresh):
            amax = jnp.max(jnp.abs(x), axis=(2, 3), keepdims=True)
            return jnp.where(amax < thresh, jnp.zeros_like(x), x)
        key = jax.random.key(seed)
        ks = jax.random.split(key, 8)
        B, H, W = (16, 28, 28)
        x = jax.random.normal(ks[0], (B, C_IN, H, W), dtype=jnp.float32)
        dw_w = jax.random.normal(ks[1], (C_IN, 1, 3, 3), dtype=jnp.float32) * 0.1
        dw_b = jax.random.normal(ks[2], (C_IN,), dtype=jnp.float32) * 0.1
        bn1_g = jnp.ones((C_IN,), jnp.float32)
        bn1_b = jnp.zeros((C_IN,), jnp.float32)
        bn1_m = jnp.zeros((C_IN,), jnp.float32)
        bn1_v = jnp.ones((C_IN,), jnp.float32)
        pw_w = jax.random.normal(ks[3], (C_OUT, C_IN, 1, 1), dtype=jnp.float32) * 0.05
        pw_b = jax.random.normal(ks[4], (C_OUT,), dtype=jnp.float32) * 0.1
        bn2_g = jnp.ones((C_OUT,), jnp.float32)
        bn2_b = jnp.zeros((C_OUT,), jnp.float32)
        bn2_m = jnp.zeros((C_OUT,), jnp.float32)
        bn2_v = jnp.ones((C_OUT,), jnp.float32)
        return dict(x=x, dw_w=dw_w, dw_b=dw_b, bn1_g=bn1_g, bn1_b=bn1_b, bn1_m=bn1_m, bn1_v=bn1_v, pw_w=pw_w, pw_b=pw_b, bn2_g=bn2_g, bn2_b=bn2_b, bn2_m=bn2_m, bn2_v=bn2_v)
    _L3_conv_all = _L3_conv_setup()
    _L3_conv_in = {k: v for k, v in _L3_conv_all.items() if k in ('dw_w', 'dw_b', 'bn1_g', 'bn1_b', 'bn1_m', 'bn1_v', 'pw_w', 'pw_b', 'bn2_g', 'bn2_b', 'bn2_m', 'bn2_v')}
    del _L3_conv_all

    def _L3_ffn_setup():
        import jax, jax.numpy as jnp
        import numpy as np
        TOP_K = 2
        key = jax.random.key(seed)
        k0, k1, k2, k3, k4 = jax.random.split(key, 5)
        B, S, D, F, E = (1, 512, 128, 256, 8)
        scale = 0.02
        hidden_states = jax.random.normal(k0, (B, S, D), dtype=jnp.float32)
        router_w = jax.random.normal(k1, (D, E), dtype=jnp.float32) * scale
        w1 = jax.random.normal(k2, (E, D, F), dtype=jnp.float32) * scale
        w2 = jax.random.normal(k3, (E, F, D), dtype=jnp.float32) * scale
        w3 = jax.random.normal(k4, (E, D, F), dtype=jnp.float32) * scale
        return {'hidden_states': hidden_states, 'router_w': router_w, 'w1': w1, 'w2': w2, 'w3': w3}
    _L3_ffn_all = _L3_ffn_setup()
    _L3_ffn_in = {k: v for k, v in _L3_ffn_all.items() if k in ('router_w', 'w1', 'w2', 'w3')}
    del _L3_ffn_all
    return {'x': x, 'L0_conv_gn_w': _L0_conv_in['gn_w'], 'L0_conv_gn_b': _L0_conv_in['gn_b'], 'L0_conv_qkv_w': _L0_conv_in['qkv_w'], 'L0_conv_qkv_b': _L0_conv_in['qkv_b'], 'L0_conv_scale': _L0_conv_in['scale'], 'L0_conv_out_w': _L0_conv_in['out_w'], 'L0_conv_out_b': _L0_conv_in['out_b'], 'L0_ffn_gate_w': _L0_ffn_in['gate_w'], 'L0_ffn_w1': _L0_ffn_in['w1'], 'L0_ffn_b1': _L0_ffn_in['b1'], 'L0_ffn_w2': _L0_ffn_in['w2'], 'L0_ffn_b2': _L0_ffn_in['b2'], 'L0_ffn_ln_g': _L0_ffn_in['ln_g'], 'L0_ffn_ln_b': _L0_ffn_in['ln_b'], 'L1_conv_Wq': _L1_conv_in['Wq'], 'L1_conv_bq': _L1_conv_in['bq'], 'L1_conv_Wk': _L1_conv_in['Wk'], 'L1_conv_bk': _L1_conv_in['bk'], 'L1_conv_Wv': _L1_conv_in['Wv'], 'L1_conv_bv': _L1_conv_in['bv'], 'L1_ffn_Wr': _L1_ffn_in['Wr'], 'L1_ffn_br': _L1_ffn_in['br'], 'L1_ffn_W1': _L1_ffn_in['W1'], 'L1_ffn_b1': _L1_ffn_in['b1'], 'L1_ffn_W2': _L1_ffn_in['W2'], 'L1_ffn_b2': _L1_ffn_in['b2'], 'L2_conv_conv_w': _L2_conv_in['conv_w'], 'L2_conv_conv_b': _L2_conv_in['conv_b'], 'L2_conv_conv_k_w': _L2_conv_in['conv_k_w'], 'L2_conv_conv_k_b': _L2_conv_in['conv_k_b'], 'L2_conv_conv_k2_w': _L2_conv_in['conv_k2_w'], 'L2_conv_conv_k2_b': _L2_conv_in['conv_k2_b'], 'L2_conv_conv_kernel_w': _L2_conv_in['conv_kernel_w'], 'L2_conv_conv_kernel_b': _L2_conv_in['conv_kernel_b'], 'L2_conv_conv_kernel2_w': _L2_conv_in['conv_kernel2_w'], 'L2_conv_conv_kernel2_b': _L2_conv_in['conv_kernel2_b'], 'L2_conv_adap_bias': _L2_conv_in['adap_bias'], 'L2_conv_atrous_bias': _L2_conv_in['atrous_bias'], 'L2_conv_fuse_w': _L2_conv_in['fuse_w'], 'L2_conv_fuse_b': _L2_conv_in['fuse_b'], 'L2_ffn_weight': _L2_ffn_in['weight'], 'L2_ffn_bias': _L2_ffn_in['bias'], 'L3_conv_dw_w': _L3_conv_in['dw_w'], 'L3_conv_dw_b': _L3_conv_in['dw_b'], 'L3_conv_bn1_g': _L3_conv_in['bn1_g'], 'L3_conv_bn1_b': _L3_conv_in['bn1_b'], 'L3_conv_bn1_m': _L3_conv_in['bn1_m'], 'L3_conv_bn1_v': _L3_conv_in['bn1_v'], 'L3_conv_pw_w': _L3_conv_in['pw_w'], 'L3_conv_pw_b': _L3_conv_in['pw_b'], 'L3_conv_bn2_g': _L3_conv_in['bn2_g'], 'L3_conv_bn2_b': _L3_conv_in['bn2_b'], 'L3_conv_bn2_m': _L3_conv_in['bn2_m'], 'L3_conv_bn2_v': _L3_conv_in['bn2_v'], 'L3_ffn_router_w': _L3_ffn_in['router_w'], 'L3_ffn_w1': _L3_ffn_in['w1'], 'L3_ffn_w2': _L3_ffn_in['w2'], 'L3_ffn_w3': _L3_ffn_in['w3']}

def reference(x, L0_conv_gn_w, L0_conv_gn_b, L0_conv_qkv_w, L0_conv_qkv_b, L0_conv_scale, L0_conv_out_w, L0_conv_out_b, L0_ffn_gate_w, L0_ffn_w1, L0_ffn_b1, L0_ffn_w2, L0_ffn_b2, L0_ffn_ln_g, L0_ffn_ln_b, L1_conv_Wq, L1_conv_bq, L1_conv_Wk, L1_conv_bk, L1_conv_Wv, L1_conv_bv, L1_ffn_Wr, L1_ffn_br, L1_ffn_W1, L1_ffn_b1, L1_ffn_W2, L1_ffn_b2, L2_conv_conv_w, L2_conv_conv_b, L2_conv_conv_k_w, L2_conv_conv_k_b, L2_conv_conv_k2_w, L2_conv_conv_k2_b, L2_conv_conv_kernel_w, L2_conv_conv_kernel_b, L2_conv_conv_kernel2_w, L2_conv_conv_kernel2_b, L2_conv_adap_bias, L2_conv_atrous_bias, L2_conv_fuse_w, L2_conv_fuse_b, L2_ffn_weight, L2_ffn_bias, L3_conv_dw_w, L3_conv_dw_b, L3_conv_bn1_g, L3_conv_bn1_b, L3_conv_bn1_m, L3_conv_bn1_v, L3_conv_pw_w, L3_conv_pw_b, L3_conv_bn2_g, L3_conv_bn2_b, L3_conv_bn2_m, L3_conv_bn2_v, L3_ffn_router_w, L3_ffn_w1, L3_ffn_w2, L3_ffn_w3):
    import jax
    import jax.numpy as jnp

    def _L0_conv_ref(x, gn_w, gn_b, qkv_w, qkv_b, scale, out_w, out_b):
        import jax, jax.numpy as jnp
        import numpy as np
        D_MODEL = 128
        D_HEAD = 16
        N_HEADS = D_MODEL // D_HEAD
        KS = 7
        GROUPS = 16
        GN_EPS = 1e-05
        COS_EPS = 1e-06

        def conv3x3(x, w, b):
            y = jax.lax.conv_general_dilated(x, w, window_strides=(1, 1), padding='SAME', dimension_numbers=('NCHW', 'OIHW', 'NCHW'))
            return y + b[None, :, None, None]

        def group_norm(x, gamma, beta):
            B, C, H, W = x.shape
            xr = x.reshape(B, GROUPS, -1)
            mean = jnp.mean(xr, axis=-1, keepdims=True)
            var = jnp.var(xr, axis=-1, keepdims=True)
            xn = ((xr - mean) * jax.lax.rsqrt(var + GN_EPS)).reshape(B, C, H, W)
            return xn * gamma[None, :, None, None] + beta[None, :, None, None]

        def cosine_scale(t, scale_h):
            s = scale_h.astype(jnp.float32)[None, None, None, :, None]
            ssq = jnp.sum(t.astype(jnp.float32) ** 2, axis=-1, keepdims=True)
            return t * (jnp.sqrt(s) * jax.lax.rsqrt(ssq + COS_EPS)).astype(t.dtype)

        def na2d(q, k, v, ks):
            B, H, W, nh, dh = q.shape
            ih = jnp.clip(jnp.arange(H) - ks // 2, 0, H - ks)[:, None] + jnp.arange(ks)[None, :]
            iw = jnp.clip(jnp.arange(W) - ks // 2, 0, W - ks)[:, None] + jnp.arange(ks)[None, :]
            kw = k[:, ih][:, :, :, iw]
            vw = v[:, ih][:, :, :, iw]
            logits = jnp.einsum('bxynd,bxiyjnd->bxynij', q, kw)
            a = jax.nn.softmax(logits.reshape(B, H, W, nh, ks * ks), axis=-1)
            a = a.reshape(B, H, W, nh, ks, ks).astype(v.dtype)
            return jnp.einsum('bxynij,bxiyjnd->bxynd', a, vw)
        skip = x
        h = group_norm(x, gn_w, gn_b)
        qkv = conv3x3(h, qkv_w, qkv_b)
        B, _, H, W = qkv.shape
        qkv = qkv.reshape(B, 3, N_HEADS, D_HEAD, H, W).transpose(1, 0, 4, 5, 2, 3)
        q, k, v = (qkv[0], qkv[1], qkv[2])
        q = cosine_scale(q, scale)
        k = cosine_scale(k, scale)
        o = na2d(q, k, v, KS)
        o = o.transpose(0, 3, 4, 1, 2).reshape(B, D_MODEL, H, W)
        y = conv3x3(o, out_w, out_b)
        return y + skip

    def _L0_ffn_ref(x, gate_w, w1, b1, w2, b2, ln_g, ln_b):
        import jax, jax.numpy as jnp
        import numpy as np
        NUM_EXPERTS = 8
        TOP_K = 2
        LN_EPS = 1e-05

        def _layernorm(x, g, b):
            mu = jnp.mean(x, axis=-1, keepdims=True)
            var = jnp.mean(jnp.square(x - mu), axis=-1, keepdims=True)
            return (x - mu) * jax.lax.rsqrt(var + LN_EPS) * g + b
        B, S, D = x.shape
        E = gate_w.shape[1]
        x_norm = _layernorm(x, ln_g, ln_b)
        xf = x_norm.reshape(B * S, D)
        logits = xf @ gate_w
        probs = jax.nn.softmax(logits, axis=-1)
        dispatch_w, expert_idx = jax.lax.top_k(probs, TOP_K)
        combine = jnp.sum(jax.nn.one_hot(expert_idx, E, dtype=xf.dtype) * dispatch_w[..., None], axis=1)
        out = jnp.zeros_like(xf)
        for e in range(E):
            h = jax.nn.gelu(xf @ w1[e] + b1[e], approximate=False)
            y = h @ w2[e] + b2[e]
            out = out + combine[:, e:e + 1] * y
        return x + out.reshape(B, S, D)

    def _L1_conv_ref(x, Wq, bq, Wk, bk, Wv, bv):
        import jax, jax.numpy as jnp
        import numpy as np
        C = 128
        CQK = C // 8
        B, Cc, H, W = x.shape
        N = H * W
        xf = x.reshape(B, Cc, N)
        q = jnp.einsum('oc,bcn->bno', Wq, xf) + bq
        k = jnp.einsum('oc,bcn->bon', Wk, xf) + bk[None, :, None]
        v = jnp.einsum('oc,bcn->bno', Wv, xf) + bv
        energy = jnp.einsum('bno,bom->bnm', q, k)
        attn = jax.nn.softmax(energy, axis=-1)
        out = jnp.einsum('bnm,bmc->bnc', attn, v)
        return out.transpose(0, 2, 1).reshape(B, Cc, H, W)

    def _L1_ffn_ref(x, Wr, br, W1, b1, W2, b2):
        import jax, jax.numpy as jnp
        import numpy as np
        E, D, H = (8, 128, 512)
        B, N = (8, 128)
        b, n, d = x.shape
        xt = x.reshape(-1, d)
        route_prob = jax.nn.softmax(xt.astype(jnp.float32) @ Wr + br, axis=-1)
        routes = jnp.argmax(route_prob, axis=-1)
        p_max = jnp.max(route_prob, axis=-1)

        def expert_step(acc, inp):
            w1, bb1, w2, bb2, e = inp
            h = jax.nn.gelu(xt @ w1 + bb1, approximate=False)
            y = h @ w2 + bb2
            return (acc + y * (routes == e)[:, None].astype(y.dtype), None)
        out, _ = jax.lax.scan(expert_step, jnp.zeros_like(xt), (W1, b1, W2, b2, jnp.arange(E)))
        out = out * (p_max / jax.lax.stop_gradient(p_max))[:, None]
        return out.reshape(b, n, d)

    def _L2_conv_ref(x, conv_w, conv_b, conv_k_w, conv_k_b, conv_k2_w, conv_k2_b, conv_kernel_w, conv_kernel_b, conv_kernel2_w, conv_kernel2_b, adap_bias, atrous_bias, fuse_w, fuse_b):
        import jax, jax.numpy as jnp
        from jax import lax
        import numpy as np
        N, C, H, W = x.shape
        Cm = conv_w.shape[0]
        kk = conv_kernel_w.shape[0]
        k = int(round(kk ** 0.5))
        pad = (k - 1) // 2
        cw = conv_w[:, :, 0, 0]
        f = jax.nn.relu(jnp.einsum('nchw,oc->nohw', x, cw) + conv_b[None, :, None, None])
        g = jax.nn.relu(jnp.einsum('nc,oc->no', x.mean((2, 3)), cw) + conv_b)
        wk = conv_kernel_w[:, 0, 0, 0]
        K_img = g[:, :, None] * wk[None, None, :] + conv_kernel_b[None, None, :]
        K_dom = K_img.mean(0)
        gk = jax.nn.relu(conv_k_w[0, 0, 0, 0] * K_img + conv_k_w[0, 1, 0, 0] * K_dom[None] + conv_k_b[0])
        Wd = gk.reshape(N * Cm, 1, k, k)
        wk2 = conv_kernel2_w[:, 0, 0, 0]
        K2_img = g[:, :, None] * wk2[None, None, :] + conv_kernel2_b[None, None, :]
        K2_dom = K2_img.mean(0)
        gk2 = jax.nn.relu(conv_k2_w[0, 0, 0, 0] * K2_img + conv_k2_w[0, 1, 0, 0] * K2_dom[None] + conv_k2_b[0])
        W2 = gk2.reshape(N * Cm, 1, 3, 3)
        fr = f.reshape(1, N * Cm, H, W)
        y1 = lax.conv_general_dilated(fr, Wd, (1, 1), [(pad, pad), (pad, pad)], feature_group_count=N * Cm)
        y1 = y1.reshape(N, Cm, H, W) + adap_bias[None, :, None, None]
        y2 = lax.conv_general_dilated(fr, W2, (1, 1), [(2, 2), (2, 2)], rhs_dilation=(2, 2), feature_group_count=N * Cm)
        y2 = y2.reshape(N, Cm, H, W) + atrous_bias[None, :, None, None]
        y = jnp.concatenate([y1, y2], axis=1)
        out = jnp.einsum('nchw,oc->nohw', y, fuse_w[:, :, 0, 0]) + fuse_b[None, :, None, None]
        return out

    def _L2_ffn_ref(x, weight, bias):
        import jax, jax.numpy as jnp
        import numpy as np
        IN_FEATURES = 128
        FEATURES = 128
        BATCH, SEQ = (8, 2048)

        def _ste(x_orig, y_proc):
            return x_orig + jax.lax.stop_gradient(y_proc - x_orig)
        weight_centered = weight - jnp.mean(weight)
        weight_bin = jnp.sign(weight_centered)
        weight_bin_ste = _ste(weight, weight_bin)
        scale_gamma = jnp.mean(jnp.abs(weight))
        effective_weight = weight_bin_ste * scale_gamma
        y = jnp.dot(x, effective_weight) + bias
        act_clipped = jnp.clip(y, -1.0, 1.0)
        quant_dequant = jnp.round(act_clipped * 7.0) / 7.0
        return _ste(y, quant_dequant)

    def _L3_conv_ref(x, dw_w, dw_b, bn1_g, bn1_b, bn1_m, bn1_v, pw_w, pw_b, bn2_g, bn2_b, bn2_m, bn2_v):
        import jax, jax.numpy as jnp
        import numpy as np
        from jax import lax
        EPS = 1e-05
        DW_THRESH = 4.0
        PW_THRESH = 0.001
        C_IN = 128
        C_OUT = 128

        def _bn(x, g, b, m, v):
            inv = g * lax.rsqrt(v + EPS)
            return x * inv[None, :, None, None] + (b - m * inv)[None, :, None, None]

        def _prune(x, thresh):
            amax = jnp.max(jnp.abs(x), axis=(2, 3), keepdims=True)
            return jnp.where(amax < thresh, jnp.zeros_like(x), x)
        dn = ('NCHW', 'OIHW', 'NCHW')
        h = lax.conv_general_dilated(x, dw_w, window_strides=(1, 1), padding=((1, 1), (1, 1)), feature_group_count=C_IN, dimension_numbers=dn)
        h = h + dw_b[None, :, None, None]
        h = jax.nn.relu(_bn(h, bn1_g, bn1_b, bn1_m, bn1_v))
        h = _prune(h, DW_THRESH)
        h = lax.conv_general_dilated(h, pw_w, window_strides=(1, 1), padding=((0, 0), (0, 0)), dimension_numbers=dn)
        h = h + pw_b[None, :, None, None]
        h = jax.nn.relu(_bn(h, bn2_g, bn2_b, bn2_m, bn2_v))
        h = _prune(h, PW_THRESH)
        return h

    def _L3_ffn_ref(hidden_states, router_w, w1, w2, w3):
        import jax, jax.numpy as jnp
        import numpy as np
        TOP_K = 2
        B, S, D = hidden_states.shape
        E = router_w.shape[1]
        x = hidden_states.reshape(-1, D)
        T = x.shape[0]
        router_logits = x @ router_w
        probs = jax.nn.softmax(router_logits.astype(jnp.float32), axis=-1)
        routing_weights, selected_experts = jax.lax.top_k(probs, TOP_K)
        routing_weights = routing_weights / routing_weights.sum(axis=-1, keepdims=True)
        routing_weights = routing_weights.astype(x.dtype)
        combine = jnp.zeros((T, E), dtype=x.dtype).at[jnp.arange(T)[:, None], selected_experts].add(routing_weights)
        gate = jax.nn.silu(jnp.einsum('td,edf->tef', x, w1))
        up = jnp.einsum('td,edf->tef', x, w3)
        h = gate * up * combine[:, :, None]
        out = jnp.einsum('tef,efd->td', h, w2)
        return out.reshape(B, S, D)

    def _gn(v, G=32, eps=1e-05):
        B_, C_, H_, W_ = v.shape
        g = v.reshape(B_, G, C_ // G, H_, W_)
        m = jnp.mean(g, axis=(2, 3, 4), keepdims=True)
        s = jnp.var(g, axis=(2, 3, 4), keepdims=True)
        return ((g - m) / jnp.sqrt(s + eps)).reshape(v.shape)

    def _ln_c(v, eps=1e-06):
        m = jnp.mean(v, axis=1, keepdims=True)
        s = jnp.var(v, axis=1, keepdims=True)
        return (v - m) / jnp.sqrt(s + eps)

    def _ln_t(v, eps=1e-05):
        m = jnp.mean(v, axis=-1, keepdims=True)
        s = jnp.var(v, axis=-1, keepdims=True)
        return (v - m) / jnp.sqrt(s + eps)

    def _to_tokens(v):
        B_, C_, H_, W_ = v.shape
        return v.reshape(B_, C_, H_ * W_).transpose(0, 2, 1)

    def _from_tokens(t, like):
        B_, C_, H_, W_ = like.shape
        return t.transpose(0, 2, 1).reshape(B_, C_, H_, W_)
    x = x + _L0_conv_ref(_ln_c(x), L0_conv_gn_w, L0_conv_gn_b, L0_conv_qkv_w, L0_conv_qkv_b, L0_conv_scale, L0_conv_out_w, L0_conv_out_b)
    t = _to_tokens(x)
    t = t + _L0_ffn_ref(_ln_t(t), L0_ffn_gate_w, L0_ffn_w1, L0_ffn_b1, L0_ffn_w2, L0_ffn_b2, L0_ffn_ln_g, L0_ffn_ln_b)
    x = _from_tokens(t, x)
    x = x + _L1_conv_ref(_ln_c(x), L1_conv_Wq, L1_conv_bq, L1_conv_Wk, L1_conv_bk, L1_conv_Wv, L1_conv_bv)
    t = _to_tokens(x)
    t = t + _L1_ffn_ref(_ln_t(t), L1_ffn_Wr, L1_ffn_br, L1_ffn_W1, L1_ffn_b1, L1_ffn_W2, L1_ffn_b2)
    x = _from_tokens(t, x)
    x = x + _L2_conv_ref(_ln_c(x), L2_conv_conv_w, L2_conv_conv_b, L2_conv_conv_k_w, L2_conv_conv_k_b, L2_conv_conv_k2_w, L2_conv_conv_k2_b, L2_conv_conv_kernel_w, L2_conv_conv_kernel_b, L2_conv_conv_kernel2_w, L2_conv_conv_kernel2_b, L2_conv_adap_bias, L2_conv_atrous_bias, L2_conv_fuse_w, L2_conv_fuse_b)
    t = _to_tokens(x)
    t = t + _L2_ffn_ref(_ln_t(t), L2_ffn_weight, L2_ffn_bias)
    x = _from_tokens(t, x)
    x = x + _L3_conv_ref(_ln_c(x), L3_conv_dw_w, L3_conv_dw_b, L3_conv_bn1_g, L3_conv_bn1_b, L3_conv_bn1_m, L3_conv_bn1_v, L3_conv_pw_w, L3_conv_pw_b, L3_conv_bn2_g, L3_conv_bn2_b, L3_conv_bn2_m, L3_conv_bn2_v)
    t = _to_tokens(x)
    t = t + _L3_ffn_ref(_ln_t(t), L3_ffn_router_w, L3_ffn_w1, L3_ffn_w2, L3_ffn_w3)
    x = _from_tokens(t, x)
    return x

_drawn_inputs = setup_inputs


def setup_inputs(seed=0):
    import zlib

    import numpy as np

    out = dict(_drawn_inputs(seed))
    spreads = {'L0_conv_gn_w': (1.0, 0.2),
     'L0_conv_gn_b': (0.0, 0.1),
     'L0_conv_qkv_b': (0.0, 0.1),
     'L0_conv_scale': (10.0, 0.2),
     'L0_conv_out_b': (0.0, 0.1),
     'L0_ffn_b1': (0.0, 0.715),
     'L0_ffn_b2': (0.0, 0.384),
     'L0_ffn_ln_g': (1.0, 0.6),
     'L0_ffn_ln_b': (0.0, 0.8),
     'L1_ffn_br': (0.0, 0.1),
     'L1_ffn_b1': (0.0, 0.318),
     'L1_ffn_b2': (0.0, 0.1),
     'L2_ffn_bias': (0.0, 0.1),
     'L3_conv_bn1_g': (1.0, 0.2),
     'L3_conv_bn1_b': (0.0, 0.1),
     'L3_conv_bn1_m': (0.0, 0.1),
     'L3_conv_bn1_v': (1.0, 0.2),
     'L3_conv_bn2_g': (1.0, 0.6),
     'L3_conv_bn2_b': (0.0, 0.406),
     'L3_conv_bn2_m': (0.0, 0.423),
     'L3_conv_bn2_v': (1.0, 0.6)}
    factors = {'L0_ffn_w1': 3.688,
     'L0_ffn_w2': 3.276,
     'L1_conv_bq': 4.802,
     'L1_conv_bk': 64.0,
     'L2_conv_conv_w': 7.698,
     'L2_conv_conv_b': 8.0,
     'L2_conv_conv_k2_w': 21.75,
     'L2_conv_conv_kernel2_w': 8.0,
     'L2_conv_conv_kernel2_b': 8.0,
     'L2_conv_adap_bias': 7.777,
     'L2_conv_atrous_bias': 8.0,
     'L2_conv_fuse_w': 3.455,
     'L2_conv_fuse_b': 3.122,
     'L3_ffn_router_w': 8.0,
     'L3_ffn_w1': 8.0,
     'L3_ffn_w2': 8.0,
     'L3_ffn_w3': 8.0}
    for name, (base, spread) in spreads.items():
        noise = np.random.default_rng([zlib.crc32(name.encode()), seed]).standard_normal(out[name].shape)
        drawn = base * np.exp(spread * noise) if base else spread * noise
        out[name] = jnp.asarray(drawn.astype(out[name].dtype))
    for name, factor in factors.items():
        out[name] = (out[name] * factor).astype(out[name].dtype)
    return out
```

```python
import concourse.bass as bass
from concourse import mybir
from concourse.alu_op_type import AluOpType as ALU
from contextlib import ExitStack, contextmanager

F32 = mybir.dt.float32
BF16 = mybir.dt.bfloat16
ACT = mybir.ActivationFunctionType
AX = mybir.AxisListType
ds = bass.ds

B, C, H, W = 2, 128, 48, 48
ROWS = B * H
TR = 8
T = TR * W
NT = ROWS // TR
TB = H // TR
NTOK = ROWS * W
NC = NTOK // 128
CH = T // 128
PW = W + 2
PF = W + 4
PK = W + 6
NH, DH = 8, 16
E = 8
QB = 8
WIN = QB + 6
KH = WIN * WIN // 2
NBLK = H // QB
VA = DH + 1
MASKED = -30000.0
FREE = 2


class Chain:

    def __init__(self, engine, semaphore):
        self.engine, self.semaphore, self.count = engine, semaphore, 0

    def __call__(self, instruction):
        self.count += 1
        instruction.then_inc(self.semaphore, 1)
        self.engine.wait_ge(self.semaphore, self.count)


class Params:

    def __init__(self, columns):
        self.at, n = {}, 0
        for name, width in columns:
            self.at[name] = (n, width)
            n += width
        self.width = n

    def __getitem__(self, name):
        return self.at[name]


PARAMS = Params([
    ("identity", 128), ("centering", 128), ("ones", 128), ("group_mean", 128), ("channel_mean", 1),
    ("head_of", NH), ("tap5", 10), ("tap3", 10),
    ("gn_w", 1), ("gn_b", 1), ("qkv_b", 3), ("scale", NH), ("out_b", 1), ("ln_g", 1), ("ln_b", 1),
    ("b1_0", 32), ("gate_0", E), ("bv", 1), ("bq", 1), ("bk", 1), ("wq", DH), ("wk", DH), ("wv", C),
    ("b1_1", 32), ("gate_1", E), ("br", E),
    ("conv_w", 128), ("conv_b", 1), ("k_w", 2), ("k_b", 1), ("k2_w", 2), ("k2_b", 1),
    ("kernel_w", 10), ("kernel_b", 10), ("kernel2_w", 10), ("kernel2_b", 10),
    ("fuse1", C), ("fuse2", C), ("adap_b", 1), ("atrous_b", 1), ("fuse_b", 1),
    ("w2f", C), ("b2f", 1),
    ("dw_w", 9), ("dw_b", 1), ("bn1_g", 1), ("bn1_b", 1), ("bn1_m", 1), ("bn1_v", 1),
    ("pw", C), ("pw_b", 1), ("bn2_g", 1), ("bn2_b", 1), ("bn2_m", 1), ("bn2_v", 1),
    ("gate_3", E),
])


class Stage:

    def __init__(self, nc, name):
        self.nc, self.name, self.sems, self.ctx = nc, name, [], ExitStack()

    def sb(self, name, shape, dt=F32):
        return self.ctx.enter_context(self.nc.sbuf_tensor(f"{self.name}_{name}", shape, dt))

    def ps(self, name, shape=(128, 512), dt=F32):
        return self.ctx.enter_context(self.nc.psum_tensor(f"{self.name}_{name}", list(shape), dt))

    def sem(self, name):
        s = self.nc.alloc_semaphore(f"{self.name}_{name}")
        self.sems.append(s)
        return s

    def __enter__(self):
        return self

    def __exit__(self, *error):
        if error[0] is None:
            self.nc.clear_and_free_semaphores(self.sems)
            self.nc.all_engine_barrier()
            self.ctx.close()


def rows48(ap):
    return ap.rearrange("p (r w) -> p r w", w=W)


def chunk(tensor, n):
    return tensor[:, :, :].rearrange("p r w -> p (r w)")[:, n * 128:(n + 1) * 128]


def along(ap, n):
    return ap.rearrange("p (a b) -> p a b", b=1).broadcast_to([ap.shape[0], ap.shape[1], n])


def tile(tensor, t):
    return tensor[:, ds(t * TR, TR), :]


def layer_norm(nc, P, name, X, eps, out, second=None, loads=()):
    with Stage(nc, name) as s:
        XC = s.sb("centred", [128, ROWS, W])
        squares = [s.sb(f"squares{u}", [128, TR, W]) for u in range(2)]
        spread = [s.sb(f"spread{u}", [128, CH, 128]) for u in range(2)]
        shifted, inv_var, rstd = (s.sb(n, [128, NC]) for n in ("shifted", "inv_var", "rstd"))
        cen = [s.ps(f"cen{u}") for u in range(2)]
        var = s.ps("var")
        bcast = [s.ps(f"bcast{u}") for u in range(2)]
        centred, copied, squared, squares_used = map(s.sem, ("centred", "copied", "squared", "squares_used"))
        step, root_in, root_out = map(s.sem, ("step", "root_in", "root_out"))
        spread_ready, turned, bcast_used = map(s.sem, ("spread_ready", "turned", "bcast_used"))
        if second:
            out2, eps2 = second
            shifted2, inv_var2, rstd2, both = (s.sb(n, [128, NC]) for n in ("shifted2", "inv_var2", "rstd2", "both"))
            spread2 = [s.sb(f"spread2{u}", [128, CH, 128]) for u in range(2)]
            scaled = [s.sb(f"scaled{u}", [128, TR, W]) for u in range(2)]
            bcast2 = [s.ps(f"bcast2{u}") for u in range(2)]
            scaled_ready, scaled_used = map(s.sem, ("scaled_ready", "scaled_used"))

        with nc.Block() as block:
            @block.sync
            def _(sp):
                for target, source, arrived in loads:
                    sp.dma_start(target, source).then_inc(arrived, 16)

            @block.tensor
            def _(pe):
                pe.sem_inc(squares_used, FREE)
                pe.sem_inc(turned, FREE)
                with pe.Fori(0, NT // 2) as i:
                    for u in range(2):
                        t = i * 2 + u
                        pe.wait_ge(copied, t + 1)
                        pe.matmul(cen[u][:, 0:T], P("centering"), tile(X, t), start=True, stop=True).then_inc(centred, 1)
                    for u in range(2):
                        t = i * 2 + u
                        pe.wait_ge(squared, t + 1)
                        for j in range(CH):
                            last = pe.matmul(var[:, ds(t * CH + j, 1)], chunk(squares[u], j), P("channel_mean"),
                                             start=True, stop=True)
                        last.then_inc(squares_used, 1)
                with pe.Fori(0, NT // 2) as i:
                    for u in range(2):
                        t = i * 2 + u
                        pe.wait_ge(spread_ready, t + 1)
                        pe.wait_ge(bcast_used, t + 1)
                        for j in range(CH):
                            last = pe.transpose(bcast[u][:, j * 128:(j + 1) * 128], spread[u][:, j, :], P("identity"))
                            if second:
                                last = pe.transpose(bcast2[u][:, j * 128:(j + 1) * 128], spread2[u][:, j, :], P("identity"))
                        last.then_inc(turned, 1)

            @block.scalar
            def _(act):
                act.preload_act_table(ACT.Sqrt)
                act.sem_inc(copied, FREE)
                with act.Fori(0, NT // 2) as i:
                    for u in range(2):
                        t = i * 2 + u
                        act.wait_ge(centred, t + 1)
                        act.activation(tile(XC, t), rows48(cen[u][:, 0:T]), ACT.Copy).then_inc(copied, 1)
                act.wait_ge(root_in, 1)
                act.activation(rstd[:, :], inv_var[:, :], ACT.Sqrt).then_inc(root_out, 1)
                if second:
                    act.wait_ge(root_in, 2)
                    act.activation(rstd2[:, :], inv_var2[:, :], ACT.Sqrt).then_inc(root_out, 1)
                    act.wait_ge(root_in, 3)
                    act.sem_inc(scaled_used, FREE)
                else:
                    act.wait_ge(root_out, 1)
                with act.Fori(0, NT // 2) as i:
                    for u in range(2):
                        t = i * 2 + u
                        act.wait_ge(turned, t + 1)
                        if second:
                            act.activation(spread2[u][:, :, :], along(both[:, ds(t * CH, CH)], 128), ACT.Copy)
                        act.activation(spread[u][:, :, :], along(rstd[:, ds(t * CH, CH)], 128), ACT.Copy).then_inc(spread_ready, 1)
                    for u in range(2 if second else 0):
                        t = i * 2 + u
                        act.wait_ge(scaled_ready, t + 1)
                        act.activation(tile(out2, t), scaled[u][:, :, :], ACT.Identity,
                                       bias=P("ln_b"), scale=P("ln_g")).then_inc(scaled_used, 1)

            @block.vector
            def _(dve):
                link = Chain(dve, step)
                with dve.Fori(0, NT // 2) as i:
                    for u in range(2):
                        t = i * 2 + u
                        dve.wait_ge(copied, t + 1 + FREE)
                        dve.wait_ge(squares_used, t + 1)
                        dve.tensor_tensor(squares[u][:, :, :], tile(XC, t), tile(XC, t), ALU.mult).then_inc(squared, 1)
                dve.wait_ge(squares_used, NT + FREE)
                link(dve.tensor_scalar(shifted[:, :], var[:, 0:NC], eps, None, ALU.add))
                dve.reciprocal(inv_var[:, :], shifted[:, :]).then_inc(root_in, 1)
                if second:
                    dve.wait_ge(root_in, 1)
                    link(dve.tensor_tensor(shifted2[:, :], inv_var[:, :], var[:, 0:NC], ALU.mult))
                    link(dve.tensor_scalar(shifted2[:, :], shifted2[:, :], eps2, None, ALU.add))
                    dve.reciprocal(inv_var2[:, :], shifted2[:, :]).then_inc(root_in, 1)
                    dve.wait_ge(root_out, 2)
                    dve.tensor_tensor(both[:, :], rstd[:, :], rstd2[:, :], ALU.mult).then_inc(root_in, 1)
                dve.sem_inc(bcast_used, FREE)
                with dve.Fori(0, NT // 2) as i:
                    for u in range(2):
                        t = i * 2 + u
                        dve.wait_ge(turned, t + 1 + FREE)
                        if second:
                            dve.wait_ge(scaled_used, t + 1)
                            dve.tensor_tensor(scaled[u][:, :, :], tile(XC, t), rows48(bcast2[u][:, 0:T]), ALU.mult).then_inc(scaled_ready, 1)
                        dve.tensor_tensor(tile(out, t), tile(XC, t), rows48(bcast[u][:, 0:T]), ALU.mult).then_inc(bcast_used, 1)


def group_norm(nc, P, XN, HP):
    with Stage(nc, "gn") as s:
        stats = s.sb("stats", [128, B, TB, 6])
        moments = s.sb("moments", [128, B, 2])
        square = s.sb("square", [128, B])
        group = s.sb("group", [128, B, 2])
        var, shifted, inv, rstd, gain, shift, drop = (
            s.sb(n, [128, B]) for n in ("var", "shifted", "inv", "rstd", "gain", "shift", "drop"))
        grouped = s.ps("grouped")
        step, moments_ready, grouped_ready, inv_ready, rstd_ready, affine_ready, zeroed = map(
            s.sem, ("step", "moments_ready", "grouped_ready", "inv_ready", "rstd_ready", "affine_ready", "zeroed"))
        with nc.Block() as block:
            @block.gpsimd
            def _(pool):
                pool.memset(HP[:, :, :], 0.0).then_inc(zeroed, 1)

            @block.vector
            def _(dve):
                link = Chain(dve, step)
                for b in range(B):
                    for t in range(TB):
                        last = dve.bn_stats(stats[:, b, t, :], XN[:, b * H + t * TR:b * H + (t + 1) * TR, :].rearrange("p r w -> p (r w)"))
                link(last)
                for b in range(B):
                    last = dve.bn_aggr(moments[:, b, :], stats[:, b, :, :].rearrange("p t s -> p (t s)"))
                link(last)
                link(dve.tensor_tensor(square[:, :], moments[:, :, 0], moments[:, :, 0], ALU.mult))
                dve.tensor_tensor(moments[:, :, 1], moments[:, :, 1], square[:, :], ALU.add).then_inc(moments_ready, 1)
                dve.wait_ge(grouped_ready, 1)
                link(dve.tensor_copy(group[:, :, :].rearrange("p b s -> p (b s)"), grouped[:, 0:2 * B]))
                link(dve.tensor_tensor(square[:, :], group[:, :, 0], group[:, :, 0], ALU.mult))
                link(dve.tensor_tensor(var[:, :], group[:, :, 1], square[:, :], ALU.subtract))
                link(dve.tensor_scalar(shifted[:, :], var[:, :], 1e-5, None, ALU.add))
                dve.reciprocal(inv[:, :], shifted[:, :]).then_inc(inv_ready, 1)
                dve.wait_ge(rstd_ready, 1)
                link(dve.tensor_scalar(gain[:, :], rstd[:, :], P("gn_w"), None, ALU.mult))
                link(dve.tensor_tensor(drop[:, :], group[:, :, 0], gain[:, :], ALU.mult))
                dve.tensor_scalar(shift[:, :], drop[:, :], -1.0, P("gn_b"), ALU.mult, ALU.add).then_inc(affine_ready, 1)
                dve.wait_ge(affine_ready, 1)
                dve.wait_ge(zeroed, 1)
                dve.tensor_scalar(HP[:, 1:1 + H, 1:1 + W], XN[:, 0:H, :], gain[:, 0:1], shift[:, 0:1], ALU.mult, ALU.add)

            @block.tensor
            def _(pe):
                pe.wait_ge(moments_ready, 1)
                pe.matmul(grouped[:, 0:2 * B], P("group_mean"), moments[:, :, :].rearrange("p b s -> p (b s)"),
                          start=True, stop=True).then_inc(grouped_ready, 1)

            @block.scalar
            def _(act):
                act.wait_ge(inv_ready, 1)
                act.activation(rstd[:, :], inv[:, :], ACT.Sqrt).then_inc(rstd_ready, 1)
                act.wait_ge(affine_ready, 1)
                act.wait_ge(zeroed, 1)
                act.activation(HP[:, PW + 1:PW + 1 + H, 1:1 + W], XN[:, H:2 * H, :], ACT.Identity,
                               bias=shift[:, 1:2], scale=gain[:, 1:2])


def qkv(nc, P, HP, wqkv, weights_loaded, Q, KP, VP):
    with Stage(nc, "qkv") as s:
        squares = [s.sb(f"squares{m}", [128, TR, W]) for m in range(2)]
        length = s.sb("length", [128, 2, NC, NH])
        inv = s.sb("inv", [128, 2, NC, NH])
        factor = s.sb("factor", [128, 2, NC, NH])
        spread = [s.sb(f"spread{m}", [128, CH, NH, DH]) for m in range(2)]
        conv = [s.ps(f"conv{c}") for c in range(3)]
        heads = [s.ps(f"heads{m}") for m in range(2)]
        bcast = [s.ps(f"bcast{m}") for m in range(2)]
        conv_ready, conv_used, evacuated, squared, squares_used, zeroed = map(
            s.sem, ("conv_ready", "conv_used", "evacuated", "squared", "squares_used", "zeroed"))
        step, inv_ready, factor_ready, spread_ready, turned, scaled = map(
            s.sem, ("step", "inv_ready", "factor_ready", "spread_ready", "turned", "scaled"))

        def in_key_image(image, b, i):
            return image[:, ds(b * PK + i * TR + 3, TR), 3:3 + W]

        with nc.Block() as block:
            @block.gpsimd
            def _(pool):
                pool.memset(KP[:, :, :], 0.0).then_inc(zeroed, 1)
                pool.memset(VP[:, :, :], 0.0).then_inc(zeroed, 1)

            @block.tensor
            def _(pe):
                pe.wait_ge(weights_loaded, 32)
                pe.sem_inc(squares_used, 1)
                with pe.Fori(0, B) as b, pe.Fori(0, TB) as i:
                    t = b * TB + i
                    for c in range(3):
                        pe.wait_ge(conv_used, t * 3 + c + 1)
                        for tap in range(9):
                            last = pe.matmul(rows48(conv[c][:, 0:T]), wqkv[:, tap, c * C:(c + 1) * C],
                                             HP[:, ds(b * PW + i * TR + tap // 3, TR), tap % 3:tap % 3 + W],
                                             start=tap == 0, stop=tap == 8)
                        last.then_inc(conv_ready, 1)
                    pe.wait_ge(squared, t + 1)
                    for m in range(2):
                        for j in range(CH):
                            last = pe.matmul(heads[m][:, ds((t * CH + j) * NH, NH)], chunk(squares[m], j), P("head_of"),
                                             start=True, stop=True)
                    last.then_inc(squares_used, 1)
                with pe.Fori(0, NT) as t:
                    for m in range(2):
                        pe.wait_ge(spread_ready, t * 2 + m + 1)
                        pe.wait_ge(scaled, t * 2 + m + 1)
                        for j in range(CH):
                            last = pe.transpose(bcast[m][:, j * 128:(j + 1) * 128],
                                                spread[m][:, j, :, :].rearrange("p h d -> p (h d)"), P("identity"))
                        last.then_inc(turned, 1)

            @block.scalar
            def _(act):
                act.preload_act_table(ACT.Sqrt)
                act.sem_inc(conv_used, 3)
                act.wait_ge(zeroed, 2)
                with act.Fori(0, B) as b, act.Fori(0, TB) as i:
                    t = b * TB + i
                    for c, target in enumerate((tile(Q, t), in_key_image(KP, b, i), in_key_image(VP, b, i))):
                        act.wait_ge(conv_ready, t * 3 + c + 1)
                        act.activation(target, rows48(conv[c][:, 0:T]), ACT.Identity, bias=P("qkv_b", first=c, width=1)).then_inc(conv_used, 1)
                act.wait_ge(inv_ready, 1)
                act.activation(factor[:, :, :, :].rearrange("p m n h -> p (m n h)"),
                               inv[:, :, :, :].rearrange("p m n h -> p (m n h)"), ACT.Sqrt).then_inc(factor_ready, 1)
                act.wait_ge(factor_ready, 1)
                act.sem_inc(turned, 2)
                with act.Fori(0, NT) as t:
                    for m in range(2):
                        act.wait_ge(turned, t * 2 + m + 1)
                        act.activation(spread[m][:, :, :, :].rearrange("p c h d -> p (c h) d"),
                                       along(factor[:, m, ds(t * CH, CH), :].rearrange("p n h -> p (n h)"), DH), ACT.Copy).then_inc(spread_ready, 1)

            @block.vector
            def _(dve):
                link = Chain(dve, step)
                with dve.Fori(0, B) as b, dve.Fori(0, TB) as i:
                    t = b * TB + i
                    dve.wait_ge(conv_used, t * 3 + 2 + 3)
                    dve.wait_ge(squares_used, t + 1)
                    dve.tensor_tensor(squares[0][:, :, :], tile(Q, t), tile(Q, t), ALU.mult)
                    dve.tensor_tensor(squares[1][:, :, :], in_key_image(KP, b, i), in_key_image(KP, b, i), ALU.mult).then_inc(squared, 1)
                dve.wait_ge(squares_used, NT + 1)
                for m in range(2):
                    last = dve.tensor_scalar(length[:, m, :, :].rearrange("p n h -> p (n h)"), heads[m][:, 0:NC * NH], 1e-6, None, ALU.add)
                link(last)
                link(dve.reciprocal(inv[:, :, :, :].rearrange("p m n h -> p (m n h)"), length[:, :, :, :].rearrange("p m n h -> p (m n h)")))
                scale = P("scale").rearrange("p (a h) -> p a h", a=1).broadcast_to([128, 2 * NC, NH])
                flat = inv[:, :, :, :].rearrange("p m n h -> p (m n) h")
                dve.tensor_tensor(flat, flat, scale, ALU.mult).then_inc(inv_ready, 1)
                dve.sem_inc(scaled, 2)
                dve.wait_ge(zeroed, 2)
                with dve.Fori(0, B) as b, dve.Fori(0, TB) as i:
                    t = b * TB + i
                    dve.wait_ge(turned, t * 2 + 1 + 2)
                    dve.tensor_tensor(tile(Q, t), tile(Q, t), rows48(bcast[0][:, 0:T]), ALU.mult).then_inc(scaled, 1)
                    dve.wait_ge(turned, t * 2 + 2 + 2)
                    dve.tensor_tensor(in_key_image(KP, b, i), in_key_image(KP, b, i), rows48(bcast[1][:, 0:T]), ALU.mult).then_inc(scaled, 1)


def neighbourhood(nc, P, Q, KP, VP, mask_dram, query_dram, OP):
    with Stage(nc, "na") as s:
        mask_all = s.sb("mask_all", [1 + 2 * QB, NBLK * NBLK, 2 * KH], BF16)
        query_side = s.sb("query_side", [1 + 2 * QB, NH, QB * QB], BF16)
        mask = [s.sb(f"mask{u}", [1 + 2 * QB, 2 * KH], BF16) for u in range(2)]
        keys = [s.sb(f"keys{u}", [128, WIN, WIN]) for u in range(2)]
        values = [s.sb(f"values{u}", [128, WIN, WIN]) for u in range(2)]
        queries = [s.sb(f"queries{u}", [128, NH, QB, QB]) for u in range(2)]
        probs = [[s.sb(f"probs{u}{h}", [KH, NH, QB * QB]) for h in range(2)] for u in range(2)]
        columns = [s.sb(f"columns{u}", [KH, 2, NH, VA]) for u in range(2)]
        inv = [s.sb(f"inv{u}", [QB * QB, NH]) for u in range(2)]
        normed = [s.sb(f"normed{u}", [QB * QB, NH, DH]) for u in range(2)]
        scores = [[s.ps(f"scores{u}{h}") for h in range(2)] for u in range(2)]
        turned_v = s.ps("turned_v")
        mixed = [s.ps(f"mixed{u}") for u in range(2)]
        turned_o = s.ps("turned_o")
        loaded, prepared, staged, queries_ready = map(s.sem, ("loaded", "prepared", "staged", "queries_ready"))
        scored, exped, v_turned, v_ready, mixed_ready, inv_ready, normed_ready, o_turned, o_stored = map(
            s.sem, ("scored", "exped", "v_turned", "v_ready", "mixed_ready", "inv_ready", "normed_ready", "o_turned", "o_stored"))

        def blocks(engine):
            with engine.Fori(0, B) as b, engine.Fori(0, NBLK) as by:
                for pair in range(NBLK // 2):
                    yield (b * NBLK + by) * NBLK + pair * 2, b, by, pair * 2

        with nc.Block() as block:
            @block.sync
            def _(sp):
                sp.dma_start(mask_all[:, :, :], mask_dram).then_inc(loaded, 16)
                sp.dma_start(query_side[:, :, :], query_dram).then_inc(loaded, 16)

            @block.gpsimd
            def _(pool):
                pool.memset(OP[:, :, :], 0.0).then_inc(prepared, 1)
                for u in range(2):
                    pool.memset(columns[u][:, :, :, :], 1.0).then_inc(prepared, 1)
                pool.wait_ge(loaded, 32)
                for n0, b, by, bx0 in blocks(pool):
                    for u in range(2):
                        n, bx = n0 + u, bx0 + u
                        pool.wait_ge(scored, n + 1)
                        row = ds(b * PK + by * QB, WIN)
                        pool.tensor_copy(keys[u][:, :, :], KP[:, row, bx * QB:bx * QB + WIN])
                        pool.tensor_copy(mask[u][:, :], mask_all[:, ds(by * NBLK + bx, 1), :].rearrange("p a k -> p (a k)"))
                        pool.tensor_copy(values[u][:, :, :], VP[:, row, bx * QB:bx * QB + WIN]).then_inc(staged, 1)

            @block.vector
            def _(dve):
                dve.sem_inc(v_ready, 1)
                dve.wait_ge(loaded, 32)
                dve.tensor_scalar(query_side[0:1, :, :], P("scale", rows=1).rearrange("p (h a) -> p h a", a=1)
                                  .broadcast_to([1, NH, QB * QB]), -1.0, None, ALU.mult).then_inc(queries_ready, 1)
                dve.wait_ge(prepared, 3)
                for n0, b, by, bx0 in blocks(dve):
                    for u in range(2):
                        n, bx = n0 + u, bx0 + u
                        dve.wait_ge(scored, n + 1)
                        patch = Q[:, ds(b * H + by * QB, QB), bx * QB:(bx + 1) * QB]
                        dve.tensor_tensor(queries[u][:, :, :, :],
                                          patch.rearrange("p (a y) x -> p a y x", a=1).broadcast_to([128, NH, QB, QB]),
                                          P("head_of").rearrange("p (h y x) -> p h y x", y=1, x=1).broadcast_to([128, NH, QB, QB]),
                                          ALU.mult).then_inc(queries_ready, 1)
                    for u in range(2):
                        n, bx = n0 + u, bx0 + u
                        dve.wait_ge(v_turned, n + 1)
                        dve.wait_ge(mixed_ready, n + 1)
                        dve.tensor_copy(columns[u][:, :, :, 0:DH].rearrange("k s h d -> k (s h) d"),
                                        turned_v[0:KH, 0:2 * C].rearrange("k (g d) -> k g d", d=DH)).then_inc(v_ready, 1)
                    for u in range(2):
                        n, bx = n0 + u, bx0 + u
                        dve.wait_ge(mixed_ready, n + 1 + FREE)
                        mix = mixed[u][0:QB * QB, 0:NH * VA].rearrange("q (h d) -> q h d", d=VA)
                        dve.wait_ge(o_turned, n + 1)
                        dve.reciprocal(inv[u][:, :], mix[:, :, DH]).then_inc(inv_ready, 1)
                        dve.wait_ge(inv_ready, n + 1)
                        dve.tensor_tensor(normed[u][:, :, :], mix[:, :, 0:DH], along(inv[u][:, :], DH), ALU.mult).then_inc(normed_ready, 1)

            @block.scalar
            def _(act):
                act.preload_act_table(ACT.Exp)
                act.sem_inc(exped, FREE * 2)
                act.sem_inc(o_stored, 1)
                act.wait_ge(prepared, 3)
                for n0, b, by, bx0 in blocks(act):
                    for u in range(2):
                        n = n0 + u
                        act.wait_ge(mixed_ready, n + 1)
                        act.wait_ge(scored, n + 1 + FREE)
                        for h in range(2):
                            act.activation(probs[u][h][:, :, :].rearrange("k h q -> k (h q)"), scores[u][h][0:KH, :], ACT.Exp).then_inc(exped, 1)
                    for u in range(2):
                        n, bx = n0 + u, bx0 + u
                        act.wait_ge(o_turned, n + 1 + FREE)
                        act.activation(OP[:, ds(b * PW + by * QB + 1, QB), 1 + bx * QB:1 + (bx + 1) * QB],
                                       turned_o[:, 0:QB * QB].rearrange("c (y x) -> c y x", x=QB), ACT.Copy).then_inc(o_stored, 1)

            @block.tensor
            def _(pe):
                pe.sem_inc(scored, FREE)
                pe.sem_inc(mixed_ready, FREE)
                pe.sem_inc(o_turned, FREE)
                pe.wait_ge(loaded, 32)
                for n0, b, by, bx0 in blocks(pe):
                    for u in range(2):
                        n = n0 + u
                        pe.wait_ge(staged, n + 1)
                        pe.wait_ge(v_ready, n + 1)
                        for h in range(2):
                            last = pe.transpose(turned_v[0:KH, h * C:(h + 1) * C],
                                                values[u][:, h * (WIN // 2):(h + 1) * (WIN // 2), :].rearrange("c y x -> c (y x)"), P("identity"))
                        last.then_inc(v_turned, 1)
                        pe.wait_ge(queries_ready, n + 2)
                        pe.wait_ge(exped, n * 2 + 2)
                        for h in range(2):
                            pe.matmul(scores[u][h][0:KH, :], keys[u][:, h * (WIN // 2):(h + 1) * (WIN // 2), :].rearrange("c y x -> c (y x)"),
                                      queries[u][:, :, :, :].rearrange("c h y x -> c (h y x)"), start=True, stop=False)
                            last = pe.matmul(scores[u][h][0:KH, :], mask[u][:, h * KH:(h + 1) * KH],
                                             query_side[:, :, :].rearrange("f h q -> f (h q)"), start=False, stop=True)
                        last.then_inc(scored, 1)
                    for u in range(2):
                        n = n0 + u
                        pe.wait_ge(exped, n * 2 + 2 + FREE * 2)
                        pe.wait_ge(v_ready, n + 1 + 1)
                        for hd in range(NH):
                            for h in range(2):
                                last = pe.matmul(mixed[u][0:QB * QB, hd * VA:(hd + 1) * VA], probs[u][h][:, hd, :],
                                                 columns[u][:, h, hd, :], start=h == 0, stop=h == 1)
                        last.then_inc(mixed_ready, 1)
                    for u in range(2):
                        n = n0 + u
                        pe.wait_ge(normed_ready, n + 1)
                        pe.wait_ge(o_stored, n + 1)
                        pe.matmul(turned_o[:, 0:QB * QB], normed[u][:, :, :].rearrange("q h d -> q (h d)"),
                                  P("identity", rows=QB * QB, width=QB * QB), start=True, stop=True).then_inc(o_turned, 1)


def out_conv(nc, P, OP, wout, XN, X):
    with Stage(nc, "oc") as s:
        conv = [s.ps(f"conv{u}") for u in range(2)]
        conv_ready, conv_used, summed = map(s.sem, ("conv_ready", "conv_used", "summed"))
        with nc.Block() as block:
            @block.gpsimd
            def _(pool):
                pool.tensor_tensor(X[:, :, :], X[:, :, :], XN[:, :, :], ALU.add).then_inc(summed, 1)

            @block.tensor
            def _(pe):
                with pe.Fori(0, B) as b, pe.Fori(0, TB // 2) as i:
                    for u in range(2):
                        t = b * TB + i * 2 + u
                        pe.wait_ge(conv_used, t + 1)
                        for tap in range(9):
                            last = pe.matmul(rows48(conv[u][:, 0:T]), wout[:, tap, :],
                                             OP[:, ds(b * PW + (i * 2 + u) * TR + tap // 3, TR), tap % 3:tap % 3 + W],
                                             start=tap == 0, stop=tap == 8)
                        last.then_inc(conv_ready, 1)

            @block.vector
            def _(dve):
                dve.sem_inc(conv_used, FREE)
                dve.wait_ge(summed, 1)
                with dve.Fori(0, NT // 2) as i:
                    for u in range(2):
                        t = i * 2 + u
                        dve.wait_ge(conv_ready, t + 1)
                        dve.scalar_tensor_tensor(tile(X, t), rows48(conv[u][:, 0:T]), P("out_b"), tile(X, t), ALU.add, ALU.add).then_inc(conv_used, 1)


def route(nc, P, name, XF, gate, bias, top, renormalise, gate_rows, gate_parts, ident16):
    with Stage(nc, name) as s:
        logits, shifted, expo, probs, left, near, pick, weights, part, rest = (
            s.sb(n, [128, NC, E]) for n in ("logits", "shifted", "expo", "probs", "left", "near", "pick", "weights", "part", "rest"))
        order = s.sb("order", [128, E])
        peak, total, inv, best = (s.sb(n, [128, NC]) for n in ("peak", "total", "inv", "best"))
        parts = s.sb("parts", [128, NC, 3, E], BF16)
        logits_ps = s.ps("logits_ps")
        turned = [s.ps(f"turned{u}", [128, 1024], BF16) for u in range(2)]
        gated, step, exp_in, exp_out, parts_ready, rows_turned, rows_used, zeroed = map(
            s.sem, ("gated", "step", "exp_in", "exp_out", "parts_ready", "rows_turned", "rows_used", "zeroed"))

        def per_token(ap):
            return along(ap[:, :], E)

        with nc.Block() as block:
            @block.gpsimd
            def _(pool):
                pool.memset(gate_rows[:, :], 0.0).then_inc(zeroed, 1)
                pool.memset(gate_parts[:, :], 0.0).then_inc(zeroed, 1)

            @block.tensor
            def _(pe):
                for n in range(NC):
                    last = pe.matmul(logits_ps[:, n * E:(n + 1) * E], chunk(XF, n), gate, start=True, stop=True)
                last.then_inc(gated, 1)
                pe.wait_ge(parts_ready, 1)
                for g in range(NC // 6):
                    if g >= 2:
                        pe.wait_ge(rows_used, 2 * (g - 1))
                    for j in range(6):
                        last = pe.transpose(turned[g % 2][0:3 * E, j * 128:(j + 1) * 128],
                                            parts[:, g * 6 + j, :, :].rearrange("p a e -> p (a e)"), ident16)
                    last.then_inc(rows_turned, 1)

            @block.scalar
            def _(act):
                act.preload_act_table(ACT.Exp)
                act.wait_ge(exp_in, 1)
                act.activation(expo[:, :, :], shifted[:, :, :], ACT.Exp).then_inc(exp_out, 1)

            @block.vector
            def _(dve):
                link = Chain(dve, step)
                for e in range(E):
                    last = dve.memset(order[:, e:e + 1], float(E - e))
                link(last)
                order_all = order[:, :].rearrange("p (a e) -> p a e", a=1).broadcast_to([128, NC, E])
                dve.wait_ge(gated, 1)
                psum = logits_ps[:, 0:NC * E].rearrange("p (n e) -> p n e", e=E)
                if bias is None:
                    link(dve.tensor_copy(logits[:, :, :], psum))
                else:
                    link(dve.tensor_tensor(logits[:, :, :], psum, bias.rearrange("p (a e) -> p a e", a=1).broadcast_to([128, NC, E]), ALU.add))
                link(dve.tensor_reduce(peak[:, :], logits[:, :, :], AX.X, ALU.max))
                dve.tensor_tensor(shifted[:, :, :], logits[:, :, :], per_token(peak), ALU.subtract).then_inc(exp_in, 1)
                dve.wait_ge(exp_out, 1)
                link(dve.tensor_reduce(total[:, :], expo[:, :, :], AX.X, ALU.add))
                link(dve.reciprocal(inv[:, :], total[:, :]))
                link(dve.tensor_tensor(probs[:, :, :], expo[:, :, :], per_token(inv), ALU.mult))
                link(dve.tensor_copy(left[:, :, :], probs[:, :, :]))
                for k in range(top):
                    link(dve.tensor_reduce(peak[:, :], left[:, :, :], AX.X, ALU.max))
                    link(dve.tensor_tensor(near[:, :, :], left[:, :, :], per_token(peak), ALU.is_equal))
                    link(dve.tensor_tensor(near[:, :, :], near[:, :, :], order_all, ALU.mult))
                    link(dve.tensor_reduce(best[:, :], near[:, :, :], AX.X, ALU.max))
                    if k == 0:
                        link(dve.tensor_tensor(pick[:, :, :], near[:, :, :], per_token(best), ALU.is_equal))
                        if top > 1:
                            link(dve.scalar_tensor_tensor(left[:, :, :], pick[:, :, :], -2.0, left[:, :, :], ALU.mult, ALU.add))
                    else:
                        link(dve.tensor_tensor(near[:, :, :], near[:, :, :], per_token(best), ALU.is_equal))
                        link(dve.tensor_tensor(pick[:, :, :], pick[:, :, :], near[:, :, :], ALU.add))
                if top == 1:
                    link(dve.tensor_copy(weights[:, :, :], pick[:, :, :]))
                else:
                    link(dve.tensor_tensor(weights[:, :, :], pick[:, :, :], probs[:, :, :], ALU.mult))
                if renormalise:
                    link(dve.tensor_reduce(total[:, :], weights[:, :, :], AX.X, ALU.add))
                    link(dve.reciprocal(inv[:, :], total[:, :]))
                    link(dve.tensor_tensor(weights[:, :, :], weights[:, :, :], per_token(inv), ALU.mult))
                source = weights
                for k in range(2):
                    link(dve.tensor_copy(parts[:, :, k, :], source[:, :, :]))
                    link(dve.tensor_copy(part[:, :, :], parts[:, :, k, :]))
                    link(dve.tensor_tensor(rest[:, :, :], source[:, :, :], part[:, :, :], ALU.subtract))
                    source = rest
                dve.tensor_copy(parts[:, :, 2, :], rest[:, :, :]).then_inc(parts_ready, 1)
                dve.wait_ge(zeroed, 2)
                for g in range(NC // 6):
                    dve.wait_ge(rows_turned, g + 1)
                    dve.tensor_copy(gate_rows[0:3 * E, g * 2 * T:(g + 1) * 2 * T], turned[g % 2][0:3 * E, 0:2 * T]).then_inc(rows_used, 1)
                    dve.tensor_copy(gate_parts[0:3 * E, g * 2 * T:(g + 1) * 2 * T], turned[g % 2][0:3 * E, 0:2 * T]).then_inc(rows_used, 1)


def experts(nc, name, XF, w_in, act_func, b1, w_out, b2, gate_rows, gate_parts, select, X, weights_loaded, extra=None, gated_unit=False):
    HC = 2 if gated_unit else 4
    with Stage(nc, name) as s:
        hidden = [s.sb(f"hidden{u}", [128, HC, T]) for u in range(2)]
        product = [s.sb(f"product{u}", [128, HC, T]) for u in range(2)]
        pre = [s.ps(f"pre{c}") for c in range(4)]
        gate = [s.ps(f"gate{u}") for u in range(2)]
        total = s.ps("total")
        pre_ready, hidden_ready, gate_ready, product_ready, product_used, total_used, summed = map(
            s.sem, ("pre_ready", "hidden_ready", "gate_ready", "product_ready", "product_used", "total_used", "summed"))
        if gated_unit:
            raised = s.sb("raised", [128, HC, T])
            raised_ready = s.sem("raised_ready")
        spare = FREE * HC

        with nc.Block() as block:
            @block.gpsimd
            def _(pool):
                if extra is not None:
                    pool.tensor_tensor(X[:, :, :], X[:, :, :], extra[:, :, :], ALU.add).then_inc(summed, 1)

            @block.tensor
            def _(pe):
                pe.wait_ge(weights_loaded, 32)
                pe.sem_inc(product_used, spare)
                with pe.Fori(0, NT) as t:
                    def into_hidden(e):
                        n = t * E + e
                        for c in range(4):
                            if c < HC:
                                pe.wait_ge(hidden_ready, n * HC + c + 1)
                            else:
                                pe.wait_ge(raised_ready, n * HC + c - HC + 1 + HC)
                            pe.matmul(rows48(pre[c][:, 0:T]), w_in(e, c), tile(XF, t), start=True, stop=True).then_inc(pre_ready, 1)
                        pe.wait_ge(product_ready, (n + 1) * HC)
                        pe.matmul(gate[e % 2][:, 0:T], select[:, e, :], gate_rows[:, ds(t * T, T)], start=True, stop=True).then_inc(gate_ready, 1)

                    into_hidden(0)
                    into_hidden(1)
                    pe.wait_ge(total_used, t + 1)
                    if b2 is not None:
                        pe.matmul(total[:, 0:T], b2, gate_parts[:, ds(t * T, T)], start=True, stop=False)
                    for e in range(E):
                        for c in range(HC):
                            pe.wait_ge(product_ready, (t * E + e) * HC + c + 1 + spare)
                            pe.matmul(total[:, 0:T], w_out(e, c), product[e % 2][:, c, :], start=b2 is None and e == 0 and c == 0,
                                      stop=e == E - 1 and c == HC - 1).then_inc(product_used, 1)
                        if e + 2 < E:
                            into_hidden(e + 2)

            @block.scalar
            def _(act):
                act.preload_act_table(act_func)
                act.sem_inc(hidden_ready, HC)
                hidden_used = raised_ready if gated_unit else product_ready
                with act.Fori(0, NT) as t:
                    for e in range(E):
                        n = t * E + e
                        for c in range(HC):
                            act.wait_ge(pre_ready, n * 4 + c + 1)
                            act.wait_ge(hidden_used, n * HC + c + 1)
                            act.activation(hidden[e % 2][:, c, :], pre[c][:, 0:T], act_func, bias=b1(e, c) if b1 else 0.0).then_inc(hidden_ready, 1)

            @block.vector
            def _(dve):
                dve.sem_inc(product_ready, spare)
                if gated_unit:
                    dve.sem_inc(raised_ready, spare)
                dve.sem_inc(total_used, 1)
                if extra is not None:
                    dve.wait_ge(summed, 1)
                with dve.Fori(0, NT) as t:
                    for e in range(E):
                        n = t * E + e
                        factor = hidden[e % 2]
                        if gated_unit:
                            factor = raised
                            dve.wait_ge(product_ready, n * HC + spare)
                            for c in range(HC):
                                dve.wait_ge(hidden_ready, n * HC + c + 1 + HC)
                                dve.wait_ge(pre_ready, n * 4 + HC + c + 1)
                                dve.tensor_tensor(raised[:, c, :], hidden[e % 2][:, c, :], pre[HC + c][:, 0:T], ALU.mult).then_inc(raised_ready, 1)
                        dve.wait_ge(gate_ready, n + 1)
                        for c in range(HC):
                            if gated_unit:
                                dve.wait_ge(raised_ready, n * HC + c + 1 + spare)
                            else:
                                dve.wait_ge(hidden_ready, n * HC + c + 1 + HC)
                            dve.wait_ge(product_used, n * HC + c + 1)
                            dve.tensor_tensor(product[e % 2][:, c, :], factor[:, c, :], gate[e % 2][:, 0:T], ALU.mult).then_inc(product_ready, 1)
                    dve.wait_ge(product_used, (t + 1) * (E * HC) + spare)
                    dve.tensor_tensor(tile(X, t), tile(X, t), rows48(total[:, 0:T]), ALU.add).then_inc(total_used, 1)


def attention(nc, P, XN, X, spare):
    KEYS = H * W
    KC = KEYS // 128
    THIRD = KC // CH
    GROUPS = KEYS // T
    bank_cols = [512, 512, 512, 512, 256]
    with Stage(nc, "at") as s:
        both = s.sb("both", [32 + DH, NTOK])
        k, q = both[0:DH, :], both[32:32 + DH, :]
        v = s.sb("v", [128, NC, C])
        with ExitStack() as first:
            proj = [first.enter_context(nc.psum_tensor(f"at_proj{u}", [128, 512], F32)) for u in range(2)]
            values = [first.enter_context(nc.psum_tensor(f"at_values{u}", [128, 512], F32)) for u in range(2)]
            projected, proj_used, valued, values_used = map(s.sem, ("projected", "proj_used", "valued", "values_used"))
            with nc.Block() as block:
                @block.tensor
                def _(pe):
                    for t in range(NT):
                        for m, (weights, m0) in enumerate(((P("wq"), 32), (P("wk"), 0))):
                            if t:
                                pe.wait_ge(proj_used, 2 * t - 1 + m)
                            pe.matmul(rows48(proj[m][m0:m0 + DH, 0:T]), weights, XN[:, t * TR:(t + 1) * TR, :], start=True, stop=True).then_inc(projected, 1)
                        if t >= 2:
                            pe.wait_ge(values_used, t - 1)
                        for j in range(CH):
                            last = pe.matmul(values[t % 2][:, j * C:(j + 1) * C], chunk(XN, t * CH + j), P("wv"), start=True, stop=True)
                        last.then_inc(valued, 1)

                @block.scalar
                def _(act):
                    for t in range(NT):
                        for m, (out, bias, m0) in enumerate(((q, "bq", 32), (k, "bk", 0))):
                            act.wait_ge(projected, 2 * t + m + 1)
                            act.activation(out[:, t * T:(t + 1) * T], proj[m][m0:m0 + DH, 0:T], ACT.Identity, bias=P(bias)[m0:m0 + DH, :]).then_inc(proj_used, 1)

                @block.vector
                def _(dve):
                    for t in range(NT):
                        dve.wait_ge(valued, t + 1)
                        dve.tensor_copy(v[:, t * CH:(t + 1) * CH, :].rearrange("p n c -> p (n c)"), values[t % 2][:, 0:T]).then_inc(values_used, 1)

        staged_q = [s.sb(f"staged_q{u}", [DH, T]) for u in range(2)]
        probs = [XN[:, u * H:(u + 1) * H, :].rearrange("p r w -> p (r w)") for u in range(2)]
        turned = [s.sb("turned", [128, KC, T])[:, :, :], spare[:, 0:KC * T].rearrange("p (m q) -> p m q", q=T)]
        peaks = s.sb("peaks", [128, 5])
        minus_peak = [s.sb(f"minus_peak{u}", [128, 1]) for u in range(2)]
        total = [s.sb(f"total{u}", [128, 1]) for u in range(2)]
        inv = [s.sb(f"inv{u}", [128, 1]) for u in range(2)]
        inv_all = [s.sb(f"inv_all{u}", [128, T]) for u in range(2)]
        normed = s.sb("normed", [128, TR, W])
        scores = s.ps("scores", [128, 2560])
        turning = [s.ps(f"turning{u}") for u in range(2)]
        mixed = s.ps("mixed")
        q_staged, scored, reduced, peaked, exped, inv_ready, turned_ready, act_evacuated, dve_evacuated, mixed_ready, added, mixed_used = map(
            s.sem, ("q_staged", "scored", "reduced", "peaked", "exped", "inv_ready", "turned_ready", "act_evacuated", "dve_evacuated",
                    "mixed_ready", "added", "mixed_used"))
        TURNS = KC // CH + 1
        BY_ACT, BY_DVE = TURNS // 2, TURNS - TURNS // 2
        SCORE_CREDIT = FREE * CH * 5

        def groups(engine):
            for b in range(B):
                yield b * GROUPS, 0, b, b - 1 if b else None
                with engine.Fori(0, GROUPS // 2 - 1) as i:
                    yield i * 2 + (b * GROUPS + 1), 1, b, b
                    yield i * 2 + (b * GROUPS + 2), 0, b, b
                yield b * GROUPS + GROUPS - 1, 1, b, b

        with nc.Block() as block:
            @block.gpsimd
            def _(pool):
                for g, par, b, last_b in groups(pool):
                    pool.wait_ge(scored, (g + 1) * (CH * 5))
                    pool.tensor_copy(staged_q[par][:, :], q[:, ds(g * T, T)]).then_inc(q_staged, 1)

            @block.tensor
            def _(pe):
                pe.sem_inc(scored, SCORE_CREDIT)

                def weigh(par, image, third):
                    for m in range(third * THIRD, (third + 1) * THIRD):
                        last = pe.matmul(mixed[:, 0:T], v[:, image * KC + m, :], turned[par][:, m, :], start=m == 0, stop=m == KC - 1)
                    if third == CH - 1:
                        last.then_inc(mixed_ready, 1)

                for g, par, b, last_b in groups(pe):
                    for c in range(CH):
                        n, np = g * CH + c, (par + c) % 2
                        if c == 0:
                            pe.wait_ge(q_staged, g + 1)
                        pe.wait_ge(exped, n + 1)
                        for j, cols in enumerate(bank_cols):
                            pe.matmul(scores[:, j * 512:j * 512 + cols], staged_q[par][:, c * 128:(c + 1) * 128],
                                      k[:, b * KEYS + j * 512:b * KEYS + j * 512 + cols], start=True, stop=True).then_inc(scored, 1)
                        if last_b is not None:
                            if c == 0:
                                pe.wait_ge(act_evacuated, g * (CH * BY_ACT) + BY_ACT)
                                pe.wait_ge(dve_evacuated, g * (CH * BY_DVE) + BY_DVE)
                                pe.wait_ge(mixed_used, g)
                            weigh(1 - par, last_b, c)
                        pe.wait_ge(exped, n + 1 + 1)
                        for j in range(TURNS):
                            bank = turning[(np + j) % 2]
                            if j % 2 == (1 if j > 1 else 0):
                                pe.wait_ge(act_evacuated, n * BY_ACT + (BY_ACT if j == 0 else BY_ACT + j // 2))
                            else:
                                pe.wait_ge(dve_evacuated, n * BY_DVE + (BY_DVE if j == 1 else BY_DVE + j // 2))
                            if j < TURNS - 1:
                                for m in range(CH):
                                    last = pe.transpose(bank[:, m * 128:(m + 1) * 128], probs[np][:, (j * CH + m) * 128:(j * CH + m + 1) * 128], P("identity"))
                            else:
                                pe.wait_ge(inv_ready, n + 1)
                                last = pe.transpose(bank[:, 0:128], inv[np][:, 0:1].broadcast_to([128, 128]), P("identity"))
                            last.then_inc(turned_ready, 1)
                pe.wait_ge(act_evacuated, B * GROUPS * CH * BY_ACT + BY_ACT)
                pe.wait_ge(dve_evacuated, B * GROUPS * CH * BY_DVE + BY_DVE)
                pe.wait_ge(mixed_used, B * GROUPS)
                for third in range(CH):
                    weigh(1, B - 1, third)

            @block.scalar
            def _(act):
                act.preload_act_table(ACT.Exp)
                act.sem_inc(exped, 1)
                act.sem_inc(act_evacuated, BY_ACT)
                for g, par, b, last_b in groups(act):
                    for c in range(CH):
                        n, np = g * CH + c, (par + c) % 2
                        act.wait_ge(peaked, n + 1 + 1)
                        act.activation(probs[np][:, :], scores[:, 0:KEYS], ACT.Exp, bias=minus_peak[np][:, 0:1],
                                       accum_out=total[np][:, 0:1]).then_inc(exped, 1)
                        for j in range(1, TURNS, 2):
                            act.wait_ge(turned_ready, n * TURNS + j + 1)
                            act.activation(turned[par][:, j * CH:(j + 1) * CH, c * 128:(c + 1) * 128],
                                           turning[(np + j) % 2][:, 0:T].rearrange("p (m q) -> p m q", q=128), ACT.Copy).then_inc(act_evacuated, 1)

            @block.vector
            def _(dve):
                dve.sem_inc(dve_evacuated, BY_DVE)
                dve.sem_inc(mixed_used, 1)
                dve.sem_inc(peaked, 1)
                dve.sem_inc(added, 1)

                def finish(g, par):
                    dve.wait_ge(added, g + 1)
                    dve.wait_ge(mixed_ready, g + 1)
                    dve.wait_ge(dve_evacuated, (g + 1) * (CH * BY_DVE) + BY_DVE)
                    dve.tensor_tensor(normed[:, :, :], rows48(mixed[:, 0:T]), rows48(inv_all[par][:, :]), ALU.mult).then_inc(mixed_used, 1)
                    dve.wait_ge(mixed_used, g + 2)
                    dve.scalar_tensor_tensor(tile(X, g), normed[:, :, :], P("bv"), tile(X, g), ALU.add, ALU.add).then_inc(added, 1)

                for g, par, b, last_b in groups(dve):
                    for c in range(CH):
                        n, np = g * CH + c, (par + c) % 2
                        dve.wait_ge(peaked, n + 1)
                        for j, cols in enumerate(bank_cols):
                            dve.wait_ge(scored, n * 5 + j + 1 + SCORE_CREDIT)
                            last = dve.tensor_reduce(peaks[:, j:j + 1], scores[:, j * 512:j * 512 + cols], AX.X, ALU.max)
                        last.then_inc(reduced, 1)
                        dve.wait_ge(reduced, n + 1)
                        dve.tensor_reduce(minus_peak[np][:, 0:1], peaks[:, :], AX.X, ALU.max, negate=True).then_inc(peaked, 1)
                        dve.wait_ge(exped, n + 1 + 1)
                        dve.reciprocal(inv[np][:, :], total[np][:, :]).then_inc(inv_ready, 1)
                        for j in range(0, TURNS, 2):
                            dve.wait_ge(turned_ready, n * TURNS + j + 1)
                            bank = turning[(np + j) % 2]
                            if j < TURNS - 1:
                                dve.tensor_copy(turned[par][:, j * CH:(j + 1) * CH, c * 128:(c + 1) * 128],
                                                bank[:, 0:T].rearrange("p (m q) -> p m q", q=128)).then_inc(dve_evacuated, 1)
                            else:
                                dve.tensor_copy(inv_all[par][:, c * 128:(c + 1) * 128], bank[:, 0:128]).then_inc(dve_evacuated, 1)
                    if last_b is not None:
                        finish(g - 1, 1 - par)
                finish(B * GROUPS - 1, 1)


def dynamic_conv(nc, P, XN, X):
    TAPS = 10
    CM = 32
    with Stage(nc, "dc") as s:
        F = s.sb("f", [128, B * PF, PF])
        filters = s.sb("filters", [128, B, TAPS, C])
        sums, mean, g = (s.sb(n, [128, B]) for n in ("sums", "mean", "g"))
        bias = s.sb("bias", [128, 1])
        kernels = [s.sb(f"kernel{m}", [128, B, TAPS]) for m in range(2)]
        middle = s.sb("middle", [128, TAPS])
        scratch = s.sb("scratch", [128, C])
        g_ps, bias_ps = s.ps("g_ps"), s.ps("bias_ps")
        pre = [s.ps(f"pre{u}") for u in range(2)]
        conv = [s.ps(f"conv{u}") for u in range(2)]
        zeroed, step, mean_ready, g_pre, g_ready, bias_pre, pre_ready, act_taken, dve_taken, filters_ready, f_ready, conv_ready, conv_used = map(
            s.sem, ("zeroed", "step", "mean_ready", "g_pre", "g_ready", "bias_pre", "pre_ready", "act_taken", "dve_taken",
                    "filters_ready", "f_ready", "conv_ready", "conv_used"))

        def copy_of_f(t, j):
            b, i = t // TB, t % TB
            row = b * PF + i * TR + 2
            first = 1 if j == 3 else 0
            return F[j * CM:(j + 1) * CM, row:row + TR, first + 2 - j:2 - j + W], first

        with nc.Block() as block:
            @block.gpsimd
            def _(pool):
                pool.memset(F[:, :, :], 0.0).then_inc(zeroed, 1)

            @block.tensor
            def _(pe):
                for t in range(NT):
                    if t >= 2:
                        pe.wait_ge(act_taken, t - 1)
                        pe.wait_ge(dve_taken, t - 1)
                    pe.matmul(rows48(pre[t % 2][:, 0:T]), P("conv_w"), XN[:, t * TR:(t + 1) * TR, :], start=True, stop=True).then_inc(pre_ready, 1)
                pe.matmul(bias_ps[:, 0:1], P("fuse1", rows=CM), P("adap_b", rows=CM), start=True, stop=False)
                pe.matmul(bias_ps[:, 0:1], P("fuse2", rows=CM), P("atrous_b", rows=CM), start=False, stop=True).then_inc(bias_pre, 1)
                pe.wait_ge(mean_ready, 1)
                pe.matmul(g_ps[:, 0:B], P("conv_w"), mean[:, :], start=True, stop=True).then_inc(g_pre, 1)
                pe.wait_ge(filters_ready, 1)
                pe.wait_ge(act_taken, NT)
                pe.wait_ge(dve_taken, NT)
                for b in range(B):
                    with pe.Fori(0, TB // 2) as i:
                        for u in range(2):
                            t = i * 2 + (b * TB + u)
                            pe.wait_ge(conv_used, t + 1)
                            for tap in range(TAPS):
                                last = pe.matmul(rows48(conv[u][:, 0:T]), filters[:, b, tap, :],
                                                 F[:, ds(i * (2 * TR) + (b * PF + u * TR + tap % 5), TR), 4 * (tap // 5):4 * (tap // 5) + W],
                                                 start=tap == 0, stop=tap == TAPS - 1)
                            last.then_inc(conv_ready, 1)

            @block.scalar
            def _(act):
                act.preload_act_table(ACT.Relu)
                act.wait_ge(zeroed, 1)
                for t in range(NT):
                    act.wait_ge(pre_ready, t + 1)
                    for j in range(2):
                        target, first = copy_of_f(t, j)
                        last = act.activation(target, rows48(pre[t % 2][j * CM:(j + 1) * CM, 0:T])[:, :, first:W], ACT.Relu,
                                              bias=P("conv_b")[j * CM:(j + 1) * CM, :])
                    last.then_inc(act_taken, 1)
                act.wait_ge(g_pre, 1)
                act.activation(g[:, :], g_ps[:, 0:B], ACT.Relu, bias=P("conv_b")).then_inc(g_ready, 1)

            @block.vector
            def _(dve):
                link = Chain(dve, step)
                for b in range(B):
                    last = dve.tensor_reduce(sums[:, b:b + 1], XN[:, b * H:(b + 1) * H, :].rearrange("p r w -> p (r w)"), AX.X, ALU.add)
                link(last)
                dve.tensor_scalar(mean[:, :], sums[:, :], 1.0 / (H * W), None, ALU.mult).then_inc(mean_ready, 1)
                dve.wait_ge(zeroed, 1)
                for t in range(NT):
                    dve.wait_ge(pre_ready, t + 1)
                    for j in range(2, 4):
                        target, first = copy_of_f(t, j)
                        last = dve.tensor_scalar(target, rows48(pre[t % 2][j * CM:(j + 1) * CM, 0:T])[:, :, first:W],
                                                 P("conv_b")[j * CM:(j + 1) * CM, :], 0.0, ALU.add, ALU.max)
                    last.then_inc(dve_taken, 1)
                dve.wait_ge(bias_pre, 1)
                link(dve.tensor_scalar(bias[:, :], bias_ps[:, 0:1], P("fuse_b"), None, ALU.add))
                dve.wait_ge(g_ready, 1)
                for kernel, w, kb, mix, mix_b, valid in ((kernels[0], "kernel_w", "kernel_b", "k_w", "k_b", "tap5"),
                                                         (kernels[1], "kernel2_w", "kernel2_b", "k2_w", "k2_b", "tap3")):
                    for b in range(B):
                        link(dve.scalar_tensor_tensor(kernel[:, b, :], P(w), g[:, b:b + 1], P(kb), ALU.mult, ALU.add))
                    link(dve.tensor_tensor(middle[:, :], kernel[:, 0, :], kernel[:, 1, :], ALU.add))
                    link(dve.tensor_scalar(middle[:, :], middle[:, :], 1.0 / B, None, ALU.mult))
                    link(dve.tensor_scalar(middle[:, :], middle[:, :], P(mix, first=1, width=1), P(mix_b), ALU.mult, ALU.add))
                    for b in range(B):
                        link(dve.scalar_tensor_tensor(kernel[:, b, :], kernel[:, b, :], P(mix, width=1), middle[:, :], ALU.mult, ALU.add))
                        link(dve.scalar_tensor_tensor(kernel[:, b, :], kernel[:, b, :], 0.0, P(valid), ALU.max, ALU.mult))
                for b in range(B):
                    for tap in range(TAPS):
                        link(dve.tensor_scalar(scratch[:, :], P("fuse2"), kernels[1][:, b, tap:tap + 1], None, ALU.mult))
                        link(dve.scalar_tensor_tensor(filters[:, b, tap, :], P("fuse1"), kernels[0][:, b, tap:tap + 1], scratch[:, :], ALU.mult, ALU.add))
                dve.sem_inc(filters_ready, 1)
                dve.sem_inc(conv_used, FREE)
                with dve.Fori(0, NT // 2) as i:
                    for u in range(2):
                        t = i * 2 + u
                        dve.wait_ge(conv_ready, t + 1)
                        dve.scalar_tensor_tensor(tile(X, t), rows48(conv[u][:, 0:T]), bias[:, 0:1], tile(X, t), ALU.add, ALU.add).then_inc(conv_used, 1)


def quantised(nc, P, U, X):
    ROUND = 12582912.0
    with Stage(nc, "qf") as s:
        sums, totals = s.sb("sums", [128, 2]), s.sb("totals", [128, 2])
        shifted, sign, weight = (s.sb(n, [128, C]) for n in ("shifted", "sign", "weight"))
        y = [s.sb(f"y{u}", [128, TR, W]) for u in range(2)]
        level = [s.sb(f"level{u}", [128, TR, W]) for u in range(2)]
        sums_ps = s.ps("sums_ps")
        product = [s.ps(f"product{u}") for u in range(2)]
        step, sums_ready, totals_ready, shifted_ready, sign_ready, weight_ready, product_ready, y_ready, y_used, rounding = map(
            s.sem, ("step", "sums_ready", "totals_ready", "shifted_ready", "sign_ready", "weight_ready", "product_ready", "y_ready", "y_used", "rounding"))
        with nc.Block() as block:
            @block.tensor
            def _(pe):
                pe.wait_ge(sums_ready, 1)
                pe.matmul(sums_ps[:, 0:2], P("ones"), sums[:, :], start=True, stop=True).then_inc(totals_ready, 1)
                pe.wait_ge(weight_ready, 1)
                with pe.Fori(0, NT // 2) as i:
                    for u in range(2):
                        t = i * 2 + u
                        pe.wait_ge(y_ready, t + 1)
                        pe.matmul(rows48(product[u][:, 0:T]), weight[:, :], tile(U, t), start=True, stop=True).then_inc(product_ready, 1)

            @block.scalar
            def _(act):
                act.preload_act_table(ACT.Sign)
                act.sem_inc(y_ready, FREE)
                act.wait_ge(shifted_ready, 1)
                act.activation(sign[:, :], shifted[:, :], ACT.Sign).then_inc(sign_ready, 1)
                with act.Fori(0, NT // 2) as i:
                    for u in range(2):
                        t = i * 2 + u
                        act.wait_ge(product_ready, t + 1)
                        act.wait_ge(y_used, t + 1)
                        act.activation(y[u][:, :, :], rows48(product[u][:, 0:T]), ACT.Identity, bias=P("b2f")).then_inc(y_ready, 1)

            @block.vector
            def _(dve):
                link = Chain(dve, step)
                dve.tensor_reduce(sums[:, 0:1], P("w2f"), AX.X, ALU.add)
                dve.tensor_reduce(sums[:, 1:2], P("w2f"), AX.X, ALU.add, apply_absolute_value=True).then_inc(sums_ready, 1)
                dve.wait_ge(totals_ready, 1)
                link(dve.tensor_scalar(totals[:, :], sums_ps[:, 0:2], 1.0 / (C * C), None, ALU.mult))
                dve.tensor_scalar(shifted[:, :], P("w2f"), totals[:, 0:1], None, ALU.subtract).then_inc(shifted_ready, 1)
                dve.wait_ge(sign_ready, 1)
                link(dve.tensor_tensor(weight[:, :], sign[:, :], P("w2f"), ALU.subtract))
                link(dve.tensor_tensor(weight[:, :], weight[:, :], P("w2f"), ALU.add))
                dve.tensor_scalar(weight[:, :], weight[:, :], totals[:, 1:2], None, ALU.mult).then_inc(weight_ready, 1)
                dve.sem_inc(y_used, FREE)
                dve.sem_inc(rounding, 1)
                with dve.Fori(0, NT // 2) as i:
                    dve.wait_ge(rounding, i * 10 + 1)
                    for u in range(2):
                        dve.wait_ge(y_ready, i * 2 + (u + 1 + FREE))
                        dve.tensor_scalar(level[u][:, :, :], y[u][:, :, :], 1.0, -1.0, ALU.min, ALU.max).then_inc(rounding, 1)
                    for k in range(5):
                        for u in range(2):
                            if k < 4:
                                dve.wait_ge(rounding, i * 10 + (2 * k + u + 1 + 1))
                            else:
                                dve.wait_ge(y_used, i * 2 + (u + 1 + FREE))
                            if k == 0:
                                done = dve.tensor_scalar(level[u][:, :, :], level[u][:, :, :], 7.0, ROUND, ALU.mult, ALU.add)
                            elif k == 1:
                                done = dve.tensor_scalar(level[u][:, :, :], level[u][:, :, :], ROUND, 1.0 / 7.0, ALU.subtract, ALU.mult)
                            elif k == 2:
                                done = dve.tensor_tensor(level[u][:, :, :], level[u][:, :, :], y[u][:, :, :], ALU.subtract)
                            elif k == 3:
                                done = dve.tensor_tensor(level[u][:, :, :], level[u][:, :, :], y[u][:, :, :], ALU.add)
                            else:
                                done = dve.tensor_tensor(tile(X, i * 2 + u), tile(X, i * 2 + u), level[u][:, :, :], ALU.add)
                            done.then_inc(y_used if k == 3 else rounding, 1)


def pruned(nc, P, XN, X):
    with Stage(nc, "pr") as s:
        XP = s.sb("xp", [128, B * PW, PW])
        acc = s.sb("acc", [128, H, W])
        H1 = s.sb("h1", [128, ROWS, W])
        diagonal = s.sb("diagonal", [128, 9, 128])
        weight = s.sb("weight", [128, B, C])
        shifted, inv, root, gain, shift = (s.sb(n, [128, 2]) for n in ("shifted", "inv", "root", "gain", "shift"))
        peak, keep = (s.sb(n, [128, 2, B]) for n in ("peak", "keep"))
        conv = [s.ps(f"conv{u}") for u in range(2)]
        zeroed, step, padded, inv_ready, root_ready, affine, diagonal_ready, conv_ready, conv_used, acc_ready, h1_ready = map(
            s.sem, ("zeroed", "step", "padded", "inv_ready", "root_ready", "affine", "diagonal_ready", "conv_ready", "conv_used", "acc_ready", "h1_ready"))
        weight_ready, mixed_ready, h2_ready = map(s.sem, ("weight_ready", "mixed_ready", "h2_ready"))
        image = lambda tensor, b: tensor[:, b * H:(b + 1) * H, :]
        with nc.Block() as block:
            @block.gpsimd
            def _(pool):
                pool.memset(XP[:, :, :], 0.0).then_inc(zeroed, 1)

            @block.tensor
            def _(pe):
                pe.wait_ge(diagonal_ready, 1)
                pe.wait_ge(padded, 2)
                with pe.Fori(0, TB // 2) as i:
                    for u in range(2):
                        pe.wait_ge(conv_used, i * 2 + (u + 1))
                        for tap in range(9):
                            last = pe.matmul(rows48(conv[u][:, 0:T]), diagonal[:, tap, :],
                                             XP[:, ds(i * (2 * TR) + (PW + u * TR + tap // 3), TR), tap % 3:tap % 3 + W], start=tap == 0, stop=tap == 8)
                        last.then_inc(conv_ready, 1)
                for b in range(B):
                    pe.wait_ge(weight_ready, b + 1)
                    with pe.Fori(0, TB // 2) as i:
                        for u in range(2):
                            pe.wait_ge(conv_used, i * 2 + (TB * (b + 1) + u + 1))
                            pe.matmul(rows48(conv[u][:, 0:T]), weight[:, b, :], tile(H1, i * 2 + (b * TB + u)), start=True, stop=True).then_inc(mixed_ready, 1)

            @block.scalar
            def _(act):
                act.preload_act_table(ACT.Sqrt)
                act.sem_inc(conv_used, FREE)
                act.wait_ge(zeroed, 1)
                for b in range(B):
                    act.activation(XP[:, b * PW + 1:b * PW + 1 + H, 1:1 + W], image(XN, b), ACT.Copy).then_inc(padded, 1)
                act.wait_ge(inv_ready, 1)
                act.activation(root[:, :], inv[:, :], ACT.Sqrt).then_inc(root_ready, 1)
                act.wait_ge(affine, 1)
                with act.Fori(0, TB // 2) as i:
                    for u in range(2):
                        act.wait_ge(conv_ready, i * 2 + (u + 1))
                        act.activation(tile(H1, i * 2 + (TB + u)), rows48(conv[u][:, 0:T]), ACT.Relu, bias=shift[:, 0:1], scale=gain[:, 0:1]).then_inc(conv_used, 1)
                act.wait_ge(acc_ready, 1)
                act.activation(image(H1, 0), acc[:, :, :], ACT.Relu, bias=shift[:, 0:1], scale=gain[:, 0:1]).then_inc(h1_ready, 1)
                with act.Fori(0, NT // 2) as i:
                    for u in range(2):
                        act.wait_ge(mixed_ready, i * 2 + (u + 1))
                        act.activation(tile(H1, i * 2 + u), rows48(conv[u][:, 0:T]), ACT.Relu, bias=shift[:, 1:2], scale=gain[:, 1:2]).then_inc(conv_used, 1)

            @block.vector
            def _(dve):
                link = Chain(dve, step)
                for m in range(2):
                    last = dve.tensor_scalar(shifted[:, m:m + 1], P(f"bn{m + 1}_v"), 1e-5, None, ALU.add)
                link(last)
                dve.reciprocal(inv[:, :], shifted[:, :]).then_inc(inv_ready, 1)
                for tap in range(9):
                    last = dve.tensor_scalar(diagonal[:, tap, :], P("identity"), P("dw_w", first=tap, width=1), None, ALU.mult)
                last.then_inc(diagonal_ready, 1)
                dve.wait_ge(root_ready, 1)
                for m, bias in enumerate(("dw_b", "pw_b")):
                    link(dve.tensor_scalar(gain[:, m:m + 1], root[:, m:m + 1], P(f"bn{m + 1}_g"), None, ALU.mult))
                    link(dve.tensor_scalar(shift[:, m:m + 1], P(bias), P(f"bn{m + 1}_m"), None, ALU.subtract))
                    link(dve.tensor_scalar(shift[:, m:m + 1], shift[:, m:m + 1], gain[:, m:m + 1], P(f"bn{m + 1}_b"), ALU.mult, ALU.add))
                dve.sem_inc(affine, 1)
                dve.wait_ge(padded, 1)
                link(dve.tensor_scalar(acc[:, :, :], XP[:, 0:H, 0:W], P("dw_w", width=1), None, ALU.mult))
                for tap in range(1, 9):
                    done = dve.scalar_tensor_tensor(acc[:, :, :], XP[:, tap // 3:tap // 3 + H, tap % 3:tap % 3 + W], P("dw_w", first=tap, width=1),
                                                    acc[:, :, :], ALU.mult, ALU.add)
                    if tap < 8:
                        link(done)
                done.then_inc(acc_ready, 1)
                for b in range(B):
                    if b == 0:
                        dve.wait_ge(h1_ready, 1)
                    else:
                        dve.wait_ge(conv_used, TB + FREE)
                    link(dve.tensor_reduce(peak[:, 0, b:b + 1], image(H1, b).rearrange("p r w -> p (r w)"), AX.X, ALU.max))
                    link(dve.tensor_scalar(keep[:, 0, b:b + 1], peak[:, 0, b:b + 1], 4.0, None, ALU.is_ge))
                    dve.tensor_scalar(weight[:, b, :], P("pw"), keep[:, 0, b:b + 1], None, ALU.mult).then_inc(weight_ready, 1)
                for b in range(B):
                    dve.wait_ge(conv_used, TB * (b + 2) + FREE)
                    link(dve.tensor_reduce(peak[:, 1, b:b + 1], image(H1, b).rearrange("p r w -> p (r w)"), AX.X, ALU.max))
                    link(dve.tensor_scalar(keep[:, 1, b:b + 1], peak[:, 1, b:b + 1], 0.001, None, ALU.is_ge))
                    dve.scalar_tensor_tensor(image(X, b), image(H1, b), keep[:, 1, b:b + 1], image(X, b), ALU.mult, ALU.add)


def build(nc, x, params, identity16, masks, query_side, select_rows, wqkv_in, wout_in, w1_0, w2_0, b2_0, w1_1, w2_1, b2_1,
          w13_3, w2_3, out, first=0, last=8):
    HID = E * 4 * 128
    HID3 = E * 2 * 128
    with ExitStack() as ctx:
        sb = lambda name, shape, dt=F32: ctx.enter_context(nc.sbuf_tensor(name, shape, dt))
        X = sb("X", [128, ROWS, W])
        U = sb("U", [128, ROWS, W])
        params_sb = sb("params_sb", [128, PARAMS.width])
        ident16 = sb("ident16", [128, 128], BF16)
        select = sb("select", [128, E, 128], BF16)
        b2 = [sb(f"b2_{m}", [128, C]) for m in range(2)]
        store_a = sb("store_a", [128, 2 * HID])
        loaded, conv_loaded, loaded_0, loaded_1, loaded_3 = map(
            nc.alloc_semaphore, ("loaded", "conv_loaded", "loaded_0", "loaded_1", "loaded_3"))

        def P(name, rows=128, first=0, width=None):
            at, w = PARAMS[name]
            return params_sb[0:rows, at + first:at + first + (width or w - first)]

        def images(tensor):
            return tensor[:, :, :].rearrange("p (b r) w -> p b (r w)", b=B)

        wqkv = store_a[:, 0:27 * C]
        wout = store_a[:, 27 * C:36 * C]
        with nc.Block() as block:
            @block.sync
            def _(sp):
                sp.dma_start(images(X), x.rearrange("b c h w -> c b (h w)")).then_inc(loaded, 16)
                sp.dma_start(params_sb[:, :], params).then_inc(loaded, 16)
                sp.dma_start(wqkv, wqkv_in).then_inc(conv_loaded, 16)
                sp.dma_start(wout, wout_in).then_inc(conv_loaded, 16)
                sp.dma_start(ident16[:, :], identity16).then_inc(loaded, 16)
                sp.dma_start(select[:, :, :], select_rows).then_inc(loaded, 16)
                sp.dma_start(b2[0][:, :], b2_0).then_inc(loaded, 16)
                sp.dma_start(b2[1][:, :], b2_1).then_inc(loaded, 16)
                sp.wait_ge(loaded, 96)

        def halves(store, width):
            return store[:, 0:width], store[:, width:2 * width]

        if first <= 0 < last:
            with ExitStack() as layer:
                lsb = lambda name, shape: layer.enter_context(nc.sbuf_tensor(name, shape, F32))
                padded = lsb("padded", [128, B * PW, PW])
                Q = lsb("Q", [128, ROWS, W])
                KP = lsb("KP", [128, B * PK, PK])
                VP = lsb("VP", [128, B * PK, PK])
                layer_norm(nc, P, "ln0", X, 1e-6, U)
                group_norm(nc, P, U, padded)
                qkv(nc, P, padded, wqkv.rearrange("p (t c) -> p t c", t=9), conv_loaded, Q, KP, VP)
                neighbourhood(nc, P, Q, KP, VP, masks, query_side, padded)
                out_conv(nc, P, padded, wout.rearrange("p (t c) -> p t c", t=9), U, X)

        store_b = sb("store_b", [128, 2 * HID])

        def chunks(weights, per_expert):
            return lambda e, c: weights[:, (e * per_expert + c) * 128:(e * per_expert + c + 1) * 128]

        def mixture(name, XF, gate, bias, top, renormalise, store, width, act_func, b1, b2, weights_loaded, extra=None, gated_unit=False):
            w_in, w_out = store
            with nc.sbuf_tensor(f"{name}_rows", [128, NTOK], BF16) as rows, nc.sbuf_tensor(f"{name}_parts", [128, NTOK], F32) as parts:
                route(nc, P, f"{name}r", XF, gate, bias, top, renormalise, rows, parts, ident16[:, :])
                experts(nc, f"{name}e", XF, chunks(w_in, 4), act_func, b1, chunks(w_out, width), b2, rows, parts, select, X,
                        weights_loaded, extra, gated_unit)

        if first <= 1 < last:
            with nc.sbuf_tensor("V", [128, ROWS, W], F32) as V:
                layer_norm(nc, P, "ln1", X, 1e-5, U, second=(V, 1e-5),
                           loads=list(zip(halves(store_a, HID) + halves(store_b, HID), (w1_0, w2_0, w1_1, w2_1), (loaded_0, loaded_0, loaded_1, loaded_1))))
                mixture("m1", V, P("gate_0"), None, 2, False, halves(store_a, HID), 4, ACT.Gelu,
                        lambda e, c: P("b1_0", first=e * 4 + c, width=1), b2[0][:, :], loaded_0, extra=U)
        if first <= 2 < last:
            layer_norm(nc, P, "ln2", X, 1e-6, U)
            attention(nc, P, U, X, store_a)
        if first <= 3 < last:
            if first > 1:
                loads = list(zip(halves(store_b, HID), (w1_1, w2_1), (loaded_1, loaded_1)))
            else:
                loads = []
            layer_norm(nc, P, "ln3", X, 1e-5, U, loads=loads + list(zip((store_a[:, 0:2 * HID3], store_a[:, 2 * HID3:3 * HID3]), (w13_3, w2_3), (loaded_3, loaded_3))))
            mixture("m3", U, P("gate_1"), P("br"), 1, False, halves(store_b, HID), 4, ACT.Gelu,
                    lambda e, c: P("b1_1", first=e * 4 + c, width=1), b2[1][:, :], loaded_1)
        if first <= 4 < last:
            layer_norm(nc, P, "ln4", X, 1e-6, U)
            dynamic_conv(nc, P, U, X)
        if first <= 5 < last:
            layer_norm(nc, P, "ln5", X, 1e-5, U)
            quantised(nc, P, U, X)
        if first <= 6 < last:
            layer_norm(nc, P, "ln6", X, 1e-6, U)
            pruned(nc, P, U, X)
        if first <= 7 < last:
            loads = list(zip((store_a[:, 0:2 * HID3], store_a[:, 2 * HID3:3 * HID3]), (w13_3, w2_3), (loaded_3, loaded_3))) if first > 3 else []
            layer_norm(nc, P, "ln7", X, 1e-5, U, loads=loads)
            mixture("m7", U, P("gate_3"), None, 2, True, (store_a[:, 0:2 * HID3], store_a[:, 2 * HID3:3 * HID3]), 2, ACT.Silu,
                    None, None, loaded_3, gated_unit=True)
        with Stage(nc, "store") as s:
            stored = s.sem("stored")
            with nc.Block() as block:
                @block.sync
                def _(sp):
                    sp.dma_start(out.rearrange("b c h w -> c b (h w)"), images(X)).then_inc(stored, 16)
                    sp.wait_ge(stored, 16)


def _pack(given):
    import numpy as np
    f = np.float32
    groups = lambda n: np.kron(np.eye(128 // n, dtype=f), np.ones((n, n), f))
    head_of = np.kron(np.eye(NH, dtype=f), np.ones((DH, 1), f))
    tap5, tap3 = np.zeros((4, 32, 10), f), np.zeros((4, 32, 10), f)
    tap5[:, :, 0:5] = 1
    tap5[0, :, 5:10] = 1
    for row in (0, 2, 4):
        tap3[0, :, row] = tap3[2, :, row] = tap3[0, :, 5 + row] = 1

    def column(a):
        return np.asarray(a).reshape(-1, 1)

    def every(a):
        return np.repeat(np.asarray(a).reshape(1, -1), 128, axis=0)

    def below(a, *at):
        out = np.zeros((128, np.asarray(a).reshape(np.shape(a)[0], -1).shape[1]), f)
        for row in at:
            out[row:row + np.shape(a)[0]] = np.asarray(a).reshape(np.shape(a)[0], -1)
        return out

    def taps5(a):
        a = np.asarray(a).reshape(5, 5)
        out = np.zeros((4, 32, 10), f)
        for j in range(4):
            out[j, :, 0:5] = a[:, j]
        out[:, :, 5:10] = a[:, 4]
        return out.reshape(128, 10)

    def taps3(a):
        a = np.asarray(a).reshape(3, 3)
        out = np.zeros((5, 5), f)
        for r in range(3):
            for c in range(3):
                out[2 * r, 2 * c] = a[r, c]
        return taps5(out)

    g = given
    four = (0, 32, 64, 96)
    fuse = np.asarray(g["L2_conv_fuse_w"])[:, :, 0, 0].T
    values = {
        "identity": np.eye(128, dtype=f), "centering": (np.eye(128) - 1 / 128).astype(f), "ones": np.ones((128, 128), f),
        "group_mean": groups(8) / 8, "channel_mean": np.full((128, 1), 1 / 128, f), "head_of": head_of,
        "tap5": tap5.reshape(128, 10), "tap3": tap3.reshape(128, 10),
        "gn_w": column(g["L0_conv_gn_w"]), "gn_b": column(g["L0_conv_gn_b"]), "qkv_b": np.asarray(g["L0_conv_qkv_b"]).reshape(3, C).T,
        "scale": every(g["L0_conv_scale"]), "out_b": column(g["L0_conv_out_b"]),
        "ln_g": column(g["L0_ffn_ln_g"]), "ln_b": column(g["L0_ffn_ln_b"]),
        "b1_0": np.asarray(g["L0_ffn_b1"]).reshape(32, 128).T, "gate_0": g["L0_ffn_gate_w"],
        "bv": column(g["L1_conv_bv"]), "bq": below(g["L1_conv_bq"], 32), "bk": below(g["L1_conv_bk"], 0),
        "wq": np.asarray(g["L1_conv_Wq"]).T, "wk": np.asarray(g["L1_conv_Wk"]).T, "wv": np.asarray(g["L1_conv_Wv"]).T,
        "b1_1": np.asarray(g["L1_ffn_b1"]).reshape(32, 128).T, "gate_1": g["L1_ffn_Wr"], "br": every(g["L1_ffn_br"]),
        "conv_w": np.tile(np.asarray(g["L2_conv_conv_w"])[:, :, 0, 0].T, (1, 4)), "conv_b": below(g["L2_conv_conv_b"], *four),
        "k_w": every(g["L2_conv_conv_k_w"]), "k_b": every(g["L2_conv_conv_k_b"]),
        "k2_w": every(g["L2_conv_conv_k2_w"]), "k2_b": every(g["L2_conv_conv_k2_b"]),
        "kernel_w": taps5(g["L2_conv_conv_kernel_w"]), "kernel_b": taps5(g["L2_conv_conv_kernel_b"]),
        "kernel2_w": taps3(g["L2_conv_conv_kernel2_w"]), "kernel2_b": taps3(g["L2_conv_conv_kernel2_b"]),
        "fuse1": below(fuse[0:32], *four), "fuse2": below(fuse[32:64], *four),
        "adap_b": below(g["L2_conv_adap_bias"], 0), "atrous_b": below(g["L2_conv_atrous_bias"], 0), "fuse_b": column(g["L2_conv_fuse_b"]),
        "w2f": g["L2_ffn_weight"], "b2f": column(g["L2_ffn_bias"]),
        "dw_w": np.asarray(g["L3_conv_dw_w"]).reshape(128, 9), "dw_b": column(g["L3_conv_dw_b"]),
        "pw": np.asarray(g["L3_conv_pw_w"])[:, :, 0, 0].T, "pw_b": column(g["L3_conv_pw_b"]), "gate_3": g["L3_ffn_router_w"],
    }
    for n in (1, 2):
        for part in "gbmv":
            values[f"bn{n}_{part}"] = column(g[f"L3_conv_bn{n}_{part}"])
    packed = np.zeros((128, PARAMS.width), f)
    for name, (at, width) in PARAMS.at.items():
        packed[:, at:at + width] = np.asarray(values[name])
    return packed


def _window_masks():
    import numpy as np
    outside = np.zeros((NBLK, QB, WIN), np.float32)
    for block in range(NBLK):
        for y in range(QB):
            start = min(max(block * QB + y - 3, 0), H - 7) - (block * QB - 3)
            outside[block, y] = MASKED
            outside[block, y, start:start + 7] = 0
    keys = np.zeros((1 + 2 * QB, NBLK, NBLK, WIN, WIN), np.float32)
    keys[0] = 1
    for y in range(QB):
        keys[1 + y] = outside[:, y][:, None, :, None]
        keys[1 + QB + y] = outside[:, y][None, :, None, :]
    queries = np.zeros((1 + 2 * QB, NH, QB, QB), np.float32)
    for y in range(QB):
        queries[1 + y, :, y, :] = 1
        queries[1 + QB + y, :, :, y] = 1
    return (keys.reshape(1 + 2 * QB, NBLK * NBLK, WIN * WIN).astype("bfloat16"), queries.reshape(1 + 2 * QB, NH, QB * QB).astype("bfloat16"))


def _inputs(given):
    import numpy as np
    g = {name: np.asarray(a) for name, a in given.items()}

    def conv(a):
        return a.transpose(1, 2, 3, 0).reshape(C, -1)

    def into(a):
        return a.transpose(1, 0, 2).reshape(C, -1)

    def out_of(a):
        return a.reshape(E, -1, 128, C).transpose(2, 0, 1, 3).reshape(128, -1)

    masks, query_side = _window_masks()
    select = np.zeros((128, E, 128), np.float32)
    for part in range(3):
        select[part * E + np.arange(E), np.arange(E)] = 1

    def three(a):
        return np.concatenate([a, a, a, np.zeros((128 - 3 * E, C), a.dtype)])

    arrays = {
        "x": g["x"], "params": _pack(g), "identity16": np.eye(128, dtype=np.float32).astype("bfloat16"),
        "masks": masks, "query_side": query_side, "select": select.astype("bfloat16"),
        "wqkv": conv(g["L0_conv_qkv_w"]), "wout": conv(g["L0_conv_out_w"]),
        "w1_0": into(g["L0_ffn_w1"]), "w2_0": out_of(g["L0_ffn_w2"]), "b2_0": three(g["L0_ffn_b2"]),
        "w1_1": into(g["L1_ffn_W1"]), "w2_1": out_of(g["L1_ffn_W2"]), "b2_1": three(g["L1_ffn_b2"]),
        "w13_3": into(np.concatenate([g["L3_ffn_w1"], g["L3_ffn_w3"]], axis=2)), "w2_3": out_of(g["L3_ffn_w2"]),
    }
    return {f"in_{name}": np.ascontiguousarray(a) for name, a in arrays.items()}


def kernel(**given):
    import concourse.bacc as bacc
    from concourse.bass_utils import run_bass_kernel_spmd

    arrays = _inputs(given)
    nc = bacc.Bacc("TRN2", target_bir_lowering=False, num_devices=1)
    tensors = [nc.dram_tensor(name, a.shape, mybir.dt.from_np(a.dtype), kind="ExternalInput").ap() for name, a in arrays.items()]
    out = nc.dram_tensor("out", arrays["in_x"].shape, F32, kind="ExternalOutput").ap()
    build(nc, *tensors, out)
    return run_bass_kernel_spmd(nc, [arrays], core_ids=[0]).results[0]["out"]
```

```python
import concourse.bass as bass
from concourse import mybir
from concourse.alu_op_type import AluOpType as ALU
from contextlib import ExitStack, contextmanager

F32 = mybir.dt.float32
BF16 = mybir.dt.bfloat16
I32 = mybir.dt.int32
ACT = mybir.ActivationFunctionType
AX = mybir.AxisListType
ds = bass.ds

B, C, H, W = 2, 128, 48, 48
ROWS = B * H
TR = 8
T = TR * W
NT = ROWS // TR
TB = H // TR
NTOK = ROWS * W
NC = NTOK // 128
CH = T // 128
PW = W + 2
PF = W + 4
PK = W + 6
NH, DH = 8, 16
E = 8
QB = 8
WIN = QB + 6
KH = WIN * WIN // 2
NBLK = H // QB
VA = DH + 1
MASKED = -30000.0
FREE = 2
ROW = C + 4
GROUP = 4
TILES = {top: -(-((top * NTOK + E * 127) // 128) // GROUP) * GROUP for top in (1, 2)}
ROUND = 12582912.0


class Chain:

    def __init__(self, engine, semaphore):
        self.engine, self.semaphore, self.count = engine, semaphore, 0

    def __call__(self, instruction):
        self.count += 1
        instruction.then_inc(self.semaphore, 1)
        self.engine.wait_ge(self.semaphore, self.count)


class Params:

    def __init__(self, columns):
        self.at, n = {}, 0
        for name, width in columns:
            self.at[name] = (n, width)
            n += width
        self.width = n

    def __getitem__(self, name):
        return self.at[name]


PARAMS = Params([
    ("identity", 128), ("centering", 128), ("ones", 128), ("group_mean", 128), ("channel_mean", 1),
    ("earlier", 128), ("token", NC), ("tile_number", TILES[2]),
    ("head_of", NH), ("tap5", 10), ("tap3", 10),
    ("gn_w", 1), ("gn_b", 1), ("qkv_b", 3), ("scale", NH), ("out_b", 1), ("ln_g", 1), ("ln_b", 1),
    ("gate_0", E), ("bv", 1), ("bq", 1), ("bk", 1), ("wq", DH), ("wk", DH), ("wv", C),
    ("gate_1", E), ("br", E),
    ("conv_w", 128), ("conv_b", 1), ("k_w", 2), ("k_b", 1), ("k2_w", 2), ("k2_b", 1),
    ("kernel_w", 10), ("kernel_b", 10), ("kernel2_w", 10), ("kernel2_b", 10),
    ("fuse1", C), ("fuse2", C), ("adap_b", 1), ("atrous_b", 1), ("fuse_b", 1),
    ("w2f", C), ("b2f", 1),
    ("dw_w", 9), ("dw_b", 1), ("bn1_g", 1), ("bn1_b", 1), ("bn1_m", 1), ("bn1_v", 1),
    ("pw", C), ("pw_b", 1), ("bn2_g", 1), ("bn2_b", 1), ("bn2_m", 1), ("bn2_v", 1),
    ("gate_3", E),
])


class Stage:

    def __init__(self, nc, name):
        self.nc, self.name, self.sems, self.ctx = nc, name, [], ExitStack()

    def sb(self, name, shape, dt=F32):
        return self.ctx.enter_context(self.nc.sbuf_tensor(f"{self.name}_{name}", shape, dt))

    def ps(self, name, shape=(128, 512), dt=F32):
        return self.ctx.enter_context(self.nc.psum_tensor(f"{self.name}_{name}", list(shape), dt))

    def sem(self, name):
        s = self.nc.alloc_semaphore(f"{self.name}_{name}")
        self.sems.append(s)
        return s

    def __enter__(self):
        return self

    def __exit__(self, *error):
        if error[0] is None:
            self.nc.clear_and_free_semaphores(self.sems)
            self.nc.all_engine_barrier()
            self.ctx.close()


def rows48(ap):
    return ap.rearrange("p (r w) -> p r w", w=W)


def chunk(tensor, n):
    return tensor[:, :, :].rearrange("p r w -> p (r w)")[:, n * 128:(n + 1) * 128]


def along(ap, n):
    return ap.rearrange("p (a b) -> p a b", b=1).broadcast_to([ap.shape[0], ap.shape[1], n])


def tile(tensor, t):
    return tensor[:, ds(t * TR, TR), :]


def layer_norm(nc, P, name, X, eps, out, second=None, loads=()):
    with Stage(nc, name) as s:
        XC = s.sb("centred", [128, ROWS, W])
        squares = [s.sb(f"squares{u}", [128, TR, W]) for u in range(2)]
        spread = [s.sb(f"spread{u}", [128, CH, 128]) for u in range(2)]
        shifted, inv_var, rstd = (s.sb(n, [128, NC]) for n in ("shifted", "inv_var", "rstd"))
        cen = [s.ps(f"cen{u}") for u in range(2)]
        var = s.ps("var")
        bcast = [s.ps(f"bcast{u}") for u in range(2)]
        centred, copied, squared, squares_used = map(s.sem, ("centred", "copied", "squared", "squares_used"))
        step, root_in, root_out = map(s.sem, ("step", "root_in", "root_out"))
        spread_ready, turned, bcast_used = map(s.sem, ("spread_ready", "turned", "bcast_used"))
        if second:
            out2, eps2 = second
            shifted2, inv_var2, rstd2, both = (s.sb(n, [128, NC]) for n in ("shifted2", "inv_var2", "rstd2", "both"))
            spread2 = [s.sb(f"spread2{u}", [128, CH, 128]) for u in range(2)]
            scaled = [s.sb(f"scaled{u}", [128, TR, W]) for u in range(2)]
            bcast2 = [s.ps(f"bcast2{u}") for u in range(2)]
            scaled_ready, scaled_used = map(s.sem, ("scaled_ready", "scaled_used"))

        with nc.Block() as block:
            @block.sync
            def _(sp):
                for target, source, arrived in loads:
                    sp.dma_start(target, source).then_inc(arrived, 16)

            @block.tensor
            def _(pe):
                pe.sem_inc(squares_used, FREE)
                pe.sem_inc(turned, FREE)
                with pe.Fori(0, NT // 2) as i:
                    for u in range(2):
                        t = i * 2 + u
                        pe.wait_ge(copied, t + 1)
                        pe.matmul(cen[u][:, 0:T], P("centering"), tile(X, t), start=True, stop=True).then_inc(centred, 1)
                    for u in range(2):
                        t = i * 2 + u
                        pe.wait_ge(squared, t + 1)
                        for j in range(CH):
                            last = pe.matmul(var[:, ds(t * CH + j, 1)], chunk(squares[u], j), P("channel_mean"),
                                             start=True, stop=True)
                        last.then_inc(squares_used, 1)
                with pe.Fori(0, NT // 2) as i:
                    for u in range(2):
                        t = i * 2 + u
                        pe.wait_ge(spread_ready, t + 1)
                        pe.wait_ge(bcast_used, t + 1)
                        for j in range(CH):
                            last = pe.transpose(bcast[u][:, j * 128:(j + 1) * 128], spread[u][:, j, :], P("identity"))
                            if second:
                                last = pe.transpose(bcast2[u][:, j * 128:(j + 1) * 128], spread2[u][:, j, :], P("identity"))
                        last.then_inc(turned, 1)

            @block.scalar
            def _(act):
                act.preload_act_table(ACT.Sqrt)
                act.sem_inc(copied, FREE)
                with act.Fori(0, NT // 2) as i:
                    for u in range(2):
                        t = i * 2 + u
                        act.wait_ge(centred, t + 1)
                        act.activation(tile(XC, t), rows48(cen[u][:, 0:T]), ACT.Copy).then_inc(copied, 1)
                act.wait_ge(root_in, 1)
                act.activation(rstd[:, :], inv_var[:, :], ACT.Sqrt).then_inc(root_out, 1)
                if second:
                    act.wait_ge(root_in, 2)
                    act.activation(rstd2[:, :], inv_var2[:, :], ACT.Sqrt).then_inc(root_out, 1)
                    act.wait_ge(root_in, 3)
                    act.sem_inc(scaled_used, FREE)
                else:
                    act.wait_ge(root_out, 1)
                with act.Fori(0, NT // 2) as i:
                    for u in range(2):
                        t = i * 2 + u
                        act.wait_ge(turned, t + 1)
                        if second:
                            act.activation(spread2[u][:, :, :], along(both[:, ds(t * CH, CH)], 128), ACT.Copy)
                        act.activation(spread[u][:, :, :], along(rstd[:, ds(t * CH, CH)], 128), ACT.Copy).then_inc(spread_ready, 1)
                    for u in range(2 if second else 0):
                        t = i * 2 + u
                        act.wait_ge(scaled_ready, t + 1)
                        act.activation(tile(out2, t), scaled[u][:, :, :], ACT.Identity,
                                       bias=P("ln_b"), scale=P("ln_g")).then_inc(scaled_used, 1)

            @block.vector
            def _(dve):
                link = Chain(dve, step)
                with dve.Fori(0, NT // 2) as i:
                    for u in range(2):
                        t = i * 2 + u
                        dve.wait_ge(copied, t + 1 + FREE)
                        dve.wait_ge(squares_used, t + 1)
                        dve.tensor_tensor(squares[u][:, :, :], tile(XC, t), tile(XC, t), ALU.mult).then_inc(squared, 1)
                dve.wait_ge(squares_used, NT + FREE)
                link(dve.tensor_scalar(shifted[:, :], var[:, 0:NC], eps, None, ALU.add))
                dve.reciprocal(inv_var[:, :], shifted[:, :]).then_inc(root_in, 1)
                if second:
                    dve.wait_ge(root_in, 1)
                    link(dve.tensor_tensor(shifted2[:, :], inv_var[:, :], var[:, 0:NC], ALU.mult))
                    link(dve.tensor_scalar(shifted2[:, :], shifted2[:, :], eps2, None, ALU.add))
                    dve.reciprocal(inv_var2[:, :], shifted2[:, :]).then_inc(root_in, 1)
                    dve.wait_ge(root_out, 2)
                    dve.tensor_tensor(both[:, :], rstd[:, :], rstd2[:, :], ALU.mult).then_inc(root_in, 1)
                dve.sem_inc(bcast_used, FREE)
                with dve.Fori(0, NT // 2) as i:
                    for u in range(2):
                        t = i * 2 + u
                        dve.wait_ge(turned, t + 1 + FREE)
                        if second:
                            dve.wait_ge(scaled_used, t + 1)
                            dve.tensor_tensor(scaled[u][:, :, :], tile(XC, t), rows48(bcast2[u][:, 0:T]), ALU.mult).then_inc(scaled_ready, 1)
                        dve.tensor_tensor(tile(out, t), tile(XC, t), rows48(bcast[u][:, 0:T]), ALU.mult).then_inc(bcast_used, 1)


def group_norm(nc, P, XN, HP):
    with Stage(nc, "gn") as s:
        stats = s.sb("stats", [128, B, TB, 6])
        moments = s.sb("moments", [128, B, 2])
        square = s.sb("square", [128, B])
        group = s.sb("group", [128, B, 2])
        var, shifted, inv, rstd, gain, shift, drop = (
            s.sb(n, [128, B]) for n in ("var", "shifted", "inv", "rstd", "gain", "shift", "drop"))
        grouped = s.ps("grouped")
        step, moments_ready, grouped_ready, inv_ready, rstd_ready, affine_ready, zeroed = map(
            s.sem, ("step", "moments_ready", "grouped_ready", "inv_ready", "rstd_ready", "affine_ready", "zeroed"))
        with nc.Block() as block:
            @block.gpsimd
            def _(pool):
                pool.memset(HP[:, :, :], 0.0).then_inc(zeroed, 1)

            @block.vector
            def _(dve):
                link = Chain(dve, step)
                for b in range(B):
                    for t in range(TB):
                        last = dve.bn_stats(stats[:, b, t, :], XN[:, b * H + t * TR:b * H + (t + 1) * TR, :].rearrange("p r w -> p (r w)"))
                link(last)
                for b in range(B):
                    last = dve.bn_aggr(moments[:, b, :], stats[:, b, :, :].rearrange("p t s -> p (t s)"))
                link(last)
                link(dve.tensor_tensor(square[:, :], moments[:, :, 0], moments[:, :, 0], ALU.mult))
                dve.tensor_tensor(moments[:, :, 1], moments[:, :, 1], square[:, :], ALU.add).then_inc(moments_ready, 1)
                dve.wait_ge(grouped_ready, 1)
                link(dve.tensor_copy(group[:, :, :].rearrange("p b s -> p (b s)"), grouped[:, 0:2 * B]))
                link(dve.tensor_tensor(square[:, :], group[:, :, 0], group[:, :, 0], ALU.mult))
                link(dve.tensor_tensor(var[:, :], group[:, :, 1], square[:, :], ALU.subtract))
                link(dve.tensor_scalar(shifted[:, :], var[:, :], 1e-5, None, ALU.add))
                dve.reciprocal(inv[:, :], shifted[:, :]).then_inc(inv_ready, 1)
                dve.wait_ge(rstd_ready, 1)
                link(dve.tensor_scalar(gain[:, :], rstd[:, :], P("gn_w"), None, ALU.mult))
                link(dve.tensor_tensor(drop[:, :], group[:, :, 0], gain[:, :], ALU.mult))
                dve.tensor_scalar(shift[:, :], drop[:, :], -1.0, P("gn_b"), ALU.mult, ALU.add).then_inc(affine_ready, 1)
                dve.wait_ge(affine_ready, 1)
                dve.wait_ge(zeroed, 1)
                dve.tensor_scalar(HP[:, 1:1 + H, 1:1 + W], XN[:, 0:H, :], gain[:, 0:1], shift[:, 0:1], ALU.mult, ALU.add)

            @block.tensor
            def _(pe):
                pe.wait_ge(moments_ready, 1)
                pe.matmul(grouped[:, 0:2 * B], P("group_mean"), moments[:, :, :].rearrange("p b s -> p (b s)"),
                          start=True, stop=True).then_inc(grouped_ready, 1)

            @block.scalar
            def _(act):
                act.wait_ge(inv_ready, 1)
                act.activation(rstd[:, :], inv[:, :], ACT.Sqrt).then_inc(rstd_ready, 1)
                act.wait_ge(affine_ready, 1)
                act.wait_ge(zeroed, 1)
                act.activation(HP[:, PW + 1:PW + 1 + H, 1:1 + W], XN[:, H:2 * H, :], ACT.Identity,
                               bias=shift[:, 1:2], scale=gain[:, 1:2])


def qkv(nc, P, HP, wqkv, weights_loaded, Q, KP, VP):
    with Stage(nc, "qkv") as s:
        squares = [s.sb(f"squares{m}", [128, TR, W]) for m in range(2)]
        length = s.sb("length", [128, 2, NC, NH])
        inv = s.sb("inv", [128, 2, NC, NH])
        factor = s.sb("factor", [128, 2, NC, NH])
        spread = [s.sb(f"spread{m}", [128, CH, NH, DH]) for m in range(2)]
        conv = [s.ps(f"conv{c}") for c in range(3)]
        heads = [s.ps(f"heads{m}") for m in range(2)]
        bcast = [s.ps(f"bcast{m}") for m in range(2)]
        conv_ready, conv_used, evacuated, squared, squares_used, zeroed = map(
            s.sem, ("conv_ready", "conv_used", "evacuated", "squared", "squares_used", "zeroed"))
        step, inv_ready, factor_ready, spread_ready, turned, scaled = map(
            s.sem, ("step", "inv_ready", "factor_ready", "spread_ready", "turned", "scaled"))

        def in_key_image(image, b, i):
            return image[:, ds(b * PK + i * TR + 3, TR), 3:3 + W]

        with nc.Block() as block:
            @block.gpsimd
            def _(pool):
                pool.memset(KP[:, :, :], 0.0).then_inc(zeroed, 1)
                pool.memset(VP[:, :, :], 0.0).then_inc(zeroed, 1)

            @block.tensor
            def _(pe):
                pe.wait_ge(weights_loaded, 32)
                pe.sem_inc(squares_used, 1)
                with pe.Fori(0, B) as b, pe.Fori(0, TB) as i:
                    t = b * TB + i
                    for c in range(3):
                        pe.wait_ge(conv_used, t * 3 + c + 1)
                        for tap in range(9):
                            last = pe.matmul(rows48(conv[c][:, 0:T]), wqkv[:, tap, c * C:(c + 1) * C],
                                             HP[:, ds(b * PW + i * TR + tap // 3, TR), tap % 3:tap % 3 + W],
                                             start=tap == 0, stop=tap == 8)
                        last.then_inc(conv_ready, 1)
                    pe.wait_ge(squared, t + 1)
                    for m in range(2):
                        for j in range(CH):
                            last = pe.matmul(heads[m][:, ds((t * CH + j) * NH, NH)], chunk(squares[m], j), P("head_of"),
                                             start=True, stop=True)
                    last.then_inc(squares_used, 1)
                with pe.Fori(0, NT) as t:
                    for m in range(2):
                        pe.wait_ge(spread_ready, t * 2 + m + 1)
                        pe.wait_ge(scaled, t * 2 + m + 1)
                        for j in range(CH):
                            last = pe.transpose(bcast[m][:, j * 128:(j + 1) * 128],
                                                spread[m][:, j, :, :].rearrange("p h d -> p (h d)"), P("identity"))
                        last.then_inc(turned, 1)

            @block.scalar
            def _(act):
                act.preload_act_table(ACT.Sqrt)
                act.sem_inc(conv_used, 3)
                act.wait_ge(zeroed, 2)
                with act.Fori(0, B) as b, act.Fori(0, TB) as i:
                    t = b * TB + i
                    for c, target in enumerate((tile(Q, t), in_key_image(KP, b, i), in_key_image(VP, b, i))):
                        act.wait_ge(conv_ready, t * 3 + c + 1)
                        act.activation(target, rows48(conv[c][:, 0:T]), ACT.Identity, bias=P("qkv_b", first=c, width=1)).then_inc(conv_used, 1)
                act.wait_ge(inv_ready, 1)
                act.activation(factor[:, :, :, :].rearrange("p m n h -> p (m n h)"),
                               inv[:, :, :, :].rearrange("p m n h -> p (m n h)"), ACT.Sqrt).then_inc(factor_ready, 1)
                act.wait_ge(factor_ready, 1)
                act.sem_inc(turned, 2)
                with act.Fori(0, NT) as t:
                    for m in range(2):
                        act.wait_ge(turned, t * 2 + m + 1)
                        act.activation(spread[m][:, :, :, :].rearrange("p c h d -> p (c h) d"),
                                       along(factor[:, m, ds(t * CH, CH), :].rearrange("p n h -> p (n h)"), DH), ACT.Copy).then_inc(spread_ready, 1)

            @block.vector
            def _(dve):
                link = Chain(dve, step)
                with dve.Fori(0, B) as b, dve.Fori(0, TB) as i:
                    t = b * TB + i
                    dve.wait_ge(conv_used, t * 3 + 2 + 3)
                    dve.wait_ge(squares_used, t + 1)
                    dve.tensor_tensor(squares[0][:, :, :], tile(Q, t), tile(Q, t), ALU.mult)
                    dve.tensor_tensor(squares[1][:, :, :], in_key_image(KP, b, i), in_key_image(KP, b, i), ALU.mult).then_inc(squared, 1)
                dve.wait_ge(squares_used, NT + 1)
                for m in range(2):
                    last = dve.tensor_scalar(length[:, m, :, :].rearrange("p n h -> p (n h)"), heads[m][:, 0:NC * NH], 1e-6, None, ALU.add)
                link(last)
                link(dve.reciprocal(inv[:, :, :, :].rearrange("p m n h -> p (m n h)"), length[:, :, :, :].rearrange("p m n h -> p (m n h)")))
                scale = P("scale").rearrange("p (a h) -> p a h", a=1).broadcast_to([128, 2 * NC, NH])
                flat = inv[:, :, :, :].rearrange("p m n h -> p (m n) h")
                dve.tensor_tensor(flat, flat, scale, ALU.mult).then_inc(inv_ready, 1)
                dve.sem_inc(scaled, 2)
                dve.wait_ge(zeroed, 2)
                with dve.Fori(0, B) as b, dve.Fori(0, TB) as i:
                    t = b * TB + i
                    dve.wait_ge(turned, t * 2 + 1 + 2)
                    dve.tensor_tensor(tile(Q, t), tile(Q, t), rows48(bcast[0][:, 0:T]), ALU.mult).then_inc(scaled, 1)
                    dve.wait_ge(turned, t * 2 + 2 + 2)
                    dve.tensor_tensor(in_key_image(KP, b, i), in_key_image(KP, b, i), rows48(bcast[1][:, 0:T]), ALU.mult).then_inc(scaled, 1)


def neighbourhood(nc, P, Q, KP, VP, mask_dram, query_dram, OP):
    with Stage(nc, "na") as s:
        mask_all = s.sb("mask_all", [1 + 2 * QB, NBLK * NBLK, 2 * KH], BF16)
        query_side = s.sb("query_side", [1 + 2 * QB, NH, QB * QB], BF16)
        mask = [s.sb(f"mask{u}", [1 + 2 * QB, 2 * KH], BF16) for u in range(2)]
        keys = [s.sb(f"keys{u}", [128, WIN, WIN]) for u in range(2)]
        values = [s.sb(f"values{u}", [128, WIN, WIN]) for u in range(2)]
        queries = [s.sb(f"queries{u}", [128, NH, QB, QB]) for u in range(2)]
        probs = [[s.sb(f"probs{u}{h}", [KH, NH, QB * QB]) for h in range(2)] for u in range(2)]
        columns = [s.sb(f"columns{u}", [KH, 2, NH, VA]) for u in range(2)]
        inv = [s.sb(f"inv{u}", [QB * QB, NH]) for u in range(2)]
        normed = [s.sb(f"normed{u}", [QB * QB, NH, DH]) for u in range(2)]
        scores = [[s.ps(f"scores{u}{h}") for h in range(2)] for u in range(2)]
        turned_v = s.ps("turned_v")
        mixed = [s.ps(f"mixed{u}") for u in range(2)]
        turned_o = s.ps("turned_o")
        loaded, prepared, staged, queries_ready = map(s.sem, ("loaded", "prepared", "staged", "queries_ready"))
        scored, exped, v_turned, v_ready, mixed_ready, inv_ready, normed_ready, o_turned, o_stored = map(
            s.sem, ("scored", "exped", "v_turned", "v_ready", "mixed_ready", "inv_ready", "normed_ready", "o_turned", "o_stored"))

        def blocks(engine):
            with engine.Fori(0, B) as b, engine.Fori(0, NBLK) as by:
                for pair in range(NBLK // 2):
                    yield (b * NBLK + by) * NBLK + pair * 2, b, by, pair * 2

        with nc.Block() as block:
            @block.sync
            def _(sp):
                sp.dma_start(mask_all[:, :, :], mask_dram).then_inc(loaded, 16)
                sp.dma_start(query_side[:, :, :], query_dram).then_inc(loaded, 16)

            @block.gpsimd
            def _(pool):
                pool.memset(OP[:, :, :], 0.0).then_inc(prepared, 1)
                for u in range(2):
                    pool.memset(columns[u][:, :, :, :], 1.0).then_inc(prepared, 1)
                pool.wait_ge(loaded, 32)
                for n0, b, by, bx0 in blocks(pool):
                    for u in range(2):
                        n, bx = n0 + u, bx0 + u
                        pool.wait_ge(scored, n + 1)
                        row = ds(b * PK + by * QB, WIN)
                        pool.tensor_copy(keys[u][:, :, :], KP[:, row, bx * QB:bx * QB + WIN])
                        pool.tensor_copy(mask[u][:, :], mask_all[:, ds(by * NBLK + bx, 1), :].rearrange("p a k -> p (a k)"))
                        pool.tensor_copy(values[u][:, :, :], VP[:, row, bx * QB:bx * QB + WIN]).then_inc(staged, 1)

            @block.vector
            def _(dve):
                dve.sem_inc(v_ready, 1)
                dve.wait_ge(loaded, 32)
                dve.tensor_scalar(query_side[0:1, :, :], P("scale", rows=1).rearrange("p (h a) -> p h a", a=1)
                                  .broadcast_to([1, NH, QB * QB]), -1.0, None, ALU.mult).then_inc(queries_ready, 1)
                dve.wait_ge(prepared, 3)
                for n0, b, by, bx0 in blocks(dve):
                    for u in range(2):
                        n, bx = n0 + u, bx0 + u
                        dve.wait_ge(scored, n + 1)
                        patch = Q[:, ds(b * H + by * QB, QB), bx * QB:(bx + 1) * QB]
                        dve.tensor_tensor(queries[u][:, :, :, :],
                                          patch.rearrange("p (a y) x -> p a y x", a=1).broadcast_to([128, NH, QB, QB]),
                                          P("head_of").rearrange("p (h y x) -> p h y x", y=1, x=1).broadcast_to([128, NH, QB, QB]),
                                          ALU.mult).then_inc(queries_ready, 1)
                    for u in range(2):
                        n, bx = n0 + u, bx0 + u
                        dve.wait_ge(v_turned, n + 1)
                        dve.wait_ge(mixed_ready, n + 1)
                        dve.tensor_copy(columns[u][:, :, :, 0:DH].rearrange("k s h d -> k (s h) d"),
                                        turned_v[0:KH, 0:2 * C].rearrange("k (g d) -> k g d", d=DH)).then_inc(v_ready, 1)
                    for u in range(2):
                        n, bx = n0 + u, bx0 + u
                        dve.wait_ge(mixed_ready, n + 1 + FREE)
                        mix = mixed[u][0:QB * QB, 0:NH * VA].rearrange("q (h d) -> q h d", d=VA)
                        dve.wait_ge(o_turned, n + 1)
                        dve.reciprocal(inv[u][:, :], mix[:, :, DH]).then_inc(inv_ready, 1)
                        dve.wait_ge(inv_ready, n + 1)
                        dve.tensor_tensor(normed[u][:, :, :], mix[:, :, 0:DH], along(inv[u][:, :], DH), ALU.mult).then_inc(normed_ready, 1)

            @block.scalar
            def _(act):
                act.preload_act_table(ACT.Exp)
                act.sem_inc(exped, FREE * 2)
                act.sem_inc(o_stored, 1)
                act.wait_ge(prepared, 3)
                for n0, b, by, bx0 in blocks(act):
                    for u in range(2):
                        n = n0 + u
                        act.wait_ge(mixed_ready, n + 1)
                        act.wait_ge(scored, n + 1 + FREE)
                        for h in range(2):
                            act.activation(probs[u][h][:, :, :].rearrange("k h q -> k (h q)"), scores[u][h][0:KH, :], ACT.Exp).then_inc(exped, 1)
                    for u in range(2):
                        n, bx = n0 + u, bx0 + u
                        act.wait_ge(o_turned, n + 1 + FREE)
                        act.activation(OP[:, ds(b * PW + by * QB + 1, QB), 1 + bx * QB:1 + (bx + 1) * QB],
                                       turned_o[:, 0:QB * QB].rearrange("c (y x) -> c y x", x=QB), ACT.Copy).then_inc(o_stored, 1)

            @block.tensor
            def _(pe):
                pe.sem_inc(scored, FREE)
                pe.sem_inc(mixed_ready, FREE)
                pe.sem_inc(o_turned, FREE)
                pe.wait_ge(loaded, 32)
                for n0, b, by, bx0 in blocks(pe):
                    for u in range(2):
                        n = n0 + u
                        pe.wait_ge(staged, n + 1)
                        pe.wait_ge(v_ready, n + 1)
                        for h in range(2):
                            last = pe.transpose(turned_v[0:KH, h * C:(h + 1) * C],
                                                values[u][:, h * (WIN // 2):(h + 1) * (WIN // 2), :].rearrange("c y x -> c (y x)"), P("identity"))
                        last.then_inc(v_turned, 1)
                        pe.wait_ge(queries_ready, n + 2)
                        pe.wait_ge(exped, n * 2 + 2)
                        for h in range(2):
                            pe.matmul(scores[u][h][0:KH, :], keys[u][:, h * (WIN // 2):(h + 1) * (WIN // 2), :].rearrange("c y x -> c (y x)"),
                                      queries[u][:, :, :, :].rearrange("c h y x -> c (h y x)"), start=True, stop=False)
                            last = pe.matmul(scores[u][h][0:KH, :], mask[u][:, h * KH:(h + 1) * KH],
                                             query_side[:, :, :].rearrange("f h q -> f (h q)"), start=False, stop=True)
                        last.then_inc(scored, 1)
                    for u in range(2):
                        n = n0 + u
                        pe.wait_ge(exped, n * 2 + 2 + FREE * 2)
                        pe.wait_ge(v_ready, n + 1 + 1)
                        for hd in range(NH):
                            for h in range(2):
                                last = pe.matmul(mixed[u][0:QB * QB, hd * VA:(hd + 1) * VA], probs[u][h][:, hd, :],
                                                 columns[u][:, h, hd, :], start=h == 0, stop=h == 1)
                        last.then_inc(mixed_ready, 1)
                    for u in range(2):
                        n = n0 + u
                        pe.wait_ge(normed_ready, n + 1)
                        pe.wait_ge(o_stored, n + 1)
                        pe.matmul(turned_o[:, 0:QB * QB], normed[u][:, :, :].rearrange("q h d -> q (h d)"),
                                  P("identity", rows=QB * QB, width=QB * QB), start=True, stop=True).then_inc(o_turned, 1)


def out_conv(nc, P, OP, wout, XN, X):
    with Stage(nc, "oc") as s:
        conv = [s.ps(f"conv{u}") for u in range(2)]
        conv_ready, conv_used, summed = map(s.sem, ("conv_ready", "conv_used", "summed"))
        with nc.Block() as block:
            @block.gpsimd
            def _(pool):
                pool.tensor_tensor(X[:, :, :], X[:, :, :], XN[:, :, :], ALU.add).then_inc(summed, 1)

            @block.tensor
            def _(pe):
                with pe.Fori(0, B) as b, pe.Fori(0, TB // 2) as i:
                    for u in range(2):
                        t = b * TB + i * 2 + u
                        pe.wait_ge(conv_used, t + 1)
                        for tap in range(9):
                            last = pe.matmul(rows48(conv[u][:, 0:T]), wout[:, tap, :],
                                             OP[:, ds(b * PW + (i * 2 + u) * TR + tap // 3, TR), tap % 3:tap % 3 + W],
                                             start=tap == 0, stop=tap == 8)
                        last.then_inc(conv_ready, 1)

            @block.vector
            def _(dve):
                dve.sem_inc(conv_used, FREE)
                dve.wait_ge(summed, 1)
                with dve.Fori(0, NT // 2) as i:
                    for u in range(2):
                        t = i * 2 + u
                        dve.wait_ge(conv_ready, t + 1)
                        dve.scalar_tensor_tensor(tile(X, t), rows48(conv[u][:, 0:T]), P("out_b"), tile(X, t), ALU.add, ALU.add).then_inc(conv_used, 1)


def prefix(link, dve, a, b, out, length, at):
    source, target, step = a, b, 1
    while step < length:
        to = out if step * 2 >= length else target
        dve.tensor_copy(at(to, 0, step), at(source, 0, step))
        link(dve.tensor_tensor(at(to, step, length), at(source, step, length), at(source, 0, length - step), ALU.add))
        source, target, step = to, source, step * 2


def dispatch(nc, P, name, XF, gate, bias, top, renormalise, slots, pads_written, expert_codes):
    groups = expert_codes.shape[1]
    tiles = groups * GROUP
    with Stage(nc, name) as s:
        logits, shifted, expo, probs, left, near, counted, other, before, place = (
            s.sb(n, [128, NC, E]) for n in ("logits", "shifted", "expo", "probs", "left", "near", "counted", "other", "before", "place"))
        pick = [s.sb(f"pick{k}", [128, NC, E]) for k in range(top)]
        order = s.sb("order", [128, E])
        peak, total, inv, best = (s.sb(n, [128, NC]) for n in ("peak", "total", "inv", "best"))
        weight = [s.sb(f"weight{k}", [128, NC]) for k in range(top)]
        tiles_of, ends, ends_a, ends_b, starts = (s.sb(n, [128, E]) for n in ("tiles_of", "ends", "ends_a", "ends_b", "starts"))
        past = s.sb("past", [128, tiles, E])
        passed = s.sb("passed", [128, tiles])
        code = s.sb("code", [128, groups])
        slot = s.sb("slot", [128, NC])
        slot_of = [s.sb(f"slot_of{k}", [128, NC], I32) for k in range(top)]
        rows = [s.sb(f"rows{k}", [128, NC, ROW]) for k in range(top)]
        logits_ps, within, totals = s.ps("logits_ps"), s.ps("within"), s.ps("totals")
        turned = [s.ps(f"turned{u}") for u in range(2)]
        gated, step, exp_in, exp_out, picked, ranked, rows_turned, rows_copied, meta_ready, scattered = map(
            s.sem, ("gated", "step", "exp_in", "exp_out", "picked", "ranked", "rows_turned", "rows_copied", "meta_ready", "scattered"))

        def per_token(ap):
            return along(ap[:, :], E)

        def flat(ap):
            return ap[:, :, :].rearrange("p n e -> p (n e)")

        def every_token(ap):
            return ap.rearrange("p (a e) -> p a e", a=1).broadcast_to([128, NC, E])

        with nc.Block() as block:
            @block.tensor
            def _(pe):
                for n in range(NC):
                    last = pe.matmul(logits_ps[:, n * E:(n + 1) * E], chunk(XF, n), gate, start=True, stop=True)
                last.then_inc(gated, 1)
                for t in range(NT):
                    if t >= 2:
                        pe.wait_ge(rows_copied, t - 1)
                    for j in range(CH):
                        last = pe.transpose(turned[t % 2][:, j * 128:(j + 1) * 128], chunk(XF, t * CH + j), P("identity"))
                    last.then_inc(rows_turned, 1)
                pe.wait_ge(picked, 1)
                pe.matmul(within[:, 0:NC * E], P("earlier"), flat(counted), start=True, stop=True)
                pe.matmul(totals[:, 0:NC * E], P("ones"), flat(counted), start=True, stop=True).then_inc(ranked, 1)

            @block.scalar
            def _(act):
                act.preload_act_table(ACT.Exp)
                act.wait_ge(exp_in, 1)
                act.activation(expo[:, :, :], shifted[:, :, :], ACT.Exp).then_inc(exp_out, 1)
                for t in range(NT):
                    act.wait_ge(rows_turned, t + 1)
                    for k in range(top):
                        last = act.activation(rows[k][:, t * CH:(t + 1) * CH, 0:C], turned[t % 2][:, 0:T].rearrange("p (n c) -> p n c", c=C), ACT.Copy)
                    last.then_inc(rows_copied, 1)

            @block.gpsimd
            def _(pool):
                pool.wait_ge(pads_written, 16)
                pool.wait_ge(rows_copied, NT)
                pool.wait_ge(meta_ready, 1)
                for k in range(top):
                    for n in range(NC):
                        pool.indirect_dma_start(slots, bass.IndirectOffsetOnAxis(ap=slot_of[k][:, n:n + 1], axis=0),
                                                rows[k][:, n, :], None).then_inc(scattered, 16)
                pool.wait_ge(scattered, 16 * top * NC)

            @block.vector
            def _(dve):
                link = Chain(dve, step)
                for k in range(top):
                    dve.memset(rows[k][:, :, C + 2:ROW], 0.0)
                for e in range(E):
                    last = dve.memset(order[:, e:e + 1], float(E - e))
                link(last)
                dve.wait_ge(gated, 1)
                psum = logits_ps[:, 0:NC * E].rearrange("p (n e) -> p n e", e=E)
                if bias is None:
                    link(dve.tensor_copy(logits[:, :, :], psum))
                else:
                    link(dve.tensor_tensor(logits[:, :, :], psum, every_token(bias), ALU.add))
                link(dve.tensor_reduce(peak[:, :], logits[:, :, :], AX.X, ALU.max))
                dve.tensor_tensor(shifted[:, :, :], logits[:, :, :], per_token(peak), ALU.subtract).then_inc(exp_in, 1)
                dve.wait_ge(exp_out, 1)
                link(dve.tensor_reduce(total[:, :], expo[:, :, :], AX.X, ALU.add))
                link(dve.reciprocal(inv[:, :], total[:, :]))
                link(dve.tensor_tensor(probs[:, :, :], expo[:, :, :], per_token(inv), ALU.mult))
                source = probs
                for k in range(top):
                    link(dve.tensor_reduce(weight[k][:, :], source[:, :, :], AX.X, ALU.max))
                    link(dve.tensor_tensor(near[:, :, :], source[:, :, :], per_token(weight[k]), ALU.is_equal))
                    link(dve.tensor_tensor(near[:, :, :], near[:, :, :], every_token(order[:, :]), ALU.mult))
                    link(dve.tensor_reduce(best[:, :], near[:, :, :], AX.X, ALU.max))
                    link(dve.tensor_tensor(pick[k][:, :, :], near[:, :, :], per_token(best), ALU.is_equal))
                    if k + 1 < top:
                        link(dve.scalar_tensor_tensor(left[:, :, :], pick[k][:, :, :], -2.0, source[:, :, :], ALU.mult, ALU.add))
                        source = left
                if top == 1:
                    dve.tensor_copy(counted[:, :, :], pick[0][:, :, :]).then_inc(picked, 1)
                    link(dve.memset(weight[0][:, :], 1.0))
                else:
                    dve.tensor_tensor(counted[:, :, :], pick[0][:, :, :], pick[1][:, :, :], ALU.add).then_inc(picked, 1)
                if renormalise:
                    link(dve.tensor_tensor(total[:, :], weight[0][:, :], weight[1][:, :], ALU.add))
                    link(dve.reciprocal(inv[:, :], total[:, :]))
                    for k in range(top):
                        link(dve.tensor_tensor(weight[k][:, :], weight[k][:, :], inv[:, :], ALU.mult))
                dve.wait_ge(ranked, 1)
                all_of = totals[:, 0:NC * E].rearrange("p (n e) -> p n e", e=E)
                link(dve.tensor_copy(other[:, :, :], all_of))
                prefix(link, dve, other, near, before, NC, lambda ap, i, j: ap[:, i:j, :])
                link(dve.tensor_scalar(tiles_of[:, :], before[:, NC - 1, :], 127.0, 1.0 / 128, ALU.add, ALU.mult))
                link(dve.tensor_scalar(tiles_of[:, :], tiles_of[:, :], 63.75 / 128, ROUND, ALU.subtract, ALU.add))
                link(dve.tensor_scalar(tiles_of[:, :], tiles_of[:, :], ROUND, None, ALU.subtract))
                link(dve.tensor_copy(ends_a[:, :], tiles_of[:, :]))
                prefix(link, dve, ends_a, ends_b, ends, E, lambda ap, i, j: ap[:, i:j])
                link(dve.tensor_tensor(starts[:, :], ends[:, :], tiles_of[:, :], ALU.subtract))
                link(dve.tensor_scalar(starts[:, :], starts[:, :], 128.0, None, ALU.mult))
                link(dve.tensor_tensor(place[:, :, :], before[:, :, :], all_of, ALU.subtract))
                link(dve.tensor_tensor(place[:, :, :], place[:, :, :], within[:, 0:NC * E].rearrange("p (n e) -> p n e", e=E), ALU.add))
                link(dve.tensor_tensor(place[:, :, :], place[:, :, :], every_token(starts[:, :]), ALU.add))
                for k in range(top):
                    link(dve.tensor_tensor(near[:, :, :], place[:, :, :], pick[k][:, :, :], ALU.mult))
                    link(dve.tensor_reduce(slot[:, :], near[:, :, :], AX.X, ALU.add))
                    link(dve.tensor_copy(slot_of[k][:, :], slot[:, :]))
                    dve.tensor_scalar(rows[k][:, :, C], P("token"), float(k * NTOK), None, ALU.add)
                    link(dve.tensor_copy(rows[k][:, :, C + 1], weight[k][:, :]))
                dve.sem_inc(meta_ready, 1)
                link(dve.tensor_tensor(past[:, :, :], ends[:, :].rearrange("p (a e) -> p a e", a=1).broadcast_to([128, tiles, E]),
                                       along(P("tile_number", width=tiles), E), ALU.is_le))
                link(dve.tensor_reduce(passed[:, :], past[:, :, :], AX.X, ALU.add))
                link(dve.tensor_scalar(passed[:, :], passed[:, :], float(E - 1), None, ALU.min))
                of_group = passed[:, :].rearrange("p (g a) -> p g a", a=GROUP)
                link(dve.tensor_copy(code[:, :], of_group[:, :, GROUP - 1]))
                for a in range(GROUP - 2, -1, -1):
                    link(dve.scalar_tensor_tensor(code[:, :], code[:, :], float(E), of_group[:, :, a], ALU.mult, ALU.add))
                link(dve.tensor_copy(passed[:, 0:groups], code[:, :]))
                link(dve.scalar_tensor_tensor(code[:, 0:groups - 1], passed[:, 1:groups], float(E ** GROUP), passed[:, 0:groups - 1], ALU.mult, ALU.add))
                dve.tensor_copy(expert_codes[0:1, :], code[0:1, :])


def experts(nc, P, name, slots, expert_codes, w_in, act_func, biases, w_out, targets, weights_loaded, gated_unit=False):
    G = GROUP
    PAIR = 2 * G
    groups = expert_codes.shape[1]
    tiles = groups * G
    HID = 256 if gated_unit else 512
    HC = HID // 128
    with Stage(nc, name) as s:
        rows = [s.sb(f"rows{u}", [128, G, ROW]) for u in range(2)]
        gates = [s.sb(f"gates{u}", [128, G]) for u in range(2)]
        to = [s.sb(f"to{u}", [128, G], I32) for u in range(2)]
        xg = [s.sb(f"xg{u}", [128, G * 128]) for u in range(2)]
        h = [s.sb(f"h{a}", [128, HID]) for a in range(G)]
        raised = [s.sb(f"raised{a}", [128, HID]) for a in range(G)] if gated_unit else h
        ht = [s.sb(f"ht{u}", [128, HID]) for u in range(2)]
        y = [[s.sb(f"y{u}{a}", [128, C]) for a in range(G)] for u in range(2)]
        x_turned = s.ps("x_turned")
        pre = [s.ps(f"pre{u}") for u in range(2)]
        h_turned = [s.ps(f"h_turned{u}") for u in range(2)]
        out = [s.ps(f"out{u}") for u in range(2)]
        rows_turned, meta_ready, xg_ready, pre_ready, biased, hidden, turned, ht_ready, out_ready, taken, y_ready, sending, sent = map(
            s.sem, ("rows_turned", "meta_ready", "xg_ready", "pre_ready", "biased", "hidden", "turned", "ht_ready",
                    "out_ready", "taken", "y_ready", "sending", "sent"))
        rows_loaded = [s.sem(f"rows_loaded{u}") for u in range(2)]
        scattered = [[s.sem(f"scattered{u}{a}") for a in range(G)] for u in range(2)]
        if gated_unit:
            raised_ready = s.sem("raised_ready")

        def steps(engine, body):
            loops = (tiles - G - 1) // PAIR
            for r in range(-2, 1):
                body(0, r)
            with engine.Fori(0, loops) as j:
                for r in range(1, 1 + PAIR):
                    body(j, r)
            for r in range(1 + loops * PAIR, tiles + 1):
                body(0, r)

        def exists(j, m):
            return not isinstance(j, int) or 0 <= m < tiles

        class Experts:

            def __init__(self, engine):
                self.engine, self.group = engine, 0

            def __call__(self, j, r):
                if r % G == 1 or r == -2:
                    self.group = max(r // G, 0)
                    self.code = self.engine.value_load(expert_codes[0:1, ds(j * 2 + self.group, 1)], min_val=0, max_val=E ** (2 * G) - 1)
                return [(self.code >> (3 * max(m - self.group * G, 0))) & (E - 1) for m in (r + 2, r - 1)]

        with nc.Block() as block:
            @block.sync
            def _(sp):
                def load(i, j, u):
                    sp.wait_ge(rows_turned, i + 1)
                    sp.wait_ge(meta_ready, i + 1)
                    sp.dma_start(rows[u][:, :, :], slots[ds(i * (G * 128), G * 128), :].rearrange("(a p) c -> p a c", p=128)).then_inc(rows_loaded[u], 16)

                with sp.Fori(0, groups // 2) as j:
                    for u in range(2):
                        load(j * 2 + u, j, u)
                if groups % 2:
                    load(groups - 1, groups // 2, 0)

            @block.tensor
            def _(pe):
                experts_of = Experts(pe)

                def turn_rows(j, g):
                    pe.wait_ge(rows_loaded[g % 2], (j + g // 2) * 16 + 16)
                    if g > 0:
                        pe.wait_ge(xg_ready, j * 2 + g)
                    for a in range(G):
                        last = pe.transpose(x_turned[:, a * 128:(a + 1) * 128], rows[g % 2][:, a, 0:C], P("identity"))
                    last.then_inc(rows_turned, 1)

                def step(j, r):
                    n = j * PAIR + r
                    into, out_of = experts_of(j, r)
                    if exists(j, r):
                        pe.wait_ge(raised_ready if gated_unit else hidden, n + 1 + G)
                        pe.wait_ge(ht_ready, n + 1)
                        for c in range(HC):
                            last = pe.transpose(h_turned[r % 2][:, c * 128:(c + 1) * 128], raised[r % G][:, c * 128:(c + 1) * 128], P("identity"))
                        last.then_inc(turned, 1)
                    if r % G == 0 and exists(j, r + G):
                        turn_rows(j, r // G + 1)
                    if exists(j, r + 2):
                        m = r + 2
                        pe.wait_ge(xg_ready, j * 2 + m // G + 1)
                        pe.wait_ge(raised_ready if gated_unit else biased, n + 2 + 1 + G - 2)
                        pe.matmul(pre[m % 2][:, :], xg[m // G % 2][:, m % G * 128:(m % G + 1) * 128], w_in[:, ds(into * 512, 512)],
                                  start=True, stop=True).then_inc(pre_ready, 1)
                    if exists(j, r - 1):
                        m = r - 1
                        pe.wait_ge(ht_ready, n - 1 + 1 + 2)
                        pe.wait_ge(taken, n - 1 + 1)
                        for c in range(HC):
                            last = pe.matmul(out[m % 2][:, 0:C], ht[m % 2][:, c * 128:(c + 1) * 128],
                                             w_out[:, ds(out_of * (HC * C) + c * C, C)], start=c == 0, stop=c == HC - 1)
                        last.then_inc(out_ready, 1)

                pe.wait_ge(*weights_loaded)
                pe.sem_inc(rows_turned, FREE)
                pe.sem_inc(turned, G)
                pe.sem_inc(out_ready, FREE)
                turn_rows(0, 0)
                steps(pe, step)

            @block.scalar
            def _(act):
                def copy_rows(j, g):
                    act.wait_ge(rows_turned, j * 2 + g + 1 + FREE)
                    act.activation(xg[g % 2][:, :], x_turned[:, 0:G * 128], ACT.Copy).then_inc(xg_ready, 1)

                def step(j, r):
                    n = j * PAIR + r
                    if exists(j, r):
                        act.wait_ge(turned, n + 1 + G)
                        act.wait_ge(out_ready, n + 1)
                        act.activation(ht[r % 2][:, :], h_turned[r % 2][:, 0:HID], ACT.Copy).then_inc(ht_ready, 1)
                    if r % G == 0 and exists(j, r + G):
                        copy_rows(j, r // G + 1)
                    if exists(j, r + 2):
                        m = r + 2
                        if gated_unit:
                            act.wait_ge(pre_ready, n + 2 + 1)
                            act.wait_ge(raised_ready, n + 2 + 1)
                            act.activation(h[m % G][:, :], pre[m % 2][:, 0:HID], act_func).then_inc(hidden, 1)
                        else:
                            act.wait_ge(biased, n + 2 + 1 + G)
                            act.activation(h[m % G][:, :], h[m % G][:, :], act_func).then_inc(hidden, 1)

                act.preload_act_table(act_func)
                act.sem_inc(hidden, G)
                act.sem_inc(ht_ready, FREE)
                copy_rows(0, 0)
                steps(act, step)

            @block.vector
            def _(dve):
                experts_of = Experts(dve)

                def step(j, r):
                    n = j * PAIR + r
                    if not gated_unit:
                        into, out_of = experts_of(j, r)
                    if exists(j, r + 2):
                        m = r + 2
                        dve.wait_ge(pre_ready, n + 2 + 1)
                        dve.wait_ge(turned, n + 2 + 1)
                        if gated_unit:
                            dve.wait_ge(hidden, n + 2 + 1 + G)
                            dve.tensor_tensor(raised[m % G][:, :], h[m % G][:, :], pre[m % 2][:, HID:2 * HID], ALU.mult).then_inc(raised_ready, 1)
                        else:
                            dve.tensor_tensor(h[m % G][:, :], pre[m % 2][:, :], biases[:, ds(into * 512, 512)], ALU.add).then_inc(biased, 1)
                    if exists(j, r - 1):
                        m = r - 1
                        a, g = m % G, m // G
                        u = g % 2
                        if a == 0:
                            dve.wait_ge(rows_loaded[u], (j + g // 2) * 16 + 16)
                            dve.wait_ge(sent, j * 2 + g + 1)
                            dve.tensor_copy(to[u][:, :], rows[u][:, :, C])
                            dve.tensor_copy(gates[u][:, :], rows[u][:, :, C + 1]).then_inc(meta_ready, 1)
                            dve.wait_ge(meta_ready, j * 2 + g + 1 + FREE)
                        dve.wait_ge(out_ready, n - 1 + 1 + FREE)
                        if gated_unit:
                            dve.tensor_scalar(y[u][a][:, :], out[m % 2][:, 0:C], gates[u][:, a:a + 1], None, ALU.mult).then_inc(taken, 1)
                        else:
                            dve.tensor_tensor(y[u][a][:, :], out[m % 2][:, 0:C], biases[:, ds(out_of * C + E * 512, C)], ALU.add).then_inc(taken, 1)
                            dve.wait_ge(taken, n - 1 + 1 + FREE)
                            dve.tensor_scalar(y[u][a][:, :], y[u][a][:, :], gates[u][:, a:a + 1], None, ALU.mult).then_inc(y_ready, 1)

                dve.sem_inc(raised_ready if gated_unit else biased, G)
                dve.sem_inc(meta_ready, FREE)
                dve.sem_inc(taken, FREE)
                steps(dve, step)

            @block.gpsimd
            def _(pool):
                def sent_group(j, u):
                    for a in range(G):
                        pool.wait_ge(scattered[u][a], j * 16 + 16)
                    pool.sem_inc(sent, 1)

                def send(i, j, u):
                    for a in range(G):
                        n = i * G + a
                        if gated_unit:
                            pool.wait_ge(taken, n + 1 + FREE)
                        else:
                            pool.wait_ge(y_ready, n + 1)
                        pool.sem_inc(sending, 1)
                        pool.indirect_dma_start(targets, bass.IndirectOffsetOnAxis(ap=to[u][:, a:a + 1], axis=0), y[u][a][:, :], None).then_inc(scattered[u][a], 16)

                pool.sem_inc(sent, FREE)
                send(0, 0, 0)
                with pool.Fori(0, (groups - 1) // 2) as j:
                    for u in range(2):
                        send(j * 2 + u + 1, j + u, (u + 1) % 2)
                        sent_group(j, u)
                for i in range((groups - 1) // 2 * 2 + 1, groups):
                    send(i, i // 2, i % 2)
                    sent_group((i - 1) // 2, (i - 1) % 2)
                sent_group((groups - 1) // 2, (groups - 1) % 2)


def combine(nc, P, name, targets, top, X, extra=None):
    PARTS = 4
    with Stage(nc, name) as s:
        rows = [s.sb(f"rows{k}", [128, NC, C]) for k in range(top)]
        turned = [s.ps(f"turned{u}") for u in range(2)]
        loaded = [s.sem(f"loaded{g}") for g in range(PARTS)]
        summed, extra_added, rows_turned, added = map(s.sem, ("summed", "extra_added", "rows_turned", "added"))
        per = NC // PARTS
        with nc.Block() as block:
            @block.sync
            def _(sp):
                for g in range(PARTS):
                    for k in range(top):
                        first = k * NTOK + g * per * 128
                        sp.dma_start(rows[k][:, g * per:(g + 1) * per, :],
                                     targets[first:first + per * 128, :].rearrange("(n p) c -> p n c", p=128)).then_inc(loaded[g], 16)

            @block.gpsimd
            def _(pool):
                if extra is not None:
                    pool.tensor_tensor(X[:, :, :], X[:, :, :], extra[:, :, :], ALU.add).then_inc(extra_added, 1)

            @block.tensor
            def _(pe):
                for t in range(NT):
                    if t % (NT // PARTS) == 0:
                        if top == 1:
                            pe.wait_ge(loaded[t // (NT // PARTS)], 16)
                        else:
                            pe.wait_ge(summed, t // (NT // PARTS) + 1)
                    if t >= 2:
                        pe.wait_ge(added, t - 1)
                    for j in range(CH):
                        last = pe.transpose(turned[t % 2][:, j * 128:(j + 1) * 128], rows[0][:, t * CH + j, :], P("identity"))
                    last.then_inc(rows_turned, 1)

            @block.vector
            def _(dve):
                for g in range(PARTS if top > 1 else 0):
                    dve.wait_ge(loaded[g], 16 * top)
                    part = slice(g * per, (g + 1) * per)
                    dve.tensor_tensor(rows[0][:, part, :], rows[0][:, part, :], rows[1][:, part, :], ALU.add).then_inc(summed, 1)
                if extra is not None:
                    dve.wait_ge(extra_added, 1)
                for t in range(NT):
                    dve.wait_ge(rows_turned, t + 1)
                    dve.tensor_tensor(X[:, t * TR:(t + 1) * TR, :], X[:, t * TR:(t + 1) * TR, :], rows48(turned[t % 2][:, 0:T]), ALU.add).then_inc(added, 1)


def attention(nc, P, XN, X, spare):
    KEYS = H * W
    KC = KEYS // 128
    THIRD = KC // CH
    GROUPS = KEYS // T
    bank_cols = [512, 512, 512, 512, 256]
    with Stage(nc, "at") as s:
        both = s.sb("both", [32 + DH, NTOK])
        k, q = both[0:DH, :], both[32:32 + DH, :]
        v = s.sb("v", [128, NC, C])
        with ExitStack() as first:
            proj = [first.enter_context(nc.psum_tensor(f"at_proj{u}", [128, 512], F32)) for u in range(2)]
            values = [first.enter_context(nc.psum_tensor(f"at_values{u}", [128, 512], F32)) for u in range(2)]
            projected, proj_used, valued, values_used = map(s.sem, ("projected", "proj_used", "valued", "values_used"))
            with nc.Block() as block:
                @block.tensor
                def _(pe):
                    for t in range(NT):
                        for m, (weights, m0) in enumerate(((P("wq"), 32), (P("wk"), 0))):
                            if t:
                                pe.wait_ge(proj_used, 2 * t - 1 + m)
                            pe.matmul(rows48(proj[m][m0:m0 + DH, 0:T]), weights, XN[:, t * TR:(t + 1) * TR, :], start=True, stop=True).then_inc(projected, 1)
                        if t >= 2:
                            pe.wait_ge(values_used, t - 1)
                        for j in range(CH):
                            last = pe.matmul(values[t % 2][:, j * C:(j + 1) * C], chunk(XN, t * CH + j), P("wv"), start=True, stop=True)
                        last.then_inc(valued, 1)

                @block.scalar
                def _(act):
                    for t in range(NT):
                        for m, (out, bias, m0) in enumerate(((q, "bq", 32), (k, "bk", 0))):
                            act.wait_ge(projected, 2 * t + m + 1)
                            act.activation(out[:, t * T:(t + 1) * T], proj[m][m0:m0 + DH, 0:T], ACT.Identity, bias=P(bias)[m0:m0 + DH, :]).then_inc(proj_used, 1)

                @block.vector
                def _(dve):
                    for t in range(NT):
                        dve.wait_ge(valued, t + 1)
                        dve.tensor_copy(v[:, t * CH:(t + 1) * CH, :].rearrange("p n c -> p (n c)"), values[t % 2][:, 0:T]).then_inc(values_used, 1)

        staged_q = [s.sb(f"staged_q{u}", [DH, T]) for u in range(2)]
        probs = [XN[:, u * H:(u + 1) * H, :].rearrange("p r w -> p (r w)") for u in range(2)]
        turned = [s.sb("turned", [128, KC, T])[:, :, :], spare[:, 0:KC * T].rearrange("p (m q) -> p m q", q=T)]
        peaks = s.sb("peaks", [128, 5])
        minus_peak = [s.sb(f"minus_peak{u}", [128, 1]) for u in range(2)]
        total = [s.sb(f"total{u}", [128, 1]) for u in range(2)]
        inv = [s.sb(f"inv{u}", [128, 1]) for u in range(2)]
        inv_all = [s.sb(f"inv_all{u}", [128, T]) for u in range(2)]
        normed = s.sb("normed", [128, TR, W])
        scores = s.ps("scores", [128, 2560])
        turning = [s.ps(f"turning{u}") for u in range(2)]
        mixed = s.ps("mixed")
        q_staged, scored, reduced, peaked, exped, inv_ready, turned_ready, act_evacuated, dve_evacuated, mixed_ready, added, mixed_used = map(
            s.sem, ("q_staged", "scored", "reduced", "peaked", "exped", "inv_ready", "turned_ready", "act_evacuated", "dve_evacuated",
                    "mixed_ready", "added", "mixed_used"))
        TURNS = KC // CH + 1
        BY_ACT, BY_DVE = TURNS // 2, TURNS - TURNS // 2
        SCORE_CREDIT = FREE * CH * 5

        def groups(engine):
            for b in range(B):
                yield b * GROUPS, 0, b, b - 1 if b else None
                with engine.Fori(0, GROUPS // 2 - 1) as i:
                    yield i * 2 + (b * GROUPS + 1), 1, b, b
                    yield i * 2 + (b * GROUPS + 2), 0, b, b
                yield b * GROUPS + GROUPS - 1, 1, b, b

        with nc.Block() as block:
            @block.gpsimd
            def _(pool):
                for g, par, b, last_b in groups(pool):
                    pool.wait_ge(scored, (g + 1) * (CH * 5))
                    pool.tensor_copy(staged_q[par][:, :], q[:, ds(g * T, T)]).then_inc(q_staged, 1)

            @block.tensor
            def _(pe):
                pe.sem_inc(scored, SCORE_CREDIT)

                def weigh(par, image, third):
                    for m in range(third * THIRD, (third + 1) * THIRD):
                        last = pe.matmul(mixed[:, 0:T], v[:, image * KC + m, :], turned[par][:, m, :], start=m == 0, stop=m == KC - 1)
                    if third == CH - 1:
                        last.then_inc(mixed_ready, 1)

                for g, par, b, last_b in groups(pe):
                    for c in range(CH):
                        n, np = g * CH + c, (par + c) % 2
                        if c == 0:
                            pe.wait_ge(q_staged, g + 1)
                        pe.wait_ge(exped, n + 1)
                        for j, cols in enumerate(bank_cols):
                            pe.matmul(scores[:, j * 512:j * 512 + cols], staged_q[par][:, c * 128:(c + 1) * 128],
                                      k[:, b * KEYS + j * 512:b * KEYS + j * 512 + cols], start=True, stop=True).then_inc(scored, 1)
                        if last_b is not None:
                            if c == 0:
                                pe.wait_ge(act_evacuated, g * (CH * BY_ACT) + BY_ACT)
                                pe.wait_ge(dve_evacuated, g * (CH * BY_DVE) + BY_DVE)
                                pe.wait_ge(mixed_used, g)
                            weigh(1 - par, last_b, c)
                        pe.wait_ge(exped, n + 1 + 1)
                        for j in range(TURNS):
                            bank = turning[(np + j) % 2]
                            if j % 2 == (1 if j > 1 else 0):
                                pe.wait_ge(act_evacuated, n * BY_ACT + (BY_ACT if j == 0 else BY_ACT + j // 2))
                            else:
                                pe.wait_ge(dve_evacuated, n * BY_DVE + (BY_DVE if j == 1 else BY_DVE + j // 2))
                            if j < TURNS - 1:
                                for m in range(CH):
                                    last = pe.transpose(bank[:, m * 128:(m + 1) * 128], probs[np][:, (j * CH + m) * 128:(j * CH + m + 1) * 128], P("identity"))
                            else:
                                pe.wait_ge(inv_ready, n + 1)
                                last = pe.transpose(bank[:, 0:128], inv[np][:, 0:1].broadcast_to([128, 128]), P("identity"))
                            last.then_inc(turned_ready, 1)
                pe.wait_ge(act_evacuated, B * GROUPS * CH * BY_ACT + BY_ACT)
                pe.wait_ge(dve_evacuated, B * GROUPS * CH * BY_DVE + BY_DVE)
                pe.wait_ge(mixed_used, B * GROUPS)
                for third in range(CH):
                    weigh(1, B - 1, third)

            @block.scalar
            def _(act):
                act.preload_act_table(ACT.Exp)
                act.sem_inc(exped, 1)
                act.sem_inc(act_evacuated, BY_ACT)
                for g, par, b, last_b in groups(act):
                    for c in range(CH):
                        n, np = g * CH + c, (par + c) % 2
                        act.wait_ge(peaked, n + 1 + 1)
                        act.activation(probs[np][:, :], scores[:, 0:KEYS], ACT.Exp, bias=minus_peak[np][:, 0:1],
                                       accum_out=total[np][:, 0:1]).then_inc(exped, 1)
                        for j in range(1, TURNS, 2):
                            act.wait_ge(turned_ready, n * TURNS + j + 1)
                            act.activation(turned[par][:, j * CH:(j + 1) * CH, c * 128:(c + 1) * 128],
                                           turning[(np + j) % 2][:, 0:T].rearrange("p (m q) -> p m q", q=128), ACT.Copy).then_inc(act_evacuated, 1)

            @block.vector
            def _(dve):
                dve.sem_inc(dve_evacuated, BY_DVE)
                dve.sem_inc(mixed_used, 1)
                dve.sem_inc(peaked, 1)
                dve.sem_inc(added, 1)

                def finish(g, par):
                    dve.wait_ge(added, g + 1)
                    dve.wait_ge(mixed_ready, g + 1)
                    dve.wait_ge(dve_evacuated, (g + 1) * (CH * BY_DVE) + BY_DVE)
                    dve.tensor_tensor(normed[:, :, :], rows48(mixed[:, 0:T]), rows48(inv_all[par][:, :]), ALU.mult).then_inc(mixed_used, 1)
                    dve.wait_ge(mixed_used, g + 2)
                    dve.scalar_tensor_tensor(tile(X, g), normed[:, :, :], P("bv"), tile(X, g), ALU.add, ALU.add).then_inc(added, 1)

                for g, par, b, last_b in groups(dve):
                    for c in range(CH):
                        n, np = g * CH + c, (par + c) % 2
                        dve.wait_ge(peaked, n + 1)
                        for j, cols in enumerate(bank_cols):
                            dve.wait_ge(scored, n * 5 + j + 1 + SCORE_CREDIT)
                            last = dve.tensor_reduce(peaks[:, j:j + 1], scores[:, j * 512:j * 512 + cols], AX.X, ALU.max)
                        last.then_inc(reduced, 1)
                        dve.wait_ge(reduced, n + 1)
                        dve.tensor_reduce(minus_peak[np][:, 0:1], peaks[:, :], AX.X, ALU.max, negate=True).then_inc(peaked, 1)
                        dve.wait_ge(exped, n + 1 + 1)
                        dve.reciprocal(inv[np][:, :], total[np][:, :]).then_inc(inv_ready, 1)
                        for j in range(0, TURNS, 2):
                            dve.wait_ge(turned_ready, n * TURNS + j + 1)
                            bank = turning[(np + j) % 2]
                            if j < TURNS - 1:
                                dve.tensor_copy(turned[par][:, j * CH:(j + 1) * CH, c * 128:(c + 1) * 128],
                                                bank[:, 0:T].rearrange("p (m q) -> p m q", q=128)).then_inc(dve_evacuated, 1)
                            else:
                                dve.tensor_copy(inv_all[par][:, c * 128:(c + 1) * 128], bank[:, 0:128]).then_inc(dve_evacuated, 1)
                    if last_b is not None:
                        finish(g - 1, 1 - par)
                finish(B * GROUPS - 1, 1)


def dynamic_conv(nc, P, XN, X):
    TAPS = 10
    CM = 32
    with Stage(nc, "dc") as s:
        F = s.sb("f", [128, B * PF, PF])
        filters = s.sb("filters", [128, B, TAPS, C])
        sums, mean, g = (s.sb(n, [128, B]) for n in ("sums", "mean", "g"))
        bias = s.sb("bias", [128, 1])
        kernels = [s.sb(f"kernel{m}", [128, B, TAPS]) for m in range(2)]
        middle = s.sb("middle", [128, TAPS])
        scratch = s.sb("scratch", [128, C])
        g_ps, bias_ps = s.ps("g_ps"), s.ps("bias_ps")
        pre = [s.ps(f"pre{u}") for u in range(2)]
        conv = [s.ps(f"conv{u}") for u in range(2)]
        zeroed, step, mean_ready, g_pre, g_ready, bias_pre, pre_ready, act_taken, dve_taken, filters_ready, f_ready, conv_ready, conv_used = map(
            s.sem, ("zeroed", "step", "mean_ready", "g_pre", "g_ready", "bias_pre", "pre_ready", "act_taken", "dve_taken",
                    "filters_ready", "f_ready", "conv_ready", "conv_used"))

        def copy_of_f(t, j):
            b, i = t // TB, t % TB
            row = b * PF + i * TR + 2
            first = 1 if j == 3 else 0
            return F[j * CM:(j + 1) * CM, row:row + TR, first + 2 - j:2 - j + W], first

        with nc.Block() as block:
            @block.gpsimd
            def _(pool):
                pool.memset(F[:, :, :], 0.0).then_inc(zeroed, 1)

            @block.tensor
            def _(pe):
                for t in range(NT):
                    if t >= 2:
                        pe.wait_ge(act_taken, t - 1)
                        pe.wait_ge(dve_taken, t - 1)
                    pe.matmul(rows48(pre[t % 2][:, 0:T]), P("conv_w"), XN[:, t * TR:(t + 1) * TR, :], start=True, stop=True).then_inc(pre_ready, 1)
                pe.matmul(bias_ps[:, 0:1], P("fuse1", rows=CM), P("adap_b", rows=CM), start=True, stop=False)
                pe.matmul(bias_ps[:, 0:1], P("fuse2", rows=CM), P("atrous_b", rows=CM), start=False, stop=True).then_inc(bias_pre, 1)
                pe.wait_ge(mean_ready, 1)
                pe.matmul(g_ps[:, 0:B], P("conv_w"), mean[:, :], start=True, stop=True).then_inc(g_pre, 1)
                pe.wait_ge(filters_ready, 1)
                pe.wait_ge(act_taken, NT)
                pe.wait_ge(dve_taken, NT)
                for b in range(B):
                    with pe.Fori(0, TB // 2) as i:
                        for u in range(2):
                            t = i * 2 + (b * TB + u)
                            pe.wait_ge(conv_used, t + 1)
                            for tap in range(TAPS):
                                last = pe.matmul(rows48(conv[u][:, 0:T]), filters[:, b, tap, :],
                                                 F[:, ds(i * (2 * TR) + (b * PF + u * TR + tap % 5), TR), 4 * (tap // 5):4 * (tap // 5) + W],
                                                 start=tap == 0, stop=tap == TAPS - 1)
                            last.then_inc(conv_ready, 1)

            @block.scalar
            def _(act):
                act.preload_act_table(ACT.Relu)
                act.wait_ge(zeroed, 1)
                for t in range(NT):
                    act.wait_ge(pre_ready, t + 1)
                    for j in range(2):
                        target, first = copy_of_f(t, j)
                        last = act.activation(target, rows48(pre[t % 2][j * CM:(j + 1) * CM, 0:T])[:, :, first:W], ACT.Relu,
                                              bias=P("conv_b")[j * CM:(j + 1) * CM, :])
                    last.then_inc(act_taken, 1)
                act.wait_ge(g_pre, 1)
                act.activation(g[:, :], g_ps[:, 0:B], ACT.Relu, bias=P("conv_b")).then_inc(g_ready, 1)

            @block.vector
            def _(dve):
                link = Chain(dve, step)
                for b in range(B):
                    last = dve.tensor_reduce(sums[:, b:b + 1], XN[:, b * H:(b + 1) * H, :].rearrange("p r w -> p (r w)"), AX.X, ALU.add)
                link(last)
                dve.tensor_scalar(mean[:, :], sums[:, :], 1.0 / (H * W), None, ALU.mult).then_inc(mean_ready, 1)
                dve.wait_ge(zeroed, 1)
                for t in range(NT):
                    dve.wait_ge(pre_ready, t + 1)
                    for j in range(2, 4):
                        target, first = copy_of_f(t, j)
                        last = dve.tensor_scalar(target, rows48(pre[t % 2][j * CM:(j + 1) * CM, 0:T])[:, :, first:W],
                                                 P("conv_b")[j * CM:(j + 1) * CM, :], 0.0, ALU.add, ALU.max)
                    last.then_inc(dve_taken, 1)
                dve.wait_ge(bias_pre, 1)
                link(dve.tensor_scalar(bias[:, :], bias_ps[:, 0:1], P("fuse_b"), None, ALU.add))
                dve.wait_ge(g_ready, 1)
                for kernel, w, kb, mix, mix_b, valid in ((kernels[0], "kernel_w", "kernel_b", "k_w", "k_b", "tap5"),
                                                         (kernels[1], "kernel2_w", "kernel2_b", "k2_w", "k2_b", "tap3")):
                    for b in range(B):
                        link(dve.scalar_tensor_tensor(kernel[:, b, :], P(w), g[:, b:b + 1], P(kb), ALU.mult, ALU.add))
                    link(dve.tensor_tensor(middle[:, :], kernel[:, 0, :], kernel[:, 1, :], ALU.add))
                    link(dve.tensor_scalar(middle[:, :], middle[:, :], 1.0 / B, None, ALU.mult))
                    link(dve.tensor_scalar(middle[:, :], middle[:, :], P(mix, first=1, width=1), P(mix_b), ALU.mult, ALU.add))
                    for b in range(B):
                        link(dve.scalar_tensor_tensor(kernel[:, b, :], kernel[:, b, :], P(mix, width=1), middle[:, :], ALU.mult, ALU.add))
                        link(dve.scalar_tensor_tensor(kernel[:, b, :], kernel[:, b, :], 0.0, P(valid), ALU.max, ALU.mult))
                for b in range(B):
                    for tap in range(TAPS):
                        link(dve.tensor_scalar(scratch[:, :], P("fuse2"), kernels[1][:, b, tap:tap + 1], None, ALU.mult))
                        link(dve.scalar_tensor_tensor(filters[:, b, tap, :], P("fuse1"), kernels[0][:, b, tap:tap + 1], scratch[:, :], ALU.mult, ALU.add))
                dve.sem_inc(filters_ready, 1)
                dve.sem_inc(conv_used, FREE)
                with dve.Fori(0, NT // 2) as i:
                    for u in range(2):
                        t = i * 2 + u
                        dve.wait_ge(conv_ready, t + 1)
                        dve.scalar_tensor_tensor(tile(X, t), rows48(conv[u][:, 0:T]), bias[:, 0:1], tile(X, t), ALU.add, ALU.add).then_inc(conv_used, 1)


def quantised(nc, P, U, X):
    with Stage(nc, "qf") as s:
        sums, totals = s.sb("sums", [128, 2]), s.sb("totals", [128, 2])
        shifted, sign, weight = (s.sb(n, [128, C]) for n in ("shifted", "sign", "weight"))
        y = [s.sb(f"y{u}", [128, TR, W]) for u in range(2)]
        level = [s.sb(f"level{u}", [128, TR, W]) for u in range(2)]
        sums_ps = s.ps("sums_ps")
        product = [s.ps(f"product{u}") for u in range(2)]
        step, sums_ready, totals_ready, shifted_ready, sign_ready, weight_ready, product_ready, y_ready, y_used, rounding = map(
            s.sem, ("step", "sums_ready", "totals_ready", "shifted_ready", "sign_ready", "weight_ready", "product_ready", "y_ready", "y_used", "rounding"))
        with nc.Block() as block:
            @block.tensor
            def _(pe):
                pe.wait_ge(sums_ready, 1)
                pe.matmul(sums_ps[:, 0:2], P("ones"), sums[:, :], start=True, stop=True).then_inc(totals_ready, 1)
                pe.wait_ge(weight_ready, 1)
                with pe.Fori(0, NT // 2) as i:
                    for u in range(2):
                        t = i * 2 + u
                        pe.wait_ge(y_ready, t + 1)
                        pe.matmul(rows48(product[u][:, 0:T]), weight[:, :], tile(U, t), start=True, stop=True).then_inc(product_ready, 1)

            @block.scalar
            def _(act):
                act.preload_act_table(ACT.Sign)
                act.sem_inc(y_ready, FREE)
                act.wait_ge(shifted_ready, 1)
                act.activation(sign[:, :], shifted[:, :], ACT.Sign).then_inc(sign_ready, 1)
                with act.Fori(0, NT // 2) as i:
                    for u in range(2):
                        t = i * 2 + u
                        act.wait_ge(product_ready, t + 1)
                        act.wait_ge(y_used, t + 1)
                        act.activation(y[u][:, :, :], rows48(product[u][:, 0:T]), ACT.Identity, bias=P("b2f")).then_inc(y_ready, 1)

            @block.vector
            def _(dve):
                link = Chain(dve, step)
                dve.tensor_reduce(sums[:, 0:1], P("w2f"), AX.X, ALU.add)
                dve.tensor_reduce(sums[:, 1:2], P("w2f"), AX.X, ALU.add, apply_absolute_value=True).then_inc(sums_ready, 1)
                dve.wait_ge(totals_ready, 1)
                link(dve.tensor_scalar(totals[:, :], sums_ps[:, 0:2], 1.0 / (C * C), None, ALU.mult))
                dve.tensor_scalar(shifted[:, :], P("w2f"), totals[:, 0:1], None, ALU.subtract).then_inc(shifted_ready, 1)
                dve.wait_ge(sign_ready, 1)
                link(dve.tensor_tensor(weight[:, :], sign[:, :], P("w2f"), ALU.subtract))
                link(dve.tensor_tensor(weight[:, :], weight[:, :], P("w2f"), ALU.add))
                dve.tensor_scalar(weight[:, :], weight[:, :], totals[:, 1:2], None, ALU.mult).then_inc(weight_ready, 1)
                dve.sem_inc(y_used, FREE)
                dve.sem_inc(rounding, 1)
                with dve.Fori(0, NT // 2) as i:
                    dve.wait_ge(rounding, i * 10 + 1)
                    for u in range(2):
                        dve.wait_ge(y_ready, i * 2 + (u + 1 + FREE))
                        dve.tensor_scalar(level[u][:, :, :], y[u][:, :, :], 1.0, -1.0, ALU.min, ALU.max).then_inc(rounding, 1)
                    for k in range(5):
                        for u in range(2):
                            if k < 4:
                                dve.wait_ge(rounding, i * 10 + (2 * k + u + 1 + 1))
                            else:
                                dve.wait_ge(y_used, i * 2 + (u + 1 + FREE))
                            if k == 0:
                                done = dve.tensor_scalar(level[u][:, :, :], level[u][:, :, :], 7.0, ROUND, ALU.mult, ALU.add)
                            elif k == 1:
                                done = dve.tensor_scalar(level[u][:, :, :], level[u][:, :, :], ROUND, 1.0 / 7.0, ALU.subtract, ALU.mult)
                            elif k == 2:
                                done = dve.tensor_tensor(level[u][:, :, :], level[u][:, :, :], y[u][:, :, :], ALU.subtract)
                            elif k == 3:
                                done = dve.tensor_tensor(level[u][:, :, :], level[u][:, :, :], y[u][:, :, :], ALU.add)
                            else:
                                done = dve.tensor_tensor(tile(X, i * 2 + u), tile(X, i * 2 + u), level[u][:, :, :], ALU.add)
                            done.then_inc(y_used if k == 3 else rounding, 1)


def pruned(nc, P, XN, X):
    with Stage(nc, "pr") as s:
        XP = s.sb("xp", [128, B * PW, PW])
        acc = s.sb("acc", [128, H, W])
        H1 = s.sb("h1", [128, ROWS, W])
        diagonal = s.sb("diagonal", [128, 9, 128])
        weight = s.sb("weight", [128, B, C])
        shifted, inv, root, gain, shift = (s.sb(n, [128, 2]) for n in ("shifted", "inv", "root", "gain", "shift"))
        peak, keep = (s.sb(n, [128, 2, B]) for n in ("peak", "keep"))
        conv = [s.ps(f"conv{u}") for u in range(2)]
        zeroed, step, padded, inv_ready, root_ready, affine, diagonal_ready, conv_ready, conv_used, acc_ready, h1_ready = map(
            s.sem, ("zeroed", "step", "padded", "inv_ready", "root_ready", "affine", "diagonal_ready", "conv_ready", "conv_used", "acc_ready", "h1_ready"))
        weight_ready, mixed_ready, h2_ready = map(s.sem, ("weight_ready", "mixed_ready", "h2_ready"))
        image = lambda tensor, b: tensor[:, b * H:(b + 1) * H, :]
        with nc.Block() as block:
            @block.gpsimd
            def _(pool):
                pool.memset(XP[:, :, :], 0.0).then_inc(zeroed, 1)

            @block.tensor
            def _(pe):
                pe.wait_ge(diagonal_ready, 1)
                pe.wait_ge(padded, 2)
                with pe.Fori(0, TB // 2) as i:
                    for u in range(2):
                        pe.wait_ge(conv_used, i * 2 + (u + 1))
                        for tap in range(9):
                            last = pe.matmul(rows48(conv[u][:, 0:T]), diagonal[:, tap, :],
                                             XP[:, ds(i * (2 * TR) + (PW + u * TR + tap // 3), TR), tap % 3:tap % 3 + W], start=tap == 0, stop=tap == 8)
                        last.then_inc(conv_ready, 1)
                for b in range(B):
                    pe.wait_ge(weight_ready, b + 1)
                    with pe.Fori(0, TB // 2) as i:
                        for u in range(2):
                            pe.wait_ge(conv_used, i * 2 + (TB * (b + 1) + u + 1))
                            pe.matmul(rows48(conv[u][:, 0:T]), weight[:, b, :], tile(H1, i * 2 + (b * TB + u)), start=True, stop=True).then_inc(mixed_ready, 1)

            @block.scalar
            def _(act):
                act.preload_act_table(ACT.Sqrt)
                act.sem_inc(conv_used, FREE)
                act.wait_ge(zeroed, 1)
                for b in range(B):
                    act.activation(XP[:, b * PW + 1:b * PW + 1 + H, 1:1 + W], image(XN, b), ACT.Copy).then_inc(padded, 1)
                act.wait_ge(inv_ready, 1)
                act.activation(root[:, :], inv[:, :], ACT.Sqrt).then_inc(root_ready, 1)
                act.wait_ge(affine, 1)
                with act.Fori(0, TB // 2) as i:
                    for u in range(2):
                        act.wait_ge(conv_ready, i * 2 + (u + 1))
                        act.activation(tile(H1, i * 2 + (TB + u)), rows48(conv[u][:, 0:T]), ACT.Relu, bias=shift[:, 0:1], scale=gain[:, 0:1]).then_inc(conv_used, 1)
                act.wait_ge(acc_ready, 1)
                act.activation(image(H1, 0), acc[:, :, :], ACT.Relu, bias=shift[:, 0:1], scale=gain[:, 0:1]).then_inc(h1_ready, 1)
                with act.Fori(0, NT // 2) as i:
                    for u in range(2):
                        act.wait_ge(mixed_ready, i * 2 + (u + 1))
                        act.activation(tile(H1, i * 2 + u), rows48(conv[u][:, 0:T]), ACT.Relu, bias=shift[:, 1:2], scale=gain[:, 1:2]).then_inc(conv_used, 1)

            @block.vector
            def _(dve):
                link = Chain(dve, step)
                for m in range(2):
                    last = dve.tensor_scalar(shifted[:, m:m + 1], P(f"bn{m + 1}_v"), 1e-5, None, ALU.add)
                link(last)
                dve.reciprocal(inv[:, :], shifted[:, :]).then_inc(inv_ready, 1)
                for tap in range(9):
                    last = dve.tensor_scalar(diagonal[:, tap, :], P("identity"), P("dw_w", first=tap, width=1), None, ALU.mult)
                last.then_inc(diagonal_ready, 1)
                dve.wait_ge(root_ready, 1)
                for m, bias in enumerate(("dw_b", "pw_b")):
                    link(dve.tensor_scalar(gain[:, m:m + 1], root[:, m:m + 1], P(f"bn{m + 1}_g"), None, ALU.mult))
                    link(dve.tensor_scalar(shift[:, m:m + 1], P(bias), P(f"bn{m + 1}_m"), None, ALU.subtract))
                    link(dve.tensor_scalar(shift[:, m:m + 1], shift[:, m:m + 1], gain[:, m:m + 1], P(f"bn{m + 1}_b"), ALU.mult, ALU.add))
                dve.sem_inc(affine, 1)
                dve.wait_ge(padded, 1)
                link(dve.tensor_scalar(acc[:, :, :], XP[:, 0:H, 0:W], P("dw_w", width=1), None, ALU.mult))
                for tap in range(1, 9):
                    done = dve.scalar_tensor_tensor(acc[:, :, :], XP[:, tap // 3:tap // 3 + H, tap % 3:tap % 3 + W], P("dw_w", first=tap, width=1),
                                                    acc[:, :, :], ALU.mult, ALU.add)
                    if tap < 8:
                        link(done)
                done.then_inc(acc_ready, 1)
                for b in range(B):
                    if b == 0:
                        dve.wait_ge(h1_ready, 1)
                    else:
                        dve.wait_ge(conv_used, TB + FREE)
                    link(dve.tensor_reduce(peak[:, 0, b:b + 1], image(H1, b).rearrange("p r w -> p (r w)"), AX.X, ALU.max))
                    link(dve.tensor_scalar(keep[:, 0, b:b + 1], peak[:, 0, b:b + 1], 4.0, None, ALU.is_ge))
                    dve.tensor_scalar(weight[:, b, :], P("pw"), keep[:, 0, b:b + 1], None, ALU.mult).then_inc(weight_ready, 1)
                for b in range(B):
                    dve.wait_ge(conv_used, TB * (b + 2) + FREE)
                    link(dve.tensor_reduce(peak[:, 1, b:b + 1], image(H1, b).rearrange("p r w -> p (r w)"), AX.X, ALU.max))
                    link(dve.tensor_scalar(keep[:, 1, b:b + 1], peak[:, 1, b:b + 1], 0.001, None, ALU.is_ge))
                    dve.scalar_tensor_tensor(image(X, b), image(H1, b), keep[:, 1, b:b + 1], image(X, b), ALU.mult, ALU.add)


def build(nc, x, params, pad_rows, masks, query_side, wqkv_in, wout_in, w1_0, w2_0, bias_0, w1_1, w2_1, bias_1, w13_3, w2_3, out,
          first=0, last=8):
    HID = E * 4 * 128
    HID3 = E * 2 * 128
    slots = nc.dram_tensor("slots", ((TILES[2] + 2 * GROUP) * 128, ROW), F32, kind="Internal").ap()
    targets = nc.dram_tensor("targets", (2 * NTOK + 2 * GROUP * 128, C), F32, kind="Internal").ap()
    with ExitStack() as ctx:
        sb = lambda name, shape, dt=F32: ctx.enter_context(nc.sbuf_tensor(name, shape, dt))
        X = sb("X", [128, ROWS, W])
        U = sb("U", [128, ROWS, W])
        params_sb = sb("params_sb", [128, PARAMS.width])
        pads = sb("pads", [128, 2 * GROUP * ROW])
        store_a = sb("store_a", [128, 2 * HID])
        loaded, conv_loaded, loaded_0, loaded_1, loaded_3 = map(
            nc.alloc_semaphore, ("loaded", "conv_loaded", "loaded_0", "loaded_1", "loaded_3"))
        pads_written = [nc.alloc_semaphore(f"pads_written{m}") for m in range(3)]

        def P(name, rows=128, first=0, width=None):
            at, w = PARAMS[name]
            return params_sb[0:rows, at + first:at + first + (width or w - first)]

        def images(tensor):
            return tensor[:, :, :].rearrange("p (b r) w -> p b (r w)", b=B)

        wqkv = store_a[:, 0:27 * C]
        wout = store_a[:, 27 * C:36 * C]
        with nc.Block() as block:
            @block.sync
            def _(sp):
                sp.dma_start(images(X), x.rearrange("b c h w -> c b (h w)")).then_inc(loaded, 16)
                sp.dma_start(params_sb[:, :], params).then_inc(loaded, 16)
                sp.dma_start(pads[:, :], pad_rows).then_inc(loaded, 16)
                if first == 0:
                    sp.dma_start(wqkv, wqkv_in).then_inc(conv_loaded, 16)
                    sp.dma_start(wout, wout_in).then_inc(conv_loaded, 16)
                sp.wait_ge(loaded, 48)

        def halves(store, width):
            return store[:, 0:width], store[:, width:2 * width]

        def write_pads(m, top):
            pairs = -(-TILES[top] // (2 * GROUP))
            return (slots[0:pairs * 2 * GROUP * 128, :].rearrange("(g p a) c -> p g (a c)", p=128, a=2 * GROUP),
                    pads[:, :].rearrange("p (g c) -> p g c", g=1).broadcast_to([128, pairs, 2 * GROUP * ROW]), pads_written[m])

        if first <= 0 < last:
            with ExitStack() as layer:
                lsb = lambda name, shape: layer.enter_context(nc.sbuf_tensor(name, shape, F32))
                padded = lsb("padded", [128, B * PW, PW])
                Q = lsb("Q", [128, ROWS, W])
                KP = lsb("KP", [128, B * PK, PK])
                VP = lsb("VP", [128, B * PK, PK])
                layer_norm(nc, P, "ln0", X, 1e-6, U)
                group_norm(nc, P, U, padded)
                qkv(nc, P, padded, wqkv.rearrange("p (t c) -> p t c", t=9), conv_loaded, Q, KP, VP)
                neighbourhood(nc, P, Q, KP, VP, masks, query_side, padded)
                out_conv(nc, P, padded, wout.rearrange("p (t c) -> p t c", t=9), U, X)

        store_b = sb("store_b", [128, 2 * HID])
        biases = sb("biases", [128, E * (512 + C)])

        def mixture(name, m, XF, gate, bias, top, renormalise, store, act_func, weights_loaded, extra=None, gated_unit=False):
            with nc.sbuf_tensor(f"{name}_expert_codes", [1, TILES[top] // GROUP], I32) as expert_codes:
                dispatch(nc, P, f"{name}d", XF, gate, bias, top, renormalise, slots, pads_written[m], expert_codes)
                experts(nc, P, f"{name}e", slots, expert_codes, store[0], act_func, biases, store[1], targets, weights_loaded, gated_unit)
            combine(nc, P, f"{name}c", targets, top, X, extra)

        def layer3_weights():
            return [(store_a[:, 0:2 * HID3], w13_3, loaded_3), (store_a[:, 2 * HID3:3 * HID3], w2_3, loaded_3)]

        def layer1_weights():
            return [(store_b[:, 0:HID], w1_1, loaded_1), (store_b[:, HID:2 * HID], w2_1, loaded_1)]

        if first <= 1 < last:
            with nc.sbuf_tensor("V", [128, ROWS, W], F32) as V:
                into, out_of = halves(store_a, HID)
                layer_norm(nc, P, "ln1", X, 1e-5, U, second=(V, 1e-5),
                           loads=[(into, w1_0, loaded_0), (out_of, w2_0, loaded_0), (biases[:, :], bias_0, loaded_0), write_pads(0, 2)] + layer1_weights())
                mixture("m1", 0, V, P("gate_0"), None, 2, False, (into, out_of), ACT.Gelu, (loaded_0, 48), extra=U)
        if first <= 2 < last:
            layer_norm(nc, P, "ln2", X, 1e-6, U)
            attention(nc, P, U, X, store_a)
        if first <= 3 < last:
            layer_norm(nc, P, "ln3", X, 1e-5, U, loads=[(biases[:, :], bias_1, loaded_1), write_pads(1, 1)]
                       + layer3_weights() + (layer1_weights() if first > 1 else []))
            mixture("m3", 1, U, P("gate_1"), P("br"), 1, False, halves(store_b, HID), ACT.Gelu, (loaded_1, 48))
        if first <= 4 < last:
            layer_norm(nc, P, "ln4", X, 1e-6, U)
            dynamic_conv(nc, P, U, X)
        if first <= 5 < last:
            layer_norm(nc, P, "ln5", X, 1e-5, U)
            quantised(nc, P, U, X)
        if first <= 6 < last:
            layer_norm(nc, P, "ln6", X, 1e-6, U)
            pruned(nc, P, U, X)
        if first <= 7 < last:
            layer_norm(nc, P, "ln7", X, 1e-5, U, loads=[write_pads(2, 2)] + (layer3_weights() if first > 3 else []))
            mixture("m7", 2, U, P("gate_3"), None, 2, True, (store_a[:, 0:2 * HID3], store_a[:, 2 * HID3:3 * HID3]), ACT.Silu,
                    (loaded_3, 32), gated_unit=True)
        with Stage(nc, "store") as s:
            stored = s.sem("stored")
            with nc.Block() as block:
                @block.sync
                def _(sp):
                    sp.dma_start(out.rearrange("b c h w -> c b (h w)"), images(X)).then_inc(stored, 16)
                    sp.wait_ge(stored, 16)


def _pack(given):
    import numpy as np
    f = np.float32
    groups = lambda n: np.kron(np.eye(128 // n, dtype=f), np.ones((n, n), f))
    head_of = np.kron(np.eye(NH, dtype=f), np.ones((DH, 1), f))
    tap5, tap3 = np.zeros((4, 32, 10), f), np.zeros((4, 32, 10), f)
    tap5[:, :, 0:5] = 1
    tap5[0, :, 5:10] = 1
    for row in (0, 2, 4):
        tap3[0, :, row] = tap3[2, :, row] = tap3[0, :, 5 + row] = 1

    def column(a):
        return np.asarray(a).reshape(-1, 1)

    def every(a):
        return np.repeat(np.asarray(a).reshape(1, -1), 128, axis=0)

    def below(a, *at):
        out = np.zeros((128, np.asarray(a).reshape(np.shape(a)[0], -1).shape[1]), f)
        for row in at:
            out[row:row + np.shape(a)[0]] = np.asarray(a).reshape(np.shape(a)[0], -1)
        return out

    def taps5(a):
        a = np.asarray(a).reshape(5, 5)
        out = np.zeros((4, 32, 10), f)
        for j in range(4):
            out[j, :, 0:5] = a[:, j]
        out[:, :, 5:10] = a[:, 4]
        return out.reshape(128, 10)

    def taps3(a):
        a = np.asarray(a).reshape(3, 3)
        out = np.zeros((5, 5), f)
        for r in range(3):
            for c in range(3):
                out[2 * r, 2 * c] = a[r, c]
        return taps5(out)

    g = given
    four = (0, 32, 64, 96)
    fuse = np.asarray(g["L2_conv_fuse_w"])[:, :, 0, 0].T
    values = {
        "identity": np.eye(128, dtype=f), "centering": (np.eye(128) - 1 / 128).astype(f), "ones": np.ones((128, 128), f),
        "group_mean": groups(8) / 8, "channel_mean": np.full((128, 1), 1 / 128, f), "head_of": head_of,
        "earlier": np.triu(np.ones((128, 128), f), 1), "token": np.arange(NTOK, dtype=f).reshape(NC, 128).T,
        "tile_number": every(np.arange(TILES[2], dtype=f)),
        "tap5": tap5.reshape(128, 10), "tap3": tap3.reshape(128, 10),
        "gn_w": column(g["L0_conv_gn_w"]), "gn_b": column(g["L0_conv_gn_b"]), "qkv_b": np.asarray(g["L0_conv_qkv_b"]).reshape(3, C).T,
        "scale": every(g["L0_conv_scale"]), "out_b": column(g["L0_conv_out_b"]),
        "ln_g": column(g["L0_ffn_ln_g"]), "ln_b": column(g["L0_ffn_ln_b"]),
        "gate_0": g["L0_ffn_gate_w"],
        "bv": column(g["L1_conv_bv"]), "bq": below(g["L1_conv_bq"], 32), "bk": below(g["L1_conv_bk"], 0),
        "wq": np.asarray(g["L1_conv_Wq"]).T, "wk": np.asarray(g["L1_conv_Wk"]).T, "wv": np.asarray(g["L1_conv_Wv"]).T,
        "gate_1": g["L1_ffn_Wr"], "br": every(g["L1_ffn_br"]),
        "conv_w": np.tile(np.asarray(g["L2_conv_conv_w"])[:, :, 0, 0].T, (1, 4)), "conv_b": below(g["L2_conv_conv_b"], *four),
        "k_w": every(g["L2_conv_conv_k_w"]), "k_b": every(g["L2_conv_conv_k_b"]),
        "k2_w": every(g["L2_conv_conv_k2_w"]), "k2_b": every(g["L2_conv_conv_k2_b"]),
        "kernel_w": taps5(g["L2_conv_conv_kernel_w"]), "kernel_b": taps5(g["L2_conv_conv_kernel_b"]),
        "kernel2_w": taps3(g["L2_conv_conv_kernel2_w"]), "kernel2_b": taps3(g["L2_conv_conv_kernel2_b"]),
        "fuse1": below(fuse[0:32], *four), "fuse2": below(fuse[32:64], *four),
        "adap_b": below(g["L2_conv_adap_bias"], 0), "atrous_b": below(g["L2_conv_atrous_bias"], 0), "fuse_b": column(g["L2_conv_fuse_b"]),
        "w2f": g["L2_ffn_weight"], "b2f": column(g["L2_ffn_bias"]),
        "dw_w": np.asarray(g["L3_conv_dw_w"]).reshape(128, 9), "dw_b": column(g["L3_conv_dw_b"]),
        "pw": np.asarray(g["L3_conv_pw_w"])[:, :, 0, 0].T, "pw_b": column(g["L3_conv_pw_b"]), "gate_3": g["L3_ffn_router_w"],
    }
    for n in (1, 2):
        for part in "gbmv":
            values[f"bn{n}_{part}"] = column(g[f"L3_conv_bn{n}_{part}"])
    packed = np.zeros((128, PARAMS.width), f)
    for name, (at, width) in PARAMS.at.items():
        packed[:, at:at + width] = np.asarray(values[name])
    return packed


def _window_masks():
    import numpy as np
    outside = np.zeros((NBLK, QB, WIN), np.float32)
    for block in range(NBLK):
        for y in range(QB):
            start = min(max(block * QB + y - 3, 0), H - 7) - (block * QB - 3)
            outside[block, y] = MASKED
            outside[block, y, start:start + 7] = 0
    keys = np.zeros((1 + 2 * QB, NBLK, NBLK, WIN, WIN), np.float32)
    keys[0] = 1
    for y in range(QB):
        keys[1 + y] = outside[:, y][:, None, :, None]
        keys[1 + QB + y] = outside[:, y][None, :, None, :]
    queries = np.zeros((1 + 2 * QB, NH, QB, QB), np.float32)
    for y in range(QB):
        queries[1 + y, :, y, :] = 1
        queries[1 + QB + y, :, :, y] = 1
    return (keys.reshape(1 + 2 * QB, NBLK * NBLK, WIN * WIN).astype("bfloat16"), queries.reshape(1 + 2 * QB, NH, QB * QB).astype("bfloat16"))


def _inputs(given):
    import numpy as np
    g = {name: np.asarray(a) for name, a in given.items()}

    def conv(a):
        return a.transpose(1, 2, 3, 0).reshape(C, -1)

    def into(a):
        return a.transpose(1, 0, 2).reshape(C, -1)

    def out_of(a):
        return a.reshape(E, -1, 128, C).transpose(2, 0, 1, 3).reshape(128, -1)

    masks, query_side = _window_masks()
    pad_rows = np.zeros((128, 2 * GROUP, ROW), np.float32)
    pad_rows[:, :, C] = 2 * NTOK + np.arange(2 * GROUP * 128).reshape(2 * GROUP, 128).T
    pad_rows = pad_rows.reshape(128, -1)

    def bias(b1, b2):
        return np.repeat(np.concatenate([b1.reshape(1, -1), b2.reshape(1, -1)], axis=1), 128, axis=0)

    arrays = {
        "x": g["x"], "params": _pack(g), "pad_rows": pad_rows,
        "masks": masks, "query_side": query_side,
        "wqkv": conv(g["L0_conv_qkv_w"]), "wout": conv(g["L0_conv_out_w"]),
        "w1_0": into(g["L0_ffn_w1"]), "w2_0": out_of(g["L0_ffn_w2"]), "bias_0": bias(g["L0_ffn_b1"], g["L0_ffn_b2"]),
        "w1_1": into(g["L1_ffn_W1"]), "w2_1": out_of(g["L1_ffn_W2"]), "bias_1": bias(g["L1_ffn_b1"], g["L1_ffn_b2"]),
        "w13_3": into(np.concatenate([g["L3_ffn_w1"], g["L3_ffn_w3"]], axis=2)), "w2_3": out_of(g["L3_ffn_w2"]),
    }
    return {f"in_{name}": np.ascontiguousarray(a) for name, a in arrays.items()}


def kernel(**given):
    import concourse.bacc as bacc
    from concourse.bass_utils import run_bass_kernel_spmd

    arrays = _inputs(given)
    nc = bacc.Bacc("TRN2", target_bir_lowering=False, num_devices=1)
    tensors = [nc.dram_tensor(name, a.shape, mybir.dt.from_np(a.dtype), kind="ExternalInput").ap() for name, a in arrays.items()]
    out = nc.dram_tensor("out", arrays["in_x"].shape, F32, kind="ExternalOutput").ap()
    build(nc, *tensors, out)
    return run_bass_kernel_spmd(nc, [arrays], core_ids=[0]).results[0]["out"]
```

```python
import concourse.bass as bass
from concourse import mybir
from concourse.alu_op_type import AluOpType as ALU
from contextlib import ExitStack

F32 = mybir.dt.float32
F32R = mybir.dt.float32r
BF16 = mybir.dt.bfloat16
I32 = mybir.dt.int32
ACT = mybir.ActivationFunctionType
AX = mybir.AxisListType
ds = bass.ds

B, C, H, W = 2, 128, 48, 48
ROWS = B * H
TR = 8
T = TR * W
NT = ROWS // TR
TB = H // TR
NTOK = ROWS * W
NC = NTOK // 128
CH = T // 128
PW = W + 2
PF = W + 4
PK = W + 6
NH, DH = 8, 16
E = 8
QB = 8
WIN = QB + 6
KH = WIN * WIN // 2
NBLK = H // QB
VA = DH + 1
MASKED = -30000.0
FREE = 2
ROW = C + 4
GROUP = 4
TILES = {top: -(-((top * NTOK + E * 127) // 128) // GROUP) * GROUP for top in (1, 2)}
ROUND = 12582912.0


class Chain:

    def __init__(self, engine, semaphore):
        self.engine, self.semaphore, self.count = engine, semaphore, 0

    def __call__(self, instruction):
        self.count += 1
        instruction.then_inc(self.semaphore, 1)
        self.engine.wait_ge(self.semaphore, self.count)


class Params:

    def __init__(self, columns):
        self.at, n = {}, 0
        for name, width in columns:
            self.at[name] = (n, width)
            n += width
        self.width = n

    def __getitem__(self, name):
        return self.at[name]


PARAMS = Params([
    ("identity", 128), ("ones", 128), ("group_mean", 128),
    ("earlier", 128), ("token_code", NC), ("tile_number", TILES[2]), ("lane", 128), ("unused_target", TILES[2]),
    ("head_of", NH), ("same_query", QB * QB), ("tap5", 10), ("tap3", 10),
    ("gn_w", 1), ("gn_b", 1), ("qkv_b", 3), ("scale", NH), ("out_b", 1), ("ln_g", 1), ("ln_b", 1),
    ("gate_0", E), ("bv", 1), ("bq", 1), ("bk", 1), ("wq", 128), ("wk", 128), ("wv", C),
    ("gate_1", E), ("br", E),
    ("conv_w", 128), ("conv_b", 1), ("k_w", 2), ("k_b", 1), ("k2_w", 2), ("k2_b", 1),
    ("kernel_w", 10), ("kernel_b", 10), ("kernel2_w", 10), ("kernel2_b", 10),
    ("fuse1", C), ("fuse2", C), ("adap_b", 1), ("atrous_b", 1), ("fuse_b", 1),
    ("w2f", C), ("b2f", 1),
    ("dw_w", 9), ("dw_b", 1), ("bn1_g", 1), ("bn1_b", 1), ("bn1_m", 1), ("bn1_v", 1),
    ("pw", C), ("pw_b", 1), ("bn2_g", 1), ("bn2_b", 1), ("bn2_m", 1), ("bn2_v", 1),
    ("gate_3", E),
])


class Stage:

    def __init__(self, nc, name):
        self.nc, self.name, self.sems, self.ctx = nc, name, [], ExitStack()

    def sb(self, name, shape, dt=F32):
        return self.ctx.enter_context(self.nc.sbuf_tensor(f"{self.name}_{name}", shape, dt))

    def ps(self, name, shape=(128, 512), dt=F32):
        return self.ctx.enter_context(self.nc.psum_tensor(f"{self.name}_{name}", list(shape), dt))

    def sem(self, name):
        s = self.nc.alloc_semaphore(f"{self.name}_{name}")
        self.sems.append(s)
        return s

    def __enter__(self):
        return self

    def __exit__(self, *error):
        if error[0] is None:
            self.nc.clear_and_free_semaphores(self.sems)
            self.nc.all_engine_barrier()
            self.ctx.close()


def rows48(ap):
    return ap.rearrange("p (r w) -> p r w", w=W)


def chunk(tensor, n):
    return tensor[:, :, :].rearrange("p r w -> p (r w)")[:, n * 128:(n + 1) * 128]


def along(ap, n):
    return ap.rearrange("p (a b) -> p a b", b=1).broadcast_to([ap.shape[0], ap.shape[1], n])


def tile(tensor, t):
    return tensor[:, ds(t * TR, TR), :]


def layer_norm(nc, P, name, X, eps, out, second=None, loads=(), gate=None):
    outputs = 2 if second else 1
    HELD = 4 // outputs
    with Stage(nc, name) as s:
        rows = s.sb("rows", [128, NC, C])
        stats = s.sb("stats", [128, NC, 6])
        total, apart, squared, var, shifted, inv_var = (s.sb(n, [128, NC]) for n in ("total", "apart", "squared", "var", "shifted", "inv_var"))
        rstd = [s.sb(f"rstd{m}", [128, NC]) for m in range(outputs)]
        scale = [rstd[0]] + ([s.sb("scale1", [128, NC])] if second else [])
        shift = [s.sb(f"shift{m}", [128, NC]) for m in range(outputs)]
        normed = [[s.sb(f"normed{m}{u}", [128, CH, C]) for u in range(HELD)] for m in range(outputs)]
        turned = [s.ps(f"turned{u}") for u in range(2)]
        back = [[s.ps(f"back{m}{u}") for u in range(HELD)] for m in range(outputs)]
        rows_turned, copied, measured, step, root_in, root_out, scale_ready = map(
            s.sem, ("rows_turned", "copied", "measured", "step", "root_in", "root_out", "scale_ready"))
        normed_by_dve, normed_by_act = s.sem("normed_by_dve"), s.sem("normed_by_act")
        turned_back, stored = ([s.sem(f"{n}{m}") for m in range(outputs)] for n in ("turned_back", "stored"))
        by_dve, by_act = (range(CH), range(CH)) if second else (range(CH - 1), range(CH - 1, CH))

        with nc.Block() as block:
            @block.sync
            def _(sp):
                for target, source, arrived in loads:
                    sp.dma_start(target, source).then_inc(arrived, 16)

            @block.tensor
            def _(pe):
                def judge(t):
                    for n in range(t * CH, (t + 1) * CH):
                        pe.matmul(gate[1][:, n * E:(n + 1) * E], chunk(second[0] if second else out, n), gate[0], start=True, stop=True)

                for t in range(NT):
                    if t >= 2:
                        pe.wait_ge(copied, t - 1)
                    for j in range(CH):
                        last = pe.transpose(turned[t % 2][:, j * 128:(j + 1) * 128], chunk(X, t * CH + j), P("identity"))
                    last.then_inc(rows_turned, 1)
                for t in range(NT):
                    for m in range(outputs):
                        if m == 0:
                            pe.wait_ge(normed_by_dve, t + 1)
                        if m == outputs - 1:
                            pe.wait_ge(normed_by_act, t + 1)
                        if t >= HELD:
                            pe.wait_ge(stored[m], t - HELD + 1)
                        for j in range(CH):
                            last = pe.transpose(back[m][t % HELD][:, j * 128:(j + 1) * 128], normed[m][t % HELD][:, j, :], P("identity"))
                        last.then_inc(turned_back[m], 1)
                    if gate and t >= HELD:
                        judge(t - HELD)
                if gate:
                    pe.wait_ge(stored[outputs - 1], NT)
                    for t in range(NT - HELD, NT):
                        judge(t)

            @block.scalar
            def _(act):
                act.preload_act_table(ACT.Sqrt)
                for t in range(NT):
                    act.wait_ge(rows_turned, t + 1)
                    act.activation(rows[:, t * CH:(t + 1) * CH, :].rearrange("p n c -> p (n c)"), turned[t % 2][:, 0:T], ACT.Copy).then_inc(copied, 1)
                for m in range(outputs):
                    act.wait_ge(root_in, m + 1)
                    act.activation(rstd[m][:, :], inv_var[:, :] if m == 0 else shifted[:, :], ACT.Sqrt).then_inc(root_out, 1)
                act.wait_ge(scale_ready, 1)
                LAG = HELD // 2
                for t in range(NT + LAG):
                    if t < NT:
                        if t >= HELD:
                            act.wait_ge(turned_back[outputs - 1], t - HELD + 1)
                        for j in by_act:
                            n, m = t * CH + j, outputs - 1
                            last = act.activation(normed[m][t % HELD][:, j, :], rows[:, n, :], ACT.Identity, bias=shift[m][:, n:n + 1], scale=scale[m][:, n:n + 1])
                        last.then_inc(normed_by_act, 1)
                    k = t - LAG
                    if k >= 0:
                        act.wait_ge(turned_back[0], k + 1)
                        act.activation(out[:, k * TR:(k + 1) * TR, :], rows48(back[0][k % HELD][:, 0:T]), ACT.Copy).then_inc(stored[0], 1)

            @block.vector
            def _(dve):
                link = Chain(dve, step)
                for t in range(NT):
                    dve.wait_ge(copied, t + 1)
                    for n in range(t * CH, (t + 1) * CH):
                        last = dve.bn_stats(stats[:, n, :], rows[:, n, :])
                last.then_inc(measured, 1)
                dve.wait_ge(measured, 1)
                link(dve.tensor_tensor(total[:, :], stats[:, :, 1], stats[:, :, 4], ALU.add))
                link(dve.tensor_tensor(apart[:, :], stats[:, :, 1], stats[:, :, 4], ALU.subtract))
                link(dve.tensor_tensor(var[:, :], stats[:, :, 2], stats[:, :, 5], ALU.add))
                link(dve.tensor_tensor(squared[:, :], apart[:, :], apart[:, :], ALU.mult))
                link(dve.scalar_tensor_tensor(squared[:, :], squared[:, :], C / 4, var[:, :], ALU.mult, ALU.add))
                link(dve.tensor_scalar(shifted[:, :], squared[:, :], 1 / C, eps, ALU.mult, ALU.add))
                dve.reciprocal(inv_var[:, :], shifted[:, :]).then_inc(root_in, 1)
                dve.wait_ge(root_in, 1)
                if second:
                    link(dve.scalar_tensor_tensor(squared[:, :], squared[:, :], 1 / C, inv_var[:, :], ALU.mult, ALU.mult))
                    link(dve.tensor_scalar(squared[:, :], squared[:, :], second[1], None, ALU.add))
                    dve.reciprocal(shifted[:, :], squared[:, :]).then_inc(root_in, 1)
                dve.wait_ge(root_out, outputs)
                if second:
                    link(dve.tensor_tensor(scale[1][:, :], rstd[0][:, :], rstd[1][:, :], ALU.mult))
                for m in range(outputs):
                    link(dve.scalar_tensor_tensor(shift[m][:, :], total[:, :], -0.5, scale[m][:, :], ALU.mult, ALU.mult))
                dve.sem_inc(scale_ready, 1)
                for t in range(NT):
                    if t >= HELD:
                        dve.wait_ge(turned_back[0], t - HELD + 1)
                    for j in by_dve:
                        n = t * CH + j
                        last = dve.tensor_scalar(normed[0][t % HELD][:, j, :], rows[:, n, :], scale[0][:, n:n + 1], shift[0][:, n:n + 1], ALU.mult, ALU.add)
                    last.then_inc(normed_by_dve, 1)
                    if second:
                        dve.wait_ge(turned_back[1], t + 1)
                        dve.tensor_scalar(second[0][:, t * TR:(t + 1) * TR, :], rows48(back[1][t % HELD][:, 0:T]), P("ln_g"), P("ln_b"),
                                          ALU.mult, ALU.add).then_inc(stored[1], 1)


def clear_padding(engine, image):
    for row, rows in ((0, 1), (PW - 1, 2), (2 * PW - 1, 1)):
        engine.memset(image[:, row:row + rows, :].bitcast(F32), 0.0)
    for b in range(B):
        for column in (0, PW - 1):
            last = engine.memset(image[:, b * PW + 1:(b + 1) * PW - 1, column:column + 1].bitcast(F32), 0.0)
    return last


def group_norm(nc, P, XN, high, low, full, weights, weights_high, weights_low, weights_loaded):
    with Stage(nc, "gn") as s:
        stats = s.sb("stats", [128, B, TB, 6])
        moments = s.sb("moments", [128, B, 2])
        square = s.sb("square", [128, B])
        group = s.sb("group", [128, B, 2])
        var, shifted, inv, rstd, gain, shift, drop = (
            s.sb(n, [128, B]) for n in ("var", "shifted", "inv", "rstd", "gain", "shift", "drop"))
        grouped = s.ps("grouped")
        step, moments_ready, grouped_ready, inv_ready, rstd_ready, affine_ready, weights_split, second_ready = map(
            s.sem, ("step", "moments_ready", "grouped_ready", "inv_ready", "rstd_ready", "affine_ready", "weights_split", "second_ready"))

        def inside(image, b):
            return image[:, b * PW + 1:b * PW + 1 + H, 1:1 + W]

        with nc.Block() as block:
            @block.gpsimd
            def _(pool):
                clear_padding(pool, high)
                clear_padding(pool, low)
                pool.wait_ge(weights_split, 1)
                pool.tensor_tensor(weights_low, weights, weights_high, ALU.subtract)

            @block.vector
            def _(dve):
                link = Chain(dve, step)
                for b in range(B):
                    for t in range(TB):
                        last = dve.bn_stats(stats[:, b, t, :], XN[:, b * H + t * TR:b * H + (t + 1) * TR, :].rearrange("p r w -> p (r w)"))
                link(last)
                for b in range(B):
                    last = dve.bn_aggr(moments[:, b, :], stats[:, b, :, :].rearrange("p t s -> p (t s)"))
                link(last)
                link(dve.tensor_tensor(square[:, :], moments[:, :, 0], moments[:, :, 0], ALU.mult))
                dve.tensor_tensor(moments[:, :, 1], moments[:, :, 1], square[:, :], ALU.add).then_inc(moments_ready, 1)
                dve.wait_ge(grouped_ready, 1)
                link(dve.tensor_copy(group[:, :, :].rearrange("p b s -> p (b s)"), grouped[:, 0:2 * B]))
                link(dve.tensor_tensor(square[:, :], group[:, :, 0], group[:, :, 0], ALU.mult))
                link(dve.tensor_tensor(var[:, :], group[:, :, 1], square[:, :], ALU.subtract))
                link(dve.tensor_scalar(shifted[:, :], var[:, :], 1e-5, None, ALU.add))
                dve.reciprocal(inv[:, :], shifted[:, :]).then_inc(inv_ready, 1)
                dve.wait_ge(rstd_ready, 1)
                link(dve.tensor_scalar(gain[:, :], rstd[:, :], P("gn_w"), None, ALU.mult))
                link(dve.tensor_tensor(drop[:, :], group[:, :, 0], gain[:, :], ALU.mult))
                dve.tensor_scalar(shift[:, :], drop[:, :], -1.0, P("gn_b"), ALU.mult, ALU.add).then_inc(affine_ready, 1)
                dve.wait_ge(affine_ready, 1)
                dve.tensor_scalar(full[:, 0:H, :], XN[:, 0:H, :], gain[:, 0:1], shift[:, 0:1], ALU.mult, ALU.add)
                link(dve.tensor_scalar(inside(high, 0), XN[:, 0:H, :], gain[:, 0:1], shift[:, 0:1], ALU.mult, ALU.add))
                dve.tensor_tensor(inside(low, 0), full[:, 0:H, :], inside(high, 0), ALU.subtract)
                dve.wait_ge(second_ready, 1)
                dve.tensor_tensor(inside(low, 1), full[:, H:2 * H, :], inside(high, 1), ALU.subtract)

            @block.tensor
            def _(pe):
                pe.wait_ge(moments_ready, 1)
                pe.matmul(grouped[:, 0:2 * B], P("group_mean"), moments[:, :, :].rearrange("p b s -> p (b s)"),
                          start=True, stop=True).then_inc(grouped_ready, 1)

            @block.scalar
            def _(act):
                act.wait_ge(weights_loaded, 32)
                act.activation(weights_high, weights, ACT.Copy).then_inc(weights_split, 1)
                act.wait_ge(inv_ready, 1)
                act.activation(rstd[:, :], inv[:, :], ACT.Sqrt).then_inc(rstd_ready, 1)
                act.wait_ge(affine_ready, 1)
                act.activation(full[:, H:2 * H, :], XN[:, H:2 * H, :], ACT.Identity, bias=shift[:, 1:2], scale=gain[:, 1:2])
                act.activation(inside(high, 1), XN[:, H:2 * H, :], ACT.Identity, bias=shift[:, 1:2], scale=gain[:, 1:2]).then_inc(second_ready, 1)


def qkv(nc, P, high, low, weights_high, weights_low, Q, KP, VP):
    UNROLLED = 6
    HELD = 4
    with Stage(nc, "qkv") as s:
        squares = [s.sb(f"squares{m}", [128, TR, W]) for m in range(2)]
        length = s.sb("length", [128, 2, NC, NH])
        inv = s.sb("inv", [128, 2, NC, NH])
        factor = s.sb("factor", [128, 2, NC, NH])
        spread = [[s.sb(f"spread{m}{u}", [128, CH, NH, DH]) for u in range(2)] for m in range(2)]
        conv = [s.ps(f"conv{c}") for c in range(3)]
        heads = [s.ps(f"heads{m}") for m in range(2)]
        bcast = [[conv[m], s.ps(f"bcast{m}")] for m in range(2)]
        conv_ready, conv_used, squared, squares_used, zeroed = map(
            s.sem, ("conv_ready", "conv_used", "squared", "squares_used", "zeroed"))
        step, inv_ready, factor_ready, spread_ready, turned, scaled = map(
            s.sem, ("step", "inv_ready", "factor_ready", "spread_ready", "turned", "scaled"))

        def in_key_image(image, b, i):
            return image[:, ds(b * PK + i * TR + 3, TR), 3:3 + W]

        with nc.Block() as block:
            @block.gpsimd
            def _(pool):
                pool.memset(KP[:, :, :], 0.0).then_inc(zeroed, 1)
                pool.memset(VP[:, :, :], 0.0).then_inc(zeroed, 1)

            @block.tensor
            def _(pe):
                def convolve(b, i):
                    t = b * TB + i
                    for c in range(3):
                        pe.wait_ge(conv_used, t * 3 + c + 1)
                        products = [(tap, w, x) for tap in range(9) for w, x in ((weights_high, high), (weights_high, low), (weights_low, high))]
                        for k, (tap, w, x) in enumerate(products):
                            last = pe.matmul(rows48(conv[c][:, 0:T]), w[:, tap, c * C:(c + 1) * C],
                                             x[:, ds(b * PW + i * TR + tap // 3, TR), tap % 3:tap % 3 + W],
                                             start=k == 0, stop=k == len(products) - 1)
                        last.then_inc(conv_ready, 1)

                def sum_heads(t):
                    pe.wait_ge(squared, t + 1)
                    for m in range(2):
                        for j in range(CH):
                            last = pe.matmul(heads[m][:, ds((t * CH + j) * NH, NH)], chunk(squares[m], j), P("head_of"),
                                             start=True, stop=True)
                    last.then_inc(squares_used, 1)

                pe.sem_inc(squares_used, 1)
                convolve(0, 0)
                for b in range(B):
                    with pe.Fori(1 - b, TB) as i:
                        sum_heads(i + (b * TB - 1))
                        convolve(b, i)
                sum_heads(NT - 1)
                with pe.Fori(0, NT // UNROLLED) as i:
                    for r in range(UNROLLED):
                        t = i * UNROLLED + r
                        for m in range(2):
                            pe.wait_ge(spread_ready, t * 2 + m + 1)
                            pe.wait_ge(scaled, t * 2 + m + 1)
                            for j in range(CH):
                                last = pe.transpose(bcast[m][r % 2][:, j * 128:(j + 1) * 128],
                                                    spread[m][r % 2][:, j, :, :].rearrange("p h d -> p (h d)"), P("identity"))
                            last.then_inc(turned, 1)

            @block.scalar
            def _(act):
                act.preload_act_table(ACT.Sqrt)
                act.sem_inc(conv_used, 3)
                act.wait_ge(zeroed, 2)
                with act.Fori(0, B) as b, act.Fori(0, TB) as i:
                    t = b * TB + i
                    for c, target in enumerate((tile(Q, t), in_key_image(KP, b, i), in_key_image(VP, b, i))):
                        act.wait_ge(conv_ready, t * 3 + c + 1)
                        act.activation(target, rows48(conv[c][:, 0:T]), ACT.Identity, bias=P("qkv_b", first=c, width=1)).then_inc(conv_used, 1)
                act.wait_ge(inv_ready, 1)
                act.activation(factor[:, :, :, :].rearrange("p m n h -> p (m n h)"),
                               inv[:, :, :, :].rearrange("p m n h -> p (m n h)"), ACT.Sqrt).then_inc(factor_ready, 1)
                act.wait_ge(factor_ready, 1)
                act.sem_inc(turned, HELD)
                with act.Fori(0, NT // UNROLLED) as i:
                    for r in range(UNROLLED):
                        t = i * UNROLLED + r
                        for m in range(2):
                            act.wait_ge(turned, t * 2 + m + 1)
                            act.activation(spread[m][r % 2][:, :, :, :].rearrange("p c h d -> p (c h) d"),
                                           along(factor[:, m, ds(t * CH, CH), :].rearrange("p n h -> p (n h)"), DH), ACT.Copy).then_inc(spread_ready, 1)

            @block.vector
            def _(dve):
                link = Chain(dve, step)
                with dve.Fori(0, B) as b, dve.Fori(0, TB) as i:
                    t = b * TB + i
                    dve.wait_ge(conv_used, t * 3 + 2 + 3)
                    dve.wait_ge(squares_used, t + 1)
                    dve.tensor_tensor(squares[0][:, :, :], tile(Q, t), tile(Q, t), ALU.mult)
                    dve.tensor_tensor(squares[1][:, :, :], in_key_image(KP, b, i), in_key_image(KP, b, i), ALU.mult).then_inc(squared, 1)
                dve.wait_ge(squares_used, NT + 1)
                for m in range(2):
                    last = dve.tensor_scalar(length[:, m, :, :].rearrange("p n h -> p (n h)"), heads[m][:, 0:NC * NH], 1e-6, None, ALU.add)
                link(last)
                link(dve.reciprocal(inv[:, :, :, :].rearrange("p m n h -> p (m n h)"), length[:, :, :, :].rearrange("p m n h -> p (m n h)")))
                scale = P("scale").rearrange("p (a h) -> p a h", a=1).broadcast_to([128, 2 * NC, NH])
                flat = inv[:, :, :, :].rearrange("p m n h -> p (m n) h")
                dve.tensor_tensor(flat, flat, scale, ALU.mult).then_inc(inv_ready, 1)
                dve.wait_ge(conv_used, NT * 3 + 3)
                dve.sem_inc(scaled, HELD)
                dve.wait_ge(zeroed, 2)
                with dve.Fori(0, B) as b, dve.Fori(0, TB // UNROLLED) as i:
                    for r in range(UNROLLED):
                        tb = i * UNROLLED + r
                        t = b * TB + tb
                        dve.wait_ge(turned, t * 2 + 1 + HELD)
                        dve.tensor_tensor(tile(Q, t), tile(Q, t), rows48(bcast[0][r % 2][:, 0:T]), ALU.mult).then_inc(scaled, 1)
                        dve.wait_ge(turned, t * 2 + 2 + HELD)
                        dve.tensor_tensor(in_key_image(KP, b, tb), in_key_image(KP, b, tb), rows48(bcast[1][r % 2][:, 0:T]), ALU.mult).then_inc(scaled, 1)


def neighbourhood(nc, P, Q, KP, VP, mask_dram, query_dram, OP):
    BLOCKS = B * NBLK * NBLK
    PAIRS = NH // 2
    NQ = QB * QB
    with Stage(nc, "na") as s:
        mask_all = s.sb("mask_all", [1 + 2 * QB, NBLK * NBLK, 2 * KH], BF16)
        query_side = s.sb("query_side", [1 + 2 * QB, NH, NQ], BF16)
        mask = [s.sb(f"mask{u}", [1 + 2 * QB, 2 * KH], BF16) for u in range(2)]
        keys_high, keys_low = ([s.sb(f"{n}{u}", [128, WIN, WIN], F32R) for u in range(2)] for n in ("keys_high", "keys_low"))
        values = [s.sb(f"values{u}", [128, WIN, WIN]) for u in range(2)]
        queries = [s.sb(f"queries{u}", [128, NH, NQ]) for u in range(2)]
        queries_high, queries_low = ([s.sb(f"{n}{u}", [128, NH, NQ], F32R) for u in range(2)] for n in ("queries_high", "queries_low"))
        probs = [s.sb(f"probs{u}", [KH, 2, NH, NQ]) for u in range(2)]
        columns = [s.sb(f"columns{u}", [KH, 2, NH, VA]) for u in range(2)]
        inv = [s.sb(f"inv{u}", [128, PAIRS]) for u in range(2)]
        normed = [s.sb(f"normed{u}", [128, PAIRS, 2, DH]) for u in range(2)]
        scores = [s.ps(f"scores{u}", (128, 1024)) for u in range(2)]
        turned_v = s.ps("turned_v")
        mixed = [s.ps(f"mixed{u}") for u in range(2)]
        turned_o = s.ps("turned_o")
        loaded, prepared, keys_rounded, staged, queries_masked, queries_rounded, queries_ready = map(
            s.sem, ("loaded", "prepared", "keys_rounded", "staged", "queries_masked", "queries_rounded", "queries_ready"))
        scored, exped, v_turned, v_ready, mixed_ready, inv_ready, normed_ready, o_turned, o_stored = map(
            s.sem, ("scored", "exped", "v_turned", "v_ready", "mixed_ready", "inv_ready", "normed_ready", "o_turned", "o_stored"))

        def block_rows(engine, body, apart):
            for b in range(B):
                first, last = 0, NBLK
                if apart == b * NBLK:
                    body(b, 0)
                    first = 1
                if apart == b * NBLK + NBLK - 1:
                    last = NBLK - 1
                with engine.Fori(first, last) as by:
                    body(b, by)
                if last < NBLK:
                    body(b, last)

        with nc.Block() as block:
            @block.sync
            def _(sp):
                sp.dma_start(mask_all[:, :, :], mask_dram).then_inc(loaded, 16)
                sp.dma_start(query_side[:, :, :], query_dram).then_inc(loaded, 16)

            @block.gpsimd
            def _(pool):
                clear_padding(pool, OP).then_inc(prepared, 1)
                for u in range(2):
                    pool.memset(columns[u][:, :, :, :], 1.0).then_inc(prepared, 1)
                    pool.memset(normed[u][:, :, :, :], 0.0).then_inc(prepared, 1)
                pool.wait_ge(loaded, 32)

                def stage(b, by):
                    for bx in range(NBLK):
                        n, u = (b * NBLK + by) * NBLK + bx, bx % 2
                        pool.wait_ge(scored, n + 1)
                        row = ds(b * PK + by * QB, WIN)
                        window = KP[:, row, bx * QB:bx * QB + WIN]
                        pool.tensor_copy(keys_high[u][:, :, :], window).then_inc(keys_rounded, 1)
                        pool.tensor_copy(values[u][:, :, :], VP[:, row, bx * QB:bx * QB + WIN])
                        pool.wait_ge(keys_rounded, n + 1)
                        pool.tensor_copy(mask[u][:, :], mask_all[:, ds(by * NBLK + bx, 1), :].rearrange("p a k -> p (a k)"))
                        pool.tensor_tensor(keys_low[u][:, :, :], window, keys_high[u][:, :, :], ALU.subtract).then_inc(staged, 1)

                block_rows(pool, stage, None)

            @block.vector
            def _(dve):
                def mask_queries(b, by, bx):
                    n, u = (b * NBLK + by) * NBLK + bx, bx % 2
                    dve.wait_ge(scored, n + 1)
                    patch = Q[:, ds(b * H + by * QB, QB), bx * QB:(bx + 1) * QB]
                    dve.tensor_tensor(queries[u][:, :, :].rearrange("p h (y x) -> p h y x", x=QB),
                                      patch.rearrange("p (a y) x -> p a y x", a=1).broadcast_to([128, NH, QB, QB]),
                                      P("head_of").rearrange("p (h y x) -> p h y x", y=1, x=1).broadcast_to([128, NH, QB, QB]),
                                      ALU.mult).then_inc(queries_masked, 1)

                def split_queries(n, u):
                    dve.wait_ge(queries_rounded, n + 1)
                    dve.tensor_tensor(queries_low[u][:, :, :], queries[u][:, :, :], queries_high[u][:, :, :], ALU.subtract).then_inc(queries_ready, 1)

                def place_values(n, u):
                    dve.wait_ge(v_turned, n + 1)
                    dve.wait_ge(mixed_ready, n + 1)
                    dve.tensor_copy(columns[u][:, :, :, 0:DH].rearrange("k s h d -> k (s h) d"),
                                    turned_v[0:KH, 0:2 * C].rearrange("k (g d) -> k g d", d=DH)).then_inc(v_ready, 1)

                def normalise(n, u):
                    dve.wait_ge(mixed_ready, n + 1 + FREE)
                    dve.wait_ge(o_turned, n + 1)
                    mix = mixed[u][:, 0:NH * VA].rearrange("q (g s f) -> q g s f", s=2, f=VA)
                    for s_ in range(2):
                        part = slice(s_ * NQ, (s_ + 1) * NQ)
                        last = dve.reciprocal(inv[u][part, :], mix[part, :, s_, DH])
                    last.then_inc(inv_ready, 1)
                    dve.wait_ge(inv_ready, n + 1)
                    for s_ in range(2):
                        part = slice(s_ * NQ, (s_ + 1) * NQ)
                        last = dve.tensor_tensor(normed[u][part, :, s_, :], mix[part, :, s_, 0:DH], along(inv[u][part, :], DH), ALU.mult)
                    last.then_inc(normed_ready, 1)

                dve.sem_inc(v_ready, 1)
                dve.wait_ge(loaded, 32)
                dve.tensor_scalar(query_side[0:1, :, :], P("scale", rows=1).rearrange("p (h a) -> p h a", a=1)
                                  .broadcast_to([1, NH, NQ]), -1.0, None, ALU.mult).then_inc(queries_ready, 1)
                dve.wait_ge(prepared, 5)

                def body(b, by):
                    for bx in range(NBLK):
                        n, u = (b * NBLK + by) * NBLK + bx, bx % 2
                        mask_queries(b, by, bx)
                        if not isinstance(n, int) or n >= 1:
                            place_values(n - 1, 1 - u)
                        split_queries(n, u)
                        if not isinstance(n, int) or n >= 2:
                            normalise(n - 2, u)

                block_rows(dve, body, 0)
                place_values(BLOCKS - 1, 1)
                normalise(BLOCKS - 2, 0)
                normalise(BLOCKS - 1, 1)

            @block.scalar
            def _(act):
                def exponentiate(n, u):
                    act.wait_ge(mixed_ready, n + 1)
                    act.wait_ge(scored, n + 1 + FREE)
                    act.activation(probs[u][:, :, :, :].rearrange("k s h q -> k (s h q)"), scores[u][0:KH, :], ACT.Exp).then_inc(exped, 1)

                def round_queries(n, u):
                    act.wait_ge(queries_masked, n + 1)
                    act.activation(queries_high[u][:, :, :], queries[u][:, :, :], ACT.Copy).then_inc(queries_rounded, 1)

                act.preload_act_table(ACT.Exp)
                act.sem_inc(exped, FREE)
                act.sem_inc(o_stored, 1)
                act.wait_ge(prepared, 5)
                for n in range(3):
                    round_queries(n, n % 2)
                exponentiate(0, 0)
                exponentiate(1, 1)

                def body(b, by):
                    for bx in range(NBLK):
                        n, u = (b * NBLK + by) * NBLK + bx, bx % 2
                        if not isinstance(n, int) or n + 3 < BLOCKS:
                            round_queries(n + 3, 1 - u)
                        if not isinstance(n, int) or n + 2 < BLOCKS:
                            exponentiate(n + 2, u)
                        act.wait_ge(o_turned, n + 1 + FREE)
                        act.activation(OP[:, ds(b * PW + by * QB + 1, QB), 1 + bx * QB:1 + (bx + 1) * QB],
                                       turned_o[:, 0:NQ].rearrange("c (y x) -> c y x", x=QB), ACT.Copy).then_inc(o_stored, 1)

                block_rows(act, body, B * NBLK - 1)

            @block.tensor
            def _(pe):
                def score(n, u):
                    pe.wait_ge(staged, n + 1)
                    pe.wait_ge(v_ready, n + 1)
                    for h in range(2):
                        last = pe.transpose(turned_v[0:KH, h * C:(h + 1) * C],
                                            values[u][:, h * (WIN // 2):(h + 1) * (WIN // 2), :].rearrange("c y x -> c (y x)"), P("identity"))
                    last.then_inc(v_turned, 1)
                    pe.wait_ge(queries_ready, n + 2)
                    pe.wait_ge(exped, n + 1)
                    for h in range(2):
                        half = scores[u][0:KH, h * 512:(h + 1) * 512]
                        for k, (key_part, query_part) in enumerate(((keys_high, queries_high), (keys_high, queries_low), (keys_low, queries_high))):
                            pe.matmul(half, key_part[u][:, h * (WIN // 2):(h + 1) * (WIN // 2), :].rearrange("c y x -> c (y x)"),
                                      query_part[u][:, :, :].rearrange("c h q -> c (h q)"), start=k == 0, stop=False)
                        last = pe.matmul(half, mask[u][:, h * KH:(h + 1) * KH],
                                         query_side[:, :, :].rearrange("f h q -> f (h q)"), start=False, stop=True)
                    last.then_inc(scored, 1)

                def weigh(n, u):
                    pe.wait_ge(exped, n + 1 + FREE)
                    pe.wait_ge(v_ready, n + 1 + 1)
                    for pair in range(PAIRS):
                        for h in range(2):
                            last = pe.matmul(mixed[u][:, pair * 2 * VA:(pair + 1) * 2 * VA],
                                             probs[u][:, h, 2 * pair:2 * pair + 2, :].rearrange("k h q -> k (h q)"),
                                             columns[u][:, h, 2 * pair:2 * pair + 2, :].rearrange("k h f -> k (h f)"), start=h == 0, stop=h == 1)
                    last.then_inc(mixed_ready, 1)

                def turn(n, u):
                    pe.wait_ge(normed_ready, n + 1)
                    pe.wait_ge(o_stored, n + 1)
                    pe.matmul(turned_o[:, 0:NQ], normed[u][:, :, :, :].rearrange("q g s d -> q (g s d)"), P("same_query"),
                              start=True, stop=True).then_inc(o_turned, 1)

                pe.sem_inc(scored, FREE)
                pe.sem_inc(mixed_ready, FREE)
                pe.sem_inc(o_turned, FREE)
                pe.wait_ge(loaded, 32)
                pe.wait_ge(prepared, 4)
                score(0, 0)
                score(1, 1)
                weigh(0, 0)
                UNROLLED = 10
                with pe.Fori(0, (BLOCKS - 2) // UNROLLED) as i:
                    for r in range(UNROLLED):
                        n = i * UNROLLED + (1 + r)
                        score(n + 1, r % 2)
                        weigh(n, 1 - r % 2)
                        turn(n - 1, r % 2)
                weigh(BLOCKS - 1, 1)
                turn(BLOCKS - 2, 0)
                turn(BLOCKS - 1, 1)


def out_conv(nc, P, OP, wout, XN, X):
    SLABS = ((0, 26), (26, PW), (PW, PW + 26), (PW + 26, 2 * PW))
    with Stage(nc, "oc") as s:
        high, low = (s.sb(n, [128, B * PW, PW], F32R) for n in ("high", "low"))
        wout_high, wout_low = (s.sb(n, [128, 9, C], F32R) for n in ("wout_high", "wout_low"))
        conv = [s.ps(f"conv{u}") for u in range(2)]
        rounded, split, conv_ready, conv_used, summed = map(s.sem, ("rounded", "split", "conv_ready", "conv_used", "summed"))
        with nc.Block() as block:
            @block.gpsimd
            def _(pool):
                pool.tensor_tensor(X[:, :, :], X[:, :, :], XN[:, :, :], ALU.add).then_inc(summed, 1)

            @block.scalar
            def _(act):
                act.activation(wout_high[:, :, :], wout[:, :, :], ACT.Copy).then_inc(rounded, 1)
                for a, b in SLABS:
                    act.activation(high[:, a:b, :], OP[:, a:b, :], ACT.Copy).then_inc(rounded, 1)

            @block.tensor
            def _(pe):
                def convolve(b, i):
                    t = b * TB + i
                    if i % 3 == 0:
                        pe.wait_ge(split, b * 2 + i // 3 + 2)
                    pe.wait_ge(conv_used, t + 1)
                    products = [(tap, w, x) for tap in range(9) for w, x in ((wout_high, high), (wout_high, low), (wout_low, high))]
                    for k, (tap, w, x) in enumerate(products):
                        last = pe.matmul(rows48(conv[i % 2][:, 0:T]), w[:, tap, :], x[:, ds(b * PW + i * TR + tap // 3, TR), tap % 3:tap % 3 + W],
                                         start=k == 0, stop=k == len(products) - 1)
                    last.then_inc(conv_ready, 1)

                with pe.Fori(0, B) as b:
                    for i in range(TB):
                        convolve(b, i)

            @block.vector
            def _(dve):
                dve.sem_inc(conv_used, FREE)
                dve.wait_ge(rounded, 1)
                dve.tensor_tensor(wout_low[:, :, :], wout[:, :, :], wout_high[:, :, :], ALU.subtract).then_inc(split, 1)
                for k, (a, b) in enumerate(SLABS):
                    dve.wait_ge(rounded, k + 2)
                    dve.tensor_tensor(low[:, a:b, :], OP[:, a:b, :], high[:, a:b, :], ALU.subtract).then_inc(split, 1)
                dve.wait_ge(summed, 1)
                with dve.Fori(0, B) as b:
                    for i in range(TB):
                        t = b * TB + i
                        dve.wait_ge(conv_ready, t + 1)
                        dve.scalar_tensor_tensor(tile(X, t), rows48(conv[i % 2][:, 0:T]), P("out_b"), tile(X, t), ALU.add, ALU.add).then_inc(conv_used, 1)


def prefix(link, dve, a, b, out, length, at):
    source, target, step = a, b, 1
    while step < length:
        to = out if step * 2 >= length else target
        dve.tensor_copy(at(to, 0, step), at(source, 0, step))
        link(dve.tensor_tensor(at(to, step, length), at(source, step, length), at(source, 0, length - step), ALU.add))
        source, target, step = to, source, step * 2


def dispatch(nc, P, name, XF, logits_ps, bias, top, renormalise, tokens, token_of, target_of, second_of, expert_codes):
    groups = expert_codes.shape[1]
    tiles = groups * GROUP
    RING = 6
    with Stage(nc, name) as s:
        logits, shifted, expo, probs, left, near, counted, other, before, place = (
            s.sb(n, [128, NC, E]) for n in ("logits", "shifted", "expo", "probs", "left", "near", "counted", "other", "before", "place"))
        pick = [s.sb(f"pick{k}", [128, NC, E]) for k in range(top)]
        order = s.sb("order", [128, E])
        peak, total, inv, best = (s.sb(n, [128, NC]) for n in ("peak", "total", "inv", "best"))
        weight = [s.sb(f"weight{k}", [128, NC]) for k in range(top)]
        tiles_of, ends, ends_a, ends_b, starts = (s.sb(n, [128, E]) for n in ("tiles_of", "ends", "ends_a", "ends_b", "starts"))
        past = s.sb("past", [128, tiles, E])
        passed = s.sb("passed", [128, tiles])
        code = s.sb("code", [128, groups])
        slot = s.sb("slot", [128, NC])
        tile_of, row_of = ([s.sb(f"{n}{k}", [128, NC]) for k in range(top)] for n in ("tile_of", "row_of"))
        has_row = [s.sb(f"has_row{r}", [128, 128], F32R) for r in range(RING)]
        has_tile = [s.sb(f"has_tile{r}", [128, tiles], F32R) for r in range(RING)]
        code_of, other_code = s.sb("code_of", [128, tiles]), s.sb("other_code", [128, tiles])
        unused = s.sb("unused", [128, tiles])
        rows = s.sb("rows", [128, NC, ROW])
        within, totals, found = s.ps("within"), s.ps("totals"), s.ps("found")
        turned = [s.ps(f"turned{u}") for u in range(2)]
        step, exp_in, exp_out, picked, ranked, rows_turned, rows_copied, gates_ready, written = map(
            s.sem, ("step", "exp_in", "exp_out", "picked", "ranked", "rows_turned", "rows_copied", "gates_ready", "written"))
        slots_ready, by_dve, by_pool, placed = map(s.sem, ("slots_ready", "by_dve", "by_pool", "placed"))
        ITEMS = [(k, n) for k in range(top) for n in range(NC)]
        POOLS = 4

        def per_token(ap):
            return along(ap[:, :], E)

        def flat(ap):
            return ap[:, :, :].rearrange("p n e -> p (n e)")

        def every_token(ap):
            return ap.rearrange("p (a e) -> p a e", a=1).broadcast_to([128, NC, E])

        with nc.Block() as block:
            @block.tensor
            def _(pe):
                for t in range(NT):
                    if t >= 2:
                        pe.wait_ge(rows_copied, t - 1)
                    for j in range(CH):
                        last = pe.transpose(turned[t % 2][:, j * 128:(j + 1) * 128], chunk(XF, t * CH + j), P("identity"))
                    last.then_inc(rows_turned, 1)
                pe.wait_ge(picked, 1)
                pe.matmul(within[:, 0:NC * E], P("earlier"), flat(counted), start=True, stop=True)
                pe.matmul(totals[:, 0:NC * E], P("ones"), flat(counted), start=True, stop=True).then_inc(ranked, 1)
                for i in range(len(ITEMS)):
                    if i % POOLS == POOLS - 1:
                        pe.wait_ge(by_pool, i // POOLS + 1)
                    else:
                        pe.wait_ge(by_dve, i - i // POOLS + 1)
                    k, n = ITEMS[i]
                    pe.matmul(found[:, k * tiles:(k + 1) * tiles], has_row[i % RING][:, :], has_tile[i % RING][:, :],
                              start=n == 0, stop=n == NC - 1).then_inc(placed, 1)

            @block.scalar
            def _(act):
                act.preload_act_table(ACT.Exp)
                act.wait_ge(exp_in, 1)
                act.activation(expo[:, :, :], shifted[:, :, :], ACT.Exp).then_inc(exp_out, 1)
                for t in range(NT):
                    act.wait_ge(rows_turned, t + 1)
                    act.activation(rows[:, t * CH:(t + 1) * CH, 0:C], turned[t % 2][:, 0:T].rearrange("p (n c) -> p n c", c=C), ACT.Copy).then_inc(rows_copied, 1)

            @block.sync
            def _(sp):
                sp.wait_ge(rows_copied, NT)
                sp.wait_ge(gates_ready, 1)
                sp.dma_start(tokens.rearrange("(n p) c -> p n c", p=128), rows[:, :, :]).then_inc(written, 16)
                sp.wait_ge(written, 16)

            def find(engine, i, ready):
                k, n = ITEMS[i]
                if i >= RING:
                    engine.wait_ge(placed, i - RING + 1)
                engine.tensor_scalar(has_row[i % RING][:, :], P("lane"), row_of[k][:, n:n + 1], None, ALU.is_equal)
                engine.tensor_scalar(has_tile[i % RING][:, :], P("tile_number", width=tiles), tile_of[k][:, n:n + 1], P("token_code", first=n, width=1),
                                     ALU.is_equal, ALU.mult).then_inc(ready, 1)

            @block.gpsimd
            def _(pool):
                pool.wait_ge(slots_ready, 1)
                for i in range(POOLS - 1, len(ITEMS), POOLS):
                    find(pool, i, by_pool)

            @block.vector
            def _(dve):
                link = Chain(dve, step)
                dve.memset(rows[:, :, C:ROW], 0.0)
                for e in range(E):
                    last = dve.memset(order[:, e:e + 1], float(E - e))
                link(last)
                psum = logits_ps[:, 0:NC * E].rearrange("p (n e) -> p n e", e=E)
                if bias is None:
                    link(dve.tensor_copy(logits[:, :, :], psum))
                else:
                    link(dve.tensor_tensor(logits[:, :, :], psum, every_token(bias), ALU.add))
                link(dve.tensor_reduce(peak[:, :], logits[:, :, :], AX.X, ALU.max))
                dve.tensor_tensor(shifted[:, :, :], logits[:, :, :], per_token(peak), ALU.subtract).then_inc(exp_in, 1)
                dve.wait_ge(exp_out, 1)
                link(dve.tensor_reduce(total[:, :], expo[:, :, :], AX.X, ALU.add))
                link(dve.reciprocal(inv[:, :], total[:, :]))
                link(dve.tensor_tensor(probs[:, :, :], expo[:, :, :], per_token(inv), ALU.mult))
                source = probs
                for k in range(top):
                    link(dve.tensor_reduce(weight[k][:, :], source[:, :, :], AX.X, ALU.max))
                    link(dve.tensor_tensor(near[:, :, :], source[:, :, :], per_token(weight[k]), ALU.is_equal))
                    link(dve.tensor_tensor(near[:, :, :], near[:, :, :], every_token(order[:, :]), ALU.mult))
                    link(dve.tensor_reduce(best[:, :], near[:, :, :], AX.X, ALU.max))
                    link(dve.tensor_tensor(pick[k][:, :, :], near[:, :, :], per_token(best), ALU.is_equal))
                    if k + 1 < top:
                        link(dve.scalar_tensor_tensor(left[:, :, :], pick[k][:, :, :], -2.0, source[:, :, :], ALU.mult, ALU.add))
                        source = left
                if top == 1:
                    dve.tensor_copy(counted[:, :, :], pick[0][:, :, :]).then_inc(picked, 1)
                    dve.sem_inc(gates_ready, 1)
                else:
                    dve.tensor_tensor(counted[:, :, :], pick[0][:, :, :], pick[1][:, :, :], ALU.add).then_inc(picked, 1)
                if renormalise:
                    link(dve.tensor_tensor(total[:, :], weight[0][:, :], weight[1][:, :], ALU.add))
                    link(dve.reciprocal(inv[:, :], total[:, :]))
                    for k in range(top):
                        link(dve.tensor_tensor(weight[k][:, :], weight[k][:, :], inv[:, :], ALU.mult))
                if top == 2:
                    for k in range(top):
                        last = dve.tensor_copy(rows[:, :, C + k], weight[k][:, :])
                    last.then_inc(gates_ready, 1)
                dve.wait_ge(ranked, 1)
                all_of = totals[:, 0:NC * E].rearrange("p (n e) -> p n e", e=E)
                link(dve.tensor_copy(other[:, :, :], all_of))
                prefix(link, dve, other, near, before, NC, lambda ap, i, j: ap[:, i:j, :])
                link(dve.tensor_scalar(tiles_of[:, :], before[:, NC - 1, :], 127.0, 1.0 / 128, ALU.add, ALU.mult))
                link(dve.tensor_scalar(tiles_of[:, :], tiles_of[:, :], 63.75 / 128, ROUND, ALU.subtract, ALU.add))
                link(dve.tensor_scalar(tiles_of[:, :], tiles_of[:, :], ROUND, None, ALU.subtract))
                link(dve.tensor_copy(ends_a[:, :], tiles_of[:, :]))
                prefix(link, dve, ends_a, ends_b, ends, E, lambda ap, i, j: ap[:, i:j])
                link(dve.tensor_tensor(starts[:, :], ends[:, :], tiles_of[:, :], ALU.subtract))
                link(dve.tensor_scalar(starts[:, :], starts[:, :], 128.0, None, ALU.mult))
                link(dve.tensor_tensor(place[:, :, :], before[:, :, :], all_of, ALU.subtract))
                link(dve.tensor_tensor(place[:, :, :], place[:, :, :], within[:, 0:NC * E].rearrange("p (n e) -> p n e", e=E), ALU.add))
                link(dve.tensor_tensor(place[:, :, :], place[:, :, :], every_token(starts[:, :]), ALU.add))
                for k in range(top):
                    link(dve.tensor_tensor(near[:, :, :], place[:, :, :], pick[k][:, :, :], ALU.mult))
                    link(dve.tensor_reduce(slot[:, :], near[:, :, :], AX.X, ALU.add))
                    link(dve.tensor_scalar(tile_of[k][:, :], slot[:, :], -63.5, 1.0 / 128, ALU.add, ALU.mult))
                    link(dve.tensor_scalar(tile_of[k][:, :], tile_of[k][:, :], ROUND, None, ALU.add))
                    link(dve.tensor_scalar(tile_of[k][:, :], tile_of[k][:, :], ROUND, None, ALU.subtract))
                    link(dve.scalar_tensor_tensor(row_of[k][:, :], tile_of[k][:, :], -128.0, slot[:, :], ALU.mult, ALU.add))
                dve.sem_inc(slots_ready, 1)
                for i in range(len(ITEMS)):
                    if i % POOLS != POOLS - 1:
                        find(dve, i, by_dve)
                link(dve.tensor_tensor(past[:, :, :], ends[:, :].rearrange("p (a e) -> p a e", a=1).broadcast_to([128, tiles, E]),
                                       along(P("tile_number", width=tiles), E), ALU.is_le))
                link(dve.tensor_reduce(passed[:, :], past[:, :, :], AX.X, ALU.add))
                link(dve.tensor_scalar(passed[:, :], passed[:, :], float(E - 1), None, ALU.min))
                of_group = passed[:, :].rearrange("p (g a) -> p g a", a=GROUP)
                link(dve.tensor_copy(code[:, :], of_group[:, :, GROUP - 1]))
                for a in range(GROUP - 2, -1, -1):
                    link(dve.scalar_tensor_tensor(code[:, :], code[:, :], float(E), of_group[:, :, a], ALU.mult, ALU.add))
                link(dve.tensor_copy(passed[:, 0:groups], code[:, :]))
                link(dve.scalar_tensor_tensor(code[:, 0:groups - 1], passed[:, 1:groups], float(E ** GROUP), passed[:, 0:groups - 1], ALU.mult, ALU.add))
                dve.tensor_copy(expert_codes[0:1, :], code[0:1, :])
                dve.wait_ge(placed, len(ITEMS))
                link(dve.tensor_copy(code_of[:, :], found[:, 0:tiles]))
                if top == 2:
                    link(dve.tensor_copy(other_code[:, :], found[:, tiles:2 * tiles]))
                    link(dve.tensor_scalar(second_of[:, :], other_code[:, :], 0.0, None, ALU.not_equal))
                    link(dve.tensor_tensor(code_of[:, :], code_of[:, :], other_code[:, :], ALU.add))
                else:
                    link(dve.memset(second_of[:, :], 0.0))
                link(dve.tensor_scalar(passed[:, :], code_of[:, :], -2.0, NTOK / 2, ALU.mult, ALU.add))
                link(dve.scalar_tensor_tensor(passed[:, :], code_of[:, :], 0.0, passed[:, :], ALU.is_lt, ALU.mult))
                link(dve.tensor_tensor(passed[:, :], passed[:, :], code_of[:, :], ALU.add))
                link(dve.tensor_scalar(unused[:, :], code_of[:, :], 0.0, None, ALU.is_equal))
                link(dve.tensor_tensor(unused[:, :], unused[:, :], P("unused_target", width=tiles), ALU.mult))
                link(dve.tensor_tensor(unused[:, :], unused[:, :], passed[:, :], ALU.add))
                link(dve.tensor_scalar(token_of[:, :], passed[:, :], 1.0, 0.0, ALU.subtract, ALU.max))
                link(dve.scalar_tensor_tensor(target_of[:, :], second_of[:, :], float(NTOK), unused[:, :], ALU.mult, ALU.add))
                dve.tensor_scalar(target_of[:, :], target_of[:, :], 1.0, None, ALU.subtract)


def experts(nc, P, name, tokens, token_of, target_of, second_of, expert_codes, w_in, act_func, biases, w_out, targets, weights_loaded, gated_unit, weighted):
    G = GROUP
    PAIR = 2 * G
    groups = expert_codes.shape[1]
    tiles = groups * G
    HID = 256 if gated_unit else 512
    HC = HID // 128
    with Stage(nc, name) as s:
        rows = [s.sb(f"rows{u}", [128, G, ROW]) for u in range(2)]
        gates = [s.sb(f"gates{u}", [128, G]) for u in range(2)]
        to = [s.sb(f"to{u}", [128, G], I32) for u in range(2)]
        source = [s.sb(f"source{u}", [128, G], I32) for u in range(2)]
        xg = [s.sb(f"xg{u}", [128, G * 128]) for u in range(2)]
        h = [s.sb(f"h{a}", [128, HID]) for a in range(G)]
        raised = [s.sb(f"raised{a}", [128, HID]) for a in range(G)] if gated_unit else h
        ht = [s.sb(f"ht{u}", [128, HID]) for u in range(2)]
        y = [[s.sb(f"y{u}{a}", [128, C]) for a in range(G)] for u in range(2)]
        x_turned = s.ps("x_turned")
        pre = [s.ps(f"pre{u}") for u in range(2)]
        h_turned = [s.ps(f"h_turned{u}") for u in range(2)]
        out = [s.ps(f"out{u}") for u in range(2)]
        rows_turned, source_ready, gates_ready, to_ready, xg_ready, pre_ready, biased, hidden, turned, ht_ready, out_ready, taken, y_ready, sending, sent = map(
            s.sem, ("rows_turned", "source_ready", "gates_ready", "to_ready", "xg_ready", "pre_ready", "biased", "hidden", "turned", "ht_ready",
                    "out_ready", "taken", "y_ready", "sending", "sent"))
        fetching, gate_step = s.sem("fetching"), s.sem("gate_step")
        apart = s.sb("apart", [128, G])
        rows_loaded = [s.sem(f"rows_loaded{u}") for u in range(2)]
        scattered = [[s.sem(f"scattered{u}{a}") for a in range(G)] for u in range(2)]
        if gated_unit:
            raised_ready = s.sem("raised_ready")

        def steps(engine, body):
            loops = (groups - 3) // 2
            for r in range(-2, 1):
                body(0, r)
            with engine.Fori(0, loops) as j:
                for r in range(1, 1 + PAIR):
                    body(j, r)
            for r in range(1 + loops * PAIR, tiles + 1):
                body(0, r)

        LOADS = 16 * G

        def exists(j, m):
            return not isinstance(j, int) or 0 <= m < tiles

        class Experts:

            def __init__(self, engine):
                self.engine, self.group = engine, 0

            def __call__(self, j, r):
                if r % G == 1 or r == -2:
                    self.group = max(r // G, 0)
                    self.code = self.engine.value_load(expert_codes[0:1, ds(j * 2 + self.group, 1)], min_val=0, max_val=E ** (2 * G) - 1)
                return [(self.code >> (3 * max(m - self.group * G, 0))) & (E - 1) for m in (r + 2, r - 1)]

        with nc.Block() as block:
            @block.tensor
            def _(pe):
                experts_of = Experts(pe)

                def turn_rows(j, g):
                    pe.wait_ge(rows_loaded[g % 2], (j + g // 2) * LOADS + LOADS)
                    if g > 0:
                        pe.wait_ge(xg_ready, j * 2 + g)
                    for a in range(G):
                        last = pe.transpose(x_turned[:, a * 128:(a + 1) * 128], rows[g % 2][:, a, 0:C], P("identity"))
                    last.then_inc(rows_turned, 1)

                def step(j, r):
                    n = j * PAIR + r
                    into, out_of = experts_of(j, r)
                    if exists(j, r):
                        pe.wait_ge(raised_ready if gated_unit else hidden, n + 1 + G)
                        pe.wait_ge(ht_ready, n + 1)
                        for c in range(HC):
                            last = pe.transpose(h_turned[r % 2][:, c * 128:(c + 1) * 128], raised[r % G][:, c * 128:(c + 1) * 128], P("identity"))
                        last.then_inc(turned, 1)
                    if r % G == 0 and exists(j, r + G):
                        turn_rows(j, r // G + 1)
                    if exists(j, r + 2):
                        m = r + 2
                        pe.wait_ge(xg_ready, j * 2 + m // G + 1)
                        pe.wait_ge(raised_ready if gated_unit else biased, n + 2 + 1 + G - 2)
                        pe.matmul(pre[m % 2][:, :], xg[m // G % 2][:, m % G * 128:(m % G + 1) * 128], w_in[:, ds(into * 512, 512)],
                                  start=True, stop=True).then_inc(pre_ready, 1)
                    if exists(j, r - 1):
                        m = r - 1
                        pe.wait_ge(ht_ready, n - 1 + 1 + 2)
                        pe.wait_ge(taken, n - 1 + 1)
                        for c in range(HC):
                            last = pe.matmul(out[m % 2][:, 0:C], ht[m % 2][:, c * 128:(c + 1) * 128],
                                             w_out[:, ds(out_of * (HC * C) + c * C, C)], start=c == 0, stop=c == HC - 1)
                        last.then_inc(out_ready, 1)

                pe.wait_ge(*weights_loaded)
                pe.sem_inc(turned, G)
                pe.sem_inc(out_ready, FREE)
                turn_rows(0, 0)
                steps(pe, step)

            @block.scalar
            def _(act):
                def copy_rows(j, g):
                    act.wait_ge(rows_turned, j * 2 + g + 1)
                    act.activation(xg[g % 2][:, :], x_turned[:, 0:G * 128], ACT.Copy).then_inc(xg_ready, 1)

                def step(j, r):
                    n = j * PAIR + r
                    if exists(j, r):
                        act.wait_ge(turned, n + 1 + G)
                        act.wait_ge(out_ready, n + 1)
                        act.activation(ht[r % 2][:, :], h_turned[r % 2][:, 0:HID], ACT.Copy).then_inc(ht_ready, 1)
                    if r % G == 0 and exists(j, r + G):
                        copy_rows(j, r // G + 1)
                    if exists(j, r + 2):
                        m = r + 2
                        if gated_unit:
                            act.wait_ge(pre_ready, n + 2 + 1)
                            act.wait_ge(raised_ready, n + 2 + 1)
                            act.activation(h[m % G][:, :], pre[m % 2][:, 0:HID], act_func).then_inc(hidden, 1)
                        else:
                            act.wait_ge(biased, n + 2 + 1 + G)
                            act.activation(h[m % G][:, :], h[m % G][:, :], act_func).then_inc(hidden, 1)

                act.preload_act_table(act_func)
                act.sem_inc(hidden, G)
                act.sem_inc(ht_ready, FREE)
                copy_rows(0, 0)
                steps(act, step)

            @block.vector
            def _(dve):
                experts_of = Experts(dve)

                def take_sources(j, g):
                    dve.tensor_copy(source[g % 2][:, :], token_of[:, ds(j * PAIR + g * G, G)]).then_inc(source_ready, 1)

                def take_gates(j, g):
                    u = g % 2
                    dve.wait_ge(rows_loaded[u], (j + g // 2) * LOADS + LOADS)
                    if weighted:
                        first, second = rows[u][:, :, C], rows[u][:, :, C + 1]
                        dve.tensor_tensor(apart[:, :], second, first, ALU.subtract).then_inc(gate_step, 1)
                        dve.wait_ge(gate_step, (j * 2 + g) * 2 + 1)
                        dve.tensor_tensor(apart[:, :], apart[:, :], second_of[:, ds(j * PAIR + g * G, G)], ALU.mult).then_inc(gate_step, 1)
                        dve.wait_ge(gate_step, (j * 2 + g) * 2 + 2)
                        dve.tensor_tensor(gates[u][:, :], apart[:, :], first, ALU.add).then_inc(gates_ready, 1)
                    else:
                        dve.sem_inc(gates_ready, 1)

                def step(j, r):
                    n = j * PAIR + r
                    if not gated_unit:
                        into, out_of = experts_of(j, r)
                    if exists(j, r + 2):
                        m = r + 2
                        dve.wait_ge(pre_ready, n + 2 + 1)
                        dve.wait_ge(turned, n + 2 + 1)
                        if gated_unit:
                            dve.wait_ge(hidden, n + 2 + 1 + G)
                            dve.tensor_tensor(raised[m % G][:, :], h[m % G][:, :], pre[m % 2][:, HID:2 * HID], ALU.mult).then_inc(raised_ready, 1)
                        else:
                            dve.tensor_tensor(h[m % G][:, :], pre[m % 2][:, :], biases[:, ds(into * 512, 512)], ALU.add).then_inc(biased, 1)
                    if exists(j, r - 1):
                        m = r - 1
                        a, g = m % G, m // G
                        u = g % 2
                        if a == 0:
                            dve.wait_ge(sent, j * 2 + g + 1)
                            dve.tensor_copy(to[u][:, :], target_of[:, ds(j * PAIR + g * G, G)]).then_inc(to_ready, 1)
                            if exists(j, m + G):
                                take_gates(j, g + 1)
                            if exists(j, m + 3 * G):
                                take_sources(j, g + 3)
                        dve.wait_ge(out_ready, n - 1 + 1 + FREE)
                        if weighted:
                            dve.wait_ge(gates_ready, j * 2 + g + 1)
                        if gated_unit:
                            dve.tensor_scalar(y[u][a][:, :], out[m % 2][:, 0:C], gates[u][:, a:a + 1], None, ALU.mult).then_inc(taken, 1)
                        else:
                            dve.tensor_tensor(y[u][a][:, :], out[m % 2][:, 0:C], biases[:, ds(out_of * C + E * 512, C)], ALU.add).then_inc(taken, 1)
                            if weighted:
                                dve.wait_ge(taken, n - 1 + 1 + FREE)
                                dve.tensor_scalar(y[u][a][:, :], y[u][a][:, :], gates[u][:, a:a + 1], None, ALU.mult).then_inc(y_ready, 1)

                dve.sem_inc(raised_ready if gated_unit else biased, G)
                dve.sem_inc(taken, FREE)
                for g in range(3):
                    if g == 2:
                        dve.wait_ge(rows_loaded[0], LOADS)
                    take_sources(0, g)
                take_gates(0, 0)
                steps(dve, step)

            @block.gpsimd
            def _(pool):
                def sent_group(j, u):
                    for a in range(G):
                        pool.wait_ge(scattered[u][a], j * 16 + 16)
                    pool.sem_inc(sent, 1)

                def gather(i, u, a):
                    if a == 0:
                        pool.wait_ge(source_ready, i + 1)
                        if not isinstance(i, int) or i >= 2:
                            pool.wait_ge(rows_turned, i - 1)
                            pool.wait_ge(gates_ready, i - 1)
                        pool.sem_inc(fetching, 1)
                    pool.indirect_dma_start(rows[u][:, a, :], None, tokens, bass.IndirectOffsetOnAxis(ap=source[u][:, a:a + 1], axis=0)).then_inc(rows_loaded[u], 16)

                def group(i, j, u):
                    for a in range(G):
                        n = i * G + a
                        if not isinstance(i, int) or i + 3 < groups:
                            gather(i + 3, 1 - u, a)
                        if a == 0:
                            pool.wait_ge(to_ready, i + 1)
                        if gated_unit or not weighted:
                            pool.wait_ge(taken, n + 1 + FREE)
                        else:
                            pool.wait_ge(y_ready, n + 1)
                        pool.sem_inc(sending, 1)
                        pool.indirect_dma_start(targets, bass.IndirectOffsetOnAxis(ap=to[u][:, a:a + 1], axis=0), y[u][a][:, :], None).then_inc(scattered[u][a], 16)

                pool.sem_inc(sent, FREE)
                for g in range(3):
                    for a in range(G):
                        gather(g, g % 2, a)
                group(0, 0, 0)
                loops = (groups - 4) // 2
                with pool.Fori(0, loops) as j:
                    for u in range(2):
                        group(j * 2 + (u + 1), j + u, 1 - u)
                        sent_group(j, u)
                for i in range(loops * 2 + 1, groups):
                    group(i, i // 2, i % 2)
                    sent_group((i - 1) // 2, (i - 1) % 2)
                sent_group((groups - 1) // 2, (groups - 1) % 2)


def combine(nc, P, name, targets, top, X, extra=None):
    PARTS = 4
    with Stage(nc, name) as s:
        rows = [s.sb(f"rows{k}", [128, NC, C]) for k in range(top)]
        turned = [s.ps(f"turned{u}") for u in range(2)]
        loaded = [s.sem(f"loaded{g}") for g in range(PARTS)]
        summed, extra_added, rows_turned, added = map(s.sem, ("summed", "extra_added", "rows_turned", "added"))
        per = NC // PARTS
        with nc.Block() as block:
            @block.sync
            def _(sp):
                for g in range(PARTS):
                    for k in range(top):
                        first = k * NTOK + g * per * 128
                        sp.dma_start(rows[k][:, g * per:(g + 1) * per, :],
                                     targets[first:first + per * 128, :].rearrange("(n p) c -> p n c", p=128)).then_inc(loaded[g], 16)

            @block.gpsimd
            def _(pool):
                if extra is not None:
                    pool.tensor_tensor(X[:, :, :], X[:, :, :], extra[:, :, :], ALU.add).then_inc(extra_added, 1)

            @block.tensor
            def _(pe):
                for t in range(NT):
                    if t % (NT // PARTS) == 0:
                        if top == 1:
                            pe.wait_ge(loaded[t // (NT // PARTS)], 16)
                        else:
                            pe.wait_ge(summed, t // (NT // PARTS) + 1)
                    if t >= 2:
                        pe.wait_ge(added, t - 1)
                    for j in range(CH):
                        last = pe.transpose(turned[t % 2][:, j * 128:(j + 1) * 128], rows[0][:, t * CH + j, :], P("identity"))
                    last.then_inc(rows_turned, 1)

            @block.vector
            def _(dve):
                for g in range(PARTS if top > 1 else 0):
                    dve.wait_ge(loaded[g], 16 * top)
                    part = slice(g * per, (g + 1) * per)
                    dve.tensor_tensor(rows[0][:, part, :], rows[0][:, part, :], rows[1][:, part, :], ALU.add).then_inc(summed, 1)
                if extra is not None:
                    dve.wait_ge(extra_added, 1)
                for t in range(NT):
                    dve.wait_ge(rows_turned, t + 1)
                    dve.tensor_tensor(X[:, t * TR:(t + 1) * TR, :], X[:, t * TR:(t + 1) * TR, :], rows48(turned[t % 2][:, 0:T]), ALU.add).then_inc(added, 1)


def attention(nc, P, XN, X):
    KEYS = H * W
    KC = KEYS // 128
    GROUPS = KEYS // T
    GS = B * GROUPS
    PIECES = 5
    PC = 512
    VC = C + 2
    STK = 112
    LOW_K, LOW_Q = 64, 96
    SCORES = 2
    RING = 6
    with Stage(nc, "at") as s:
        q, k = (s.sb(n, [STK, NTOK], F32R) for n in ("q", "k"))
        high = [s.sb(f"high{m}", [128, T], F32R) for m in range(2)]
        v = s.sb("v", [128, NC, VC])
        with ExitStack() as first:
            proj = [first.enter_context(nc.psum_tensor(f"at_proj{m}", [128, 512], F32)) for m in range(2)]
            values = [first.enter_context(nc.psum_tensor(f"at_values{u}", [128, 512], F32)) for u in range(2)]
            projected, copied, proj_used, valued, values_used = map(s.sem, ("projected", "copied", "proj_used", "valued", "values_used"))
            with nc.Block() as block:
                @block.tensor
                def _(pe):
                    for t in range(NT):
                        for m, weights in enumerate(("wq", "wk")):
                            if t:
                                pe.wait_ge(proj_used, 2 * t - 1 + m)
                            pe.matmul(rows48(proj[m][0:128, 0:T]), P(weights), XN[:, t * TR:(t + 1) * TR, :], start=True, stop=True).then_inc(projected, 1)
                        if t >= 2:
                            pe.wait_ge(values_used, t - 1)
                        for j in range(CH):
                            last = pe.matmul(values[t % 2][:, j * C:(j + 1) * C], chunk(XN, t * CH + j), P("wv"), start=True, stop=True)
                        last.then_inc(valued, 1)

                @block.scalar
                def _(act):
                    for t in range(NT):
                        for m, (out, bias) in enumerate(((q, "bq"), (k, "bk"))):
                            act.wait_ge(projected, 2 * t + m + 1)
                            if t:
                                act.wait_ge(proj_used, 2 * t - 1 + m)
                            act.activation(high[m][0:STK, :], proj[m][0:STK, 0:T], ACT.Identity, bias=P(bias, rows=STK))
                            act.activation(out[:, t * T:(t + 1) * T], proj[m][0:STK, 0:T], ACT.Identity, bias=P(bias, rows=STK)).then_inc(copied, 1)

                @block.vector
                def _(dve):
                    dve.memset(v[:, :, C:VC], 1.0)
                    for t in range(NT):
                        for m, (out, bias, low) in enumerate(((q, "bq", LOW_Q), (k, "bk", LOW_K))):
                            rows = slice(low, low + DH)
                            dve.wait_ge(copied, 2 * t + m + 1)
                            dve.scalar_tensor_tensor(out[rows, t * T:(t + 1) * T], proj[m][rows, 0:T], P(bias)[rows, :], high[m][rows, :],
                                                     ALU.add, ALU.subtract).then_inc(proj_used, 1)
                        dve.wait_ge(valued, t + 1)
                        dve.tensor_copy(v[:, t * CH:(t + 1) * CH, 0:C], values[t % 2][:, 0:T].rearrange("p (n c) -> p n c", c=C)).then_inc(values_used, 1)

        staged = [s.sb(f"staged{u}", [STK, T], F32R) for u in range(2)]
        peaks = s.sb("peaks", [128, CH, PIECES])
        minus_peak = s.sb("minus_peak", [128, CH])
        peak_high = s.sb("peak_high", [128, CH], F32R)
        peak_parts = s.sb("peak_parts", [128, CH, 32])
        probs = [s.sb(f"probs{r}", [128, T]) for r in range(RING)]
        inv = s.sb("inv", [128, CH])
        normed = s.sb("normed", [128, CH, C])
        sampled = [s.ps(f"sampled{u}") for u in range(2)]
        scores = [s.ps(f"scores{u}") for u in range(SCORES)]
        mixed = [s.ps(f"mixed{c}") for c in range(CH)]
        turned = s.ps("turned")
        q_staged, sampled_ready, sampled_used, peaks_ready, peaks_turned, peaks_staged, scored, exped, mixed_ready, normed_ready, mix_turned, added, step = map(
            s.sem, ("q_staged", "sampled_ready", "sampled_used", "peaks_ready", "peaks_turned", "peaks_staged", "scored", "exped",
                    "mixed_ready", "normed_ready", "mix_turned", "added", "step"))
        peak_step, inv_ready = s.sem("peak_step"), s.sem("inv_ready")

        def groups(engine, body):
            for b in range(B):
                body(b * GROUPS, 0, b, b)
                with engine.Fori(0, GROUPS // 2 - 1) as i:
                    for u in range(2):
                        body(i * 2 + (b * GROUPS + 1 + u), 1 - u, b, b)
                body(b * GROUPS + GROUPS - 1, 1, b, b + 1 if b + 1 < B else None)

        with nc.Block() as block:
            @block.gpsimd
            def _(pool):
                pool.tensor_copy(staged[0][:, :], q[:, 0:T]).then_inc(q_staged, 1)

                def stage(g, u, b, after):
                    if after is not None:
                        pool.wait_ge(scored, g * KC + SCORES)
                        pool.tensor_copy(staged[1 - u][:, :], q[:, ds((g + 1) * T, T)]).then_inc(q_staged, 1)

                groups(pool, stage)

            @block.tensor
            def _(pe):
                def sample(g, u, image, j, c):
                    piece = c * PIECES + j
                    number = g * (CH * PIECES) + piece
                    if piece == 0:
                        pe.wait_ge(q_staged, g + 1)
                    pe.wait_ge(sampled_used, number + 1)
                    cols = min(PC, KEYS - j * PC)
                    pe.matmul(sampled[(u + piece) % 2][:, 0:cols], staged[u][:, c * 128:(c + 1) * 128],
                              k[:, image * KEYS + j * PC:image * KEYS + j * PC + cols], start=True, stop=True).then_inc(sampled_ready, 1)

                def turn_peaks(g):
                    pe.wait_ge(peaks_ready, g + 1)
                    pe.wait_ge(added, g + 1)
                    for c in range(CH):
                        last = pe.matmul(turned[0:32, c * 128:(c + 1) * 128], peak_parts[:, c, :], P("identity"), start=True, stop=True)
                    last.then_inc(peaks_turned, 1)

                def weigh(g, b, n):
                    pe.wait_ge(exped, g * KC + n + 1 + SCORES)
                    if n == 0:
                        pe.wait_ge(normed_ready, g + 1)
                    for c in range(CH):
                        last = pe.matmul(mixed[c][:, 0:VC], probs[n % RING][:, c * 128:(c + 1) * 128], v[:, b * KC + n, :],
                                         start=n == 0, stop=n == KC - 1)
                    last.then_inc(mixed_ready, 1)

                def turn_mix(g):
                    pe.wait_ge(normed_ready, g + 1 + 1)
                    for c in range(CH):
                        last = pe.transpose(turned[:, c * 128:(c + 1) * 128], normed[:, c, :], P("identity"))
                    last.then_inc(mix_turned, 1)

                def body(g, u, b, after):
                    pe.wait_ge(peaks_staged, g + 1)
                    for n in range(KC):
                        pe.wait_ge(exped, g * KC + n + 1)
                        pe.matmul(scores[n % SCORES][:, 0:T], k[:, (b * KC + n) * 128:(b * KC + n + 1) * 128], staged[u][:, :],
                                  start=True, stop=True).then_inc(scored, 1)
                        if n >= 2:
                            weigh(g, b, n - 2)
                        if after is not None and n < CH * PIECES:
                            sample(g + 1, 1 - u, after, n % PIECES, n // PIECES)
                        if n == 5 and not (isinstance(g, int) and g == 0):
                            turn_mix(g - 1)
                    weigh(g, b, KC - 2)
                    weigh(g, b, KC - 1)
                    if after is not None:
                        turn_peaks(g + 1)

                pe.sem_inc(scored, SCORES)
                pe.sem_inc(mixed_ready, RING)
                for piece in range(CH * PIECES):
                    sample(0, 0, 0, piece % PIECES, piece // PIECES)
                turn_peaks(0)
                groups(pe, body)
                turn_mix(GS - 1)

            @block.scalar
            def _(act):
                act.preload_act_table(ACT.Exp)
                act.sem_inc(exped, SCORES)

                def body(g, u, b, after):
                    for n in range(KC):
                        act.wait_ge(scored, g * KC + n + 1 + SCORES)
                        act.wait_ge(mixed_ready, g * KC + n + 1)
                        act.activation(probs[n % RING][:, :], scores[n % SCORES][:, 0:T], ACT.Exp).then_inc(exped, 1)

                groups(act, body)

            @block.vector
            def _(dve):
                link = Chain(dve, step)

                def take_peaks(g, u, pieces):
                    for piece in pieces:
                        c, j = piece // PIECES, piece % PIECES
                        dve.wait_ge(sampled_ready, g * (CH * PIECES) + piece + 1)
                        dve.tensor_reduce(peaks[:, c, j:j + 1], sampled[(u + piece) % 2][:, 0:min(PC, KEYS - j * PC)], AX.X, ALU.max).then_inc(sampled_used, 1)

                def stage_peaks(g, u):
                    dve.wait_ge(sampled_used, (g + 1) * (CH * PIECES) + FREE)
                    dve.wait_ge(peaks_turned, g + 1)
                    dve.tensor_reduce(minus_peak[:, :], peaks[:, :, :], AX.X, ALU.max, negate=True).then_inc(peak_step, 1)
                    dve.wait_ge(peak_step, g * 2 + 1)
                    dve.tensor_copy(peak_high[:, :], minus_peak[:, :]).then_inc(peak_step, 1)
                    dve.wait_ge(peak_step, g * 2 + 2)
                    dve.tensor_copy(peak_parts[:, :, 0], peak_high[:, :])
                    dve.tensor_tensor(peak_parts[:, :, 1], minus_peak[:, :], peak_high[:, :], ALU.subtract).then_inc(peaks_ready, 1)
                    dve.wait_ge(peaks_turned, g + 1 + 1)
                    dve.tensor_copy(staged[u][0:32, :], turned[0:32, 0:T]).then_inc(peaks_staged, 1)

                def normalise(g):
                    dve.wait_ge(mixed_ready, (g + 1) * KC + RING)
                    dve.wait_ge(mix_turned, g + 1)
                    for c in range(CH):
                        last = dve.reciprocal(inv[:, c:c + 1], mixed[c][:, C:C + 1])
                    last.then_inc(inv_ready, 1)
                    dve.wait_ge(inv_ready, g + 1)
                    for c in range(CH):
                        last = dve.tensor_scalar(normed[:, c, :], mixed[c][:, 0:C], inv[:, c:c + 1], None, ALU.mult)
                    last.then_inc(normed_ready, 1)

                def add(g):
                    dve.wait_ge(mix_turned, g + 1 + 1)
                    dve.scalar_tensor_tensor(tile(X, g), rows48(turned[:, 0:T]), P("bv"), tile(X, g), ALU.add, ALU.add).then_inc(added, 1)

                def body(g, u, b, after):
                    before = not (isinstance(g, int) and g == 0)
                    if before:
                        normalise(g - 1)
                    if after is not None:
                        take_peaks(g + 1, 1 - u, range(6))
                    if before:
                        add(g - 1)
                    if after is not None:
                        take_peaks(g + 1, 1 - u, range(6, CH * PIECES))
                        stage_peaks(g + 1, 1 - u)

                dve.sem_inc(sampled_used, FREE)
                dve.sem_inc(peaks_turned, 1)
                dve.sem_inc(mix_turned, 1)
                dve.sem_inc(normed_ready, 1)
                dve.sem_inc(added, 2)
                link(dve.memset(peak_parts[:, :, :], 0.0))
                dve.wait_ge(q_staged, 1)
                take_peaks(0, 0, range(CH * PIECES))
                stage_peaks(0, 0)
                groups(dve, body)
                normalise(GS - 1)
                add(GS - 1)


def dynamic_conv(nc, P, XN, X):
    TAPS = 10
    CM = 32
    with Stage(nc, "dc") as s:
        F = s.sb("f", [128, B * PF, PF])
        filters = s.sb("filters", [128, B, TAPS, C])
        f_high, f_low = (s.sb(n, [128, B * PF, PF], F32R) for n in ("f_high", "f_low"))
        filters_high, filters_low = (s.sb(n, [128, B, TAPS, C], F32R) for n in ("filters_high", "filters_low"))
        sums, mean, g = (s.sb(n, [128, B]) for n in ("sums", "mean", "g"))
        bias = s.sb("bias", [128, 1])
        kernels = [s.sb(f"kernel{m}", [128, B, TAPS]) for m in range(2)]
        middle = s.sb("middle", [128, TAPS])
        second_part = s.sb("second_part", [128, B, TAPS, C])
        g_ps, bias_ps = s.ps("g_ps"), s.ps("bias_ps")
        pre = [s.ps(f"pre{u}") for u in range(2)]
        conv = [s.ps(f"conv{u}") for u in range(2)]
        kernels_ready, part_ready, f_rounded, f_split, rounded, split = map(
            s.sem, ("kernels_ready", "part_ready", "f_rounded", "f_split", "rounded", "split"))
        zeroed, step, mean_ready, g_pre, g_ready, bias_pre, pre_ready, act_taken, dve_taken, filters_ready, conv_ready, conv_used = map(
            s.sem, ("zeroed", "step", "mean_ready", "g_pre", "g_ready", "bias_pre", "pre_ready", "act_taken", "dve_taken",
                    "filters_ready", "conv_ready", "conv_used"))

        def copy_of_f(t, j):
            b, i = t // TB, t % TB
            row = b * PF + i * TR + 2
            first = 1 if j == 3 else 0
            return F[j * CM:(j + 1) * CM, row:row + TR, first + 2 - j:2 - j + W], first

        with nc.Block() as block:
            @block.gpsimd
            def _(pool):
                pool.memset(F[:, :, :], 0.0).then_inc(zeroed, 1)
                for b in range(B):
                    pool.wait_ge(f_rounded, b + 1)
                    image = slice(b * PF, (b + 1) * PF)
                    pool.tensor_tensor(f_low[:, image, :], F[:, image, :], f_high[:, image, :], ALU.subtract).then_inc(f_split, 1)

            @block.tensor
            def _(pe):
                for t in range(NT):
                    if t >= 2:
                        pe.wait_ge(act_taken, t - 1)
                        pe.wait_ge(dve_taken, t - 1)
                    pe.matmul(rows48(pre[t % 2][:, 0:T]), P("conv_w"), XN[:, t * TR:(t + 1) * TR, :], start=True, stop=True).then_inc(pre_ready, 1)
                pe.matmul(bias_ps[:, 0:1], P("fuse1", rows=CM), P("adap_b", rows=CM), start=True, stop=False)
                pe.matmul(bias_ps[:, 0:1], P("fuse2", rows=CM), P("atrous_b", rows=CM), start=False, stop=True).then_inc(bias_pre, 1)
                pe.wait_ge(mean_ready, 1)
                pe.matmul(g_ps[:, 0:B], P("conv_w"), mean[:, :], start=True, stop=True).then_inc(g_pre, 1)
                for b in range(B):
                    pe.wait_ge(f_split, b + 1)
                    pe.wait_ge(split, b + 1)
                    with pe.Fori(0, TB // 2) as i:
                        for u in range(2):
                            t = i * 2 + (b * TB + u)
                            pe.wait_ge(conv_used, t + 1)
                            products = [(tap, w, x) for tap in range(TAPS)
                                        for w, x in ((filters_high, f_high), (filters_high, f_low), (filters_low, f_high))]
                            for k, (tap, w, x) in enumerate(products):
                                last = pe.matmul(rows48(conv[u][:, 0:T]), w[:, b, tap, :],
                                                 x[:, ds(i * (2 * TR) + (b * PF + u * TR + tap % 5), TR), 4 * (tap // 5):4 * (tap // 5) + W],
                                                 start=k == 0, stop=k == len(products) - 1)
                            last.then_inc(conv_ready, 1)

            @block.scalar
            def _(act):
                act.preload_act_table(ACT.Relu)
                act.wait_ge(zeroed, 1)
                for t in range(NT):
                    act.wait_ge(pre_ready, t + 1)
                    for j in range(2):
                        target, first = copy_of_f(t, j)
                        last = act.activation(target, rows48(pre[t % 2][j * CM:(j + 1) * CM, 0:T])[:, :, first:W], ACT.Relu,
                                              bias=P("conv_b")[j * CM:(j + 1) * CM, :])
                    last.then_inc(act_taken, 1)
                act.wait_ge(g_pre, 1)
                act.activation(g[:, :], g_ps[:, 0:B], ACT.Relu, bias=P("conv_b")).then_inc(g_ready, 1)
                act.wait_ge(dve_taken, NT)
                act.wait_ge(act_taken, NT)
                for b in range(B):
                    image = slice(b * PF, (b + 1) * PF)
                    act.activation(f_high[:, image, :], F[:, image, :], ACT.Copy).then_inc(f_rounded, 1)
                    act.wait_ge(kernels_ready, 1)
                    for tap in range(TAPS):
                        act.activation(second_part[:, b, tap, :], P("fuse2"), ACT.Copy, scale=kernels[1][:, b, tap:tap + 1]).then_inc(part_ready, 1)
                    act.wait_ge(filters_ready, (b + 1) * TAPS)
                    act.activation(filters_high[:, b, :, :], filters[:, b, :, :], ACT.Copy).then_inc(rounded, 1)

            @block.vector
            def _(dve):
                link = Chain(dve, step)
                for b in range(B):
                    last = dve.tensor_reduce(sums[:, b:b + 1], XN[:, b * H:(b + 1) * H, :].rearrange("p r w -> p (r w)"), AX.X, ALU.add)
                link(last)
                dve.tensor_scalar(mean[:, :], sums[:, :], 1.0 / (H * W), None, ALU.mult).then_inc(mean_ready, 1)
                dve.wait_ge(zeroed, 1)
                for t in range(NT):
                    dve.wait_ge(pre_ready, t + 1)
                    for j in range(2, 4):
                        target, first = copy_of_f(t, j)
                        last = dve.tensor_scalar(target, rows48(pre[t % 2][j * CM:(j + 1) * CM, 0:T])[:, :, first:W],
                                                 P("conv_b")[j * CM:(j + 1) * CM, :], 0.0, ALU.add, ALU.max)
                    last.then_inc(dve_taken, 1)
                dve.wait_ge(bias_pre, 1)
                link(dve.tensor_scalar(bias[:, :], bias_ps[:, 0:1], P("fuse_b"), None, ALU.add))
                dve.wait_ge(g_ready, 1)
                for kernel, w, kb, mix, mix_b, valid in ((kernels[0], "kernel_w", "kernel_b", "k_w", "k_b", "tap5"),
                                                         (kernels[1], "kernel2_w", "kernel2_b", "k2_w", "k2_b", "tap3")):
                    for b in range(B):
                        link(dve.scalar_tensor_tensor(kernel[:, b, :], P(w), g[:, b:b + 1], P(kb), ALU.mult, ALU.add))
                    link(dve.tensor_tensor(middle[:, :], kernel[:, 0, :], kernel[:, 1, :], ALU.add))
                    link(dve.tensor_scalar(middle[:, :], middle[:, :], 1.0 / B, None, ALU.mult))
                    link(dve.tensor_scalar(middle[:, :], middle[:, :], P(mix, first=1, width=1), P(mix_b), ALU.mult, ALU.add))
                    for b in range(B):
                        link(dve.scalar_tensor_tensor(kernel[:, b, :], kernel[:, b, :], P(mix, width=1), middle[:, :], ALU.mult, ALU.add))
                        link(dve.scalar_tensor_tensor(kernel[:, b, :], kernel[:, b, :], 0.0, P(valid), ALU.max, ALU.mult))
                dve.sem_inc(kernels_ready, 1)
                for b in range(B):
                    for tap in range(TAPS):
                        dve.wait_ge(part_ready, b * TAPS + tap + 1)
                        dve.scalar_tensor_tensor(filters[:, b, tap, :], P("fuse1"), kernels[0][:, b, tap:tap + 1], second_part[:, b, tap, :],
                                                 ALU.mult, ALU.add).then_inc(filters_ready, 1)
                    dve.wait_ge(rounded, b + 1)
                    dve.tensor_tensor(filters_low[:, b, :, :], filters[:, b, :, :], filters_high[:, b, :, :], ALU.subtract).then_inc(split, 1)
                dve.sem_inc(conv_used, FREE)
                with dve.Fori(0, NT // 2) as i:
                    for u in range(2):
                        t = i * 2 + u
                        dve.wait_ge(conv_ready, t + 1)
                        dve.scalar_tensor_tensor(tile(X, t), rows48(conv[u][:, 0:T]), bias[:, 0:1], tile(X, t), ALU.add, ALU.add).then_inc(conv_used, 1)


def quantised(nc, P, U, X):
    with Stage(nc, "qf") as s:
        sums, totals = s.sb("sums", [128, 2]), s.sb("totals", [128, 2])
        shifted, sign, weight = (s.sb(n, [128, C]) for n in ("shifted", "sign", "weight"))
        y = [s.sb(f"y{u}", [128, TR, W]) for u in range(2)]
        level = [s.sb(f"level{u}", [128, TR, W]) for u in range(2)]
        sums_ps = s.ps("sums_ps")
        product = [s.ps(f"product{u}") for u in range(2)]
        step, sums_ready, totals_ready, shifted_ready, sign_ready, weight_ready, product_ready, y_ready, y_used, rounding = map(
            s.sem, ("step", "sums_ready", "totals_ready", "shifted_ready", "sign_ready", "weight_ready", "product_ready", "y_ready", "y_used", "rounding"))
        with nc.Block() as block:
            @block.tensor
            def _(pe):
                pe.wait_ge(sums_ready, 1)
                pe.matmul(sums_ps[:, 0:2], P("ones"), sums[:, :], start=True, stop=True).then_inc(totals_ready, 1)
                pe.wait_ge(weight_ready, 1)
                with pe.Fori(0, NT // 2) as i:
                    for u in range(2):
                        t = i * 2 + u
                        pe.wait_ge(y_ready, t + 1)
                        pe.matmul(rows48(product[u][:, 0:T]), weight[:, :], tile(U, t), start=True, stop=True).then_inc(product_ready, 1)

            @block.scalar
            def _(act):
                act.preload_act_table(ACT.Sign)
                act.sem_inc(y_ready, FREE)
                act.wait_ge(shifted_ready, 1)
                act.activation(sign[:, :], shifted[:, :], ACT.Sign).then_inc(sign_ready, 1)
                with act.Fori(0, NT // 2) as i:
                    for u in range(2):
                        t = i * 2 + u
                        act.wait_ge(product_ready, t + 1)
                        act.wait_ge(y_used, t + 1)
                        act.activation(y[u][:, :, :], rows48(product[u][:, 0:T]), ACT.Identity, bias=P("b2f")).then_inc(y_ready, 1)

            @block.vector
            def _(dve):
                link = Chain(dve, step)
                dve.tensor_reduce(sums[:, 0:1], P("w2f"), AX.X, ALU.add)
                dve.tensor_reduce(sums[:, 1:2], P("w2f"), AX.X, ALU.add, apply_absolute_value=True).then_inc(sums_ready, 1)
                dve.wait_ge(totals_ready, 1)
                link(dve.tensor_scalar(totals[:, :], sums_ps[:, 0:2], 1.0 / (C * C), None, ALU.mult))
                dve.tensor_scalar(shifted[:, :], P("w2f"), totals[:, 0:1], None, ALU.subtract).then_inc(shifted_ready, 1)
                dve.wait_ge(sign_ready, 1)
                link(dve.tensor_tensor(weight[:, :], sign[:, :], P("w2f"), ALU.subtract))
                link(dve.tensor_tensor(weight[:, :], weight[:, :], P("w2f"), ALU.add))
                dve.tensor_scalar(weight[:, :], weight[:, :], totals[:, 1:2], None, ALU.mult).then_inc(weight_ready, 1)
                dve.sem_inc(y_used, FREE)
                dve.sem_inc(rounding, 1)
                with dve.Fori(0, NT // 2) as i:
                    dve.wait_ge(rounding, i * 10 + 1)
                    for u in range(2):
                        dve.wait_ge(y_ready, i * 2 + (u + 1 + FREE))
                        dve.tensor_scalar(level[u][:, :, :], y[u][:, :, :], 1.0, -1.0, ALU.min, ALU.max).then_inc(rounding, 1)
                    for k in range(5):
                        for u in range(2):
                            if k < 4:
                                dve.wait_ge(rounding, i * 10 + (2 * k + u + 1 + 1))
                            else:
                                dve.wait_ge(y_used, i * 2 + (u + 1 + FREE))
                            if k == 0:
                                done = dve.tensor_scalar(level[u][:, :, :], level[u][:, :, :], 7.0, ROUND, ALU.mult, ALU.add)
                            elif k == 1:
                                done = dve.tensor_scalar(level[u][:, :, :], level[u][:, :, :], ROUND, 1.0 / 7.0, ALU.subtract, ALU.mult)
                            elif k == 2:
                                done = dve.tensor_tensor(level[u][:, :, :], level[u][:, :, :], y[u][:, :, :], ALU.subtract)
                            elif k == 3:
                                done = dve.tensor_tensor(level[u][:, :, :], level[u][:, :, :], y[u][:, :, :], ALU.add)
                            else:
                                done = dve.tensor_tensor(tile(X, i * 2 + u), tile(X, i * 2 + u), level[u][:, :, :], ALU.add)
                            done.then_inc(y_used if k == 3 else rounding, 1)


def pruned(nc, P, XN, X):
    with Stage(nc, "pr") as s:
        XP = s.sb("xp", [128, B * PW, PW])
        acc = s.sb("acc", [128, H, W])
        H1 = s.sb("h1", [128, ROWS, W])
        diagonal = s.sb("diagonal", [128, 9, 128])
        weight = s.sb("weight", [128, B, C])
        shifted, inv, root, gain, shift = (s.sb(n, [128, 2]) for n in ("shifted", "inv", "root", "gain", "shift"))
        peak, keep = (s.sb(n, [128, 2, B]) for n in ("peak", "keep"))
        conv = [s.ps(f"conv{u}") for u in range(2)]
        zeroed, step, padded, inv_ready, root_ready, affine, diagonal_ready, conv_ready, conv_used, acc_ready, h1_ready = map(
            s.sem, ("zeroed", "step", "padded", "inv_ready", "root_ready", "affine", "diagonal_ready", "conv_ready", "conv_used", "acc_ready", "h1_ready"))
        weight_ready, mixed_ready = map(s.sem, ("weight_ready", "mixed_ready"))
        image = lambda tensor, b: tensor[:, b * H:(b + 1) * H, :]
        with nc.Block() as block:
            @block.gpsimd
            def _(pool):
                pool.memset(XP[:, :, :], 0.0).then_inc(zeroed, 1)

            @block.tensor
            def _(pe):
                pe.wait_ge(diagonal_ready, 1)
                pe.wait_ge(padded, 2)
                with pe.Fori(0, TB // 2) as i:
                    for u in range(2):
                        pe.wait_ge(conv_used, i * 2 + (u + 1))
                        for tap in range(9):
                            last = pe.matmul(rows48(conv[u][:, 0:T]), diagonal[:, tap, :],
                                             XP[:, ds(i * (2 * TR) + (PW + u * TR + tap // 3), TR), tap % 3:tap % 3 + W], start=tap == 0, stop=tap == 8)
                        last.then_inc(conv_ready, 1)
                for b in range(B):
                    pe.wait_ge(weight_ready, b + 1)
                    with pe.Fori(0, TB // 2) as i:
                        for u in range(2):
                            pe.wait_ge(conv_used, i * 2 + (TB * (b + 1) + u + 1))
                            pe.matmul(rows48(conv[u][:, 0:T]), weight[:, b, :], tile(H1, i * 2 + (b * TB + u)), start=True, stop=True).then_inc(mixed_ready, 1)

            @block.scalar
            def _(act):
                act.preload_act_table(ACT.Sqrt)
                act.sem_inc(conv_used, FREE)
                act.wait_ge(zeroed, 1)
                for b in range(B):
                    act.activation(XP[:, b * PW + 1:b * PW + 1 + H, 1:1 + W], image(XN, b), ACT.Copy).then_inc(padded, 1)
                act.wait_ge(inv_ready, 1)
                act.activation(root[:, :], inv[:, :], ACT.Sqrt).then_inc(root_ready, 1)
                act.wait_ge(affine, 1)
                with act.Fori(0, TB // 2) as i:
                    for u in range(2):
                        act.wait_ge(conv_ready, i * 2 + (u + 1))
                        act.activation(tile(H1, i * 2 + (TB + u)), rows48(conv[u][:, 0:T]), ACT.Relu, bias=shift[:, 0:1], scale=gain[:, 0:1]).then_inc(conv_used, 1)
                act.wait_ge(acc_ready, 1)
                act.activation(image(H1, 0), acc[:, :, :], ACT.Relu, bias=shift[:, 0:1], scale=gain[:, 0:1]).then_inc(h1_ready, 1)
                with act.Fori(0, NT // 2) as i:
                    for u in range(2):
                        act.wait_ge(mixed_ready, i * 2 + (u + 1))
                        act.activation(tile(H1, i * 2 + u), rows48(conv[u][:, 0:T]), ACT.Relu, bias=shift[:, 1:2], scale=gain[:, 1:2]).then_inc(conv_used, 1)

            @block.vector
            def _(dve):
                link = Chain(dve, step)
                for m in range(2):
                    last = dve.tensor_scalar(shifted[:, m:m + 1], P(f"bn{m + 1}_v"), 1e-5, None, ALU.add)
                link(last)
                dve.reciprocal(inv[:, :], shifted[:, :]).then_inc(inv_ready, 1)
                for tap in range(9):
                    last = dve.tensor_scalar(diagonal[:, tap, :], P("identity"), P("dw_w", first=tap, width=1), None, ALU.mult)
                last.then_inc(diagonal_ready, 1)
                dve.wait_ge(root_ready, 1)
                for m, bias in enumerate(("dw_b", "pw_b")):
                    link(dve.tensor_scalar(gain[:, m:m + 1], root[:, m:m + 1], P(f"bn{m + 1}_g"), None, ALU.mult))
                    link(dve.tensor_scalar(shift[:, m:m + 1], P(bias), P(f"bn{m + 1}_m"), None, ALU.subtract))
                    link(dve.tensor_scalar(shift[:, m:m + 1], shift[:, m:m + 1], gain[:, m:m + 1], P(f"bn{m + 1}_b"), ALU.mult, ALU.add))
                dve.sem_inc(affine, 1)
                dve.wait_ge(padded, 1)
                link(dve.tensor_scalar(acc[:, :, :], XP[:, 0:H, 0:W], P("dw_w", width=1), None, ALU.mult))
                for tap in range(1, 9):
                    done = dve.scalar_tensor_tensor(acc[:, :, :], XP[:, tap // 3:tap // 3 + H, tap % 3:tap % 3 + W], P("dw_w", first=tap, width=1),
                                                    acc[:, :, :], ALU.mult, ALU.add)
                    if tap < 8:
                        link(done)
                done.then_inc(acc_ready, 1)
                for b in range(B):
                    if b == 0:
                        dve.wait_ge(h1_ready, 1)
                    else:
                        dve.wait_ge(conv_used, TB + FREE)
                    link(dve.tensor_reduce(peak[:, 0, b:b + 1], image(H1, b).rearrange("p r w -> p (r w)"), AX.X, ALU.max))
                    link(dve.tensor_scalar(keep[:, 0, b:b + 1], peak[:, 0, b:b + 1], 4.0, None, ALU.is_ge))
                    dve.tensor_scalar(weight[:, b, :], P("pw"), keep[:, 0, b:b + 1], None, ALU.mult).then_inc(weight_ready, 1)
                for b in range(B):
                    dve.wait_ge(conv_used, TB * (b + 2) + FREE)
                    link(dve.tensor_reduce(peak[:, 1, b:b + 1], image(H1, b).rearrange("p r w -> p (r w)"), AX.X, ALU.max))
                    link(dve.tensor_scalar(keep[:, 1, b:b + 1], peak[:, 1, b:b + 1], 0.001, None, ALU.is_ge))
                    dve.scalar_tensor_tensor(image(X, b), image(H1, b), keep[:, 1, b:b + 1], image(X, b), ALU.mult, ALU.add)


def build(nc, x, params, masks, query_side, wqkv_in, wout_in, w1_0, w2_0, bias_0, w1_1, w2_1, bias_1, w13_3, w2_3, out,
          first=0, last=8):
    HID = E * 4 * 128
    HID3 = E * 2 * 128
    tokens = nc.dram_tensor("tokens", (NTOK, ROW), F32, kind="Internal").ap()
    targets = nc.dram_tensor("targets", (2 * NTOK + 2 * GROUP * 128, C), F32, kind="Internal").ap()
    with ExitStack() as ctx:
        sb = lambda name, shape, dt=F32: ctx.enter_context(nc.sbuf_tensor(name, shape, dt))
        X = sb("X", [128, ROWS, W])
        U = sb("U", [128, ROWS, W])
        params_sb = sb("params_sb", [128, PARAMS.width])
        loaded, conv_loaded, loaded_0, loaded_1, loaded_3 = map(
            nc.alloc_semaphore, ("loaded", "conv_loaded", "loaded_0", "loaded_1", "loaded_3"))

        def P(name, rows=128, first=0, width=None):
            at, w = PARAMS[name]
            return params_sb[0:rows, at + first:at + first + (width or w - first)]

        def images(tensor):
            return tensor[:, :, :].rearrange("p (b r) w -> p b (r w)", b=B)

        with nc.Block() as block:
            @block.sync
            def _(sp):
                sp.dma_start(images(X), x.rearrange("b c h w -> c b (h w)")).then_inc(loaded, 16)
                sp.dma_start(params_sb[:, :], params).then_inc(loaded, 16)
                sp.wait_ge(loaded, 32)

        def halves(store, width):
            return store[:, 0:width], store[:, width:2 * width]

        if first <= 0 < last:
            with ExitStack() as layer:
                lsb = lambda name, shape: layer.enter_context(nc.sbuf_tensor(name, shape, F32))
                Q = lsb("Q", [128, ROWS, W])
                KP = lsb("KP", [128, B * PK, PK])
                VP = lsb("VP", [128, B * PK, PK])
                wout = lsb("wout", [128, 9, C])
                flat = lambda w: w[:, :, :].rearrange("p a b -> p (a b)")
                wqkv = flat(KP)[:, 0:27 * C]
                layer_norm(nc, P, "ln0", X, 1e-6, U, loads=[(wqkv, wqkv_in, conv_loaded), (flat(wout), wout_in, conv_loaded)])
                with ExitStack() as split:
                    high, low, wqkv_high, wqkv_low = (split.enter_context(nc.sbuf_tensor(name, shape, F32R)) for name, shape in (
                        ("high", [128, B * PW, PW]), ("low", [128, B * PW, PW]), ("wqkv_high", [128, 9, 3 * C]), ("wqkv_low", [128, 9, 3 * C])))
                    group_norm(nc, P, U, high, low, Q, wqkv, flat(wqkv_high), flat(wqkv_low), conv_loaded)
                    qkv(nc, P, high, low, wqkv_high, wqkv_low, Q, KP, VP)
                attended = lsb("attended", [128, B * PW, PW])
                neighbourhood(nc, P, Q, KP, VP, masks, query_side, attended)
                out_conv(nc, P, attended, wout, U, X)

        store_a = sb("store_a", [128, 2 * HID])
        until_3 = ctx.enter_context(ExitStack())
        store_b = until_3.enter_context(nc.sbuf_tensor("store_b", [128, 2 * HID], F32))
        biases = until_3.enter_context(nc.sbuf_tensor("biases", [128, E * (512 + C)], F32))

        def mixture(name, XF, logits, bias, top, renormalise, store, act_func, weights_loaded, extra=None, gated_unit=False):
            with ExitStack() as tables:
                token_of, target_of, second_of = (tables.enter_context(nc.sbuf_tensor(f"{name}_{n}", [128, TILES[top]], F32))
                                                  for n in ("token_of", "target_of", "second_of"))
                expert_codes = tables.enter_context(nc.sbuf_tensor(f"{name}_expert_codes", [1, TILES[top] // GROUP], I32))
                dispatch(nc, P, f"{name}d", XF, logits, bias, top, renormalise, tokens, token_of, target_of, second_of, expert_codes)
                experts(nc, P, f"{name}e", tokens, token_of, target_of, second_of, expert_codes, store[0], act_func, biases, store[1],
                        targets, weights_loaded, gated_unit, weighted=top == 2)
            combine(nc, P, f"{name}c", targets, top, X, extra)

        def layer3_weights():
            return [(store_a[:, 0:2 * HID3], w13_3, loaded_3), (store_a[:, 2 * HID3:3 * HID3], w2_3, loaded_3)]

        def layer1_weights():
            return [(store_b[:, 0:HID], w1_1, loaded_1), (store_b[:, HID:2 * HID], w2_1, loaded_1)]

        if first <= 1 < last:
            with nc.sbuf_tensor("V", [128, ROWS, W], F32) as V, nc.psum_tensor("logits_1", [128, 512], F32) as logits:
                into, out_of = halves(store_a, HID)
                layer_norm(nc, P, "ln1", X, 1e-5, U, second=(V, 1e-5),
                           loads=[(into, w1_0, loaded_0), (out_of, w2_0, loaded_0), (biases[:, :], bias_0, loaded_0)] + layer1_weights(),
                           gate=(P("gate_0"), logits))
                mixture("m1", V, logits, None, 2, False, (into, out_of), ACT.Gelu, (loaded_0, 48), extra=U)
        if first <= 2 < last:
            layer_norm(nc, P, "ln2", X, 1e-6, U)
            attention(nc, P, U, X)
        if first <= 3 < last:
            with nc.psum_tensor("logits_3", [128, 512], F32) as logits:
                layer_norm(nc, P, "ln3", X, 1e-5, U, loads=[(biases[:, :], bias_1, loaded_1)]
                           + layer3_weights() + (layer1_weights() if first > 1 else []), gate=(P("gate_1"), logits))
                mixture("m3", U, logits, P("br"), 1, False, halves(store_b, HID), ACT.Gelu, (loaded_1, 48))
        until_3.close()
        if first <= 4 < last:
            layer_norm(nc, P, "ln4", X, 1e-6, U)
            dynamic_conv(nc, P, U, X)
        if first <= 5 < last:
            layer_norm(nc, P, "ln5", X, 1e-5, U)
            quantised(nc, P, U, X)
        if first <= 6 < last:
            layer_norm(nc, P, "ln6", X, 1e-6, U)
            pruned(nc, P, U, X)
        if first <= 7 < last:
            with nc.psum_tensor("logits_7", [128, 512], F32) as logits:
                layer_norm(nc, P, "ln7", X, 1e-5, U, loads=layer3_weights() if first > 3 else [], gate=(P("gate_3"), logits))
                mixture("m7", U, logits, None, 2, True, (store_a[:, 0:2 * HID3], store_a[:, 2 * HID3:3 * HID3]), ACT.Silu,
                        (loaded_3, 32), gated_unit=True)
        with Stage(nc, "store") as s:
            stored = s.sem("stored")
            with nc.Block() as block:
                @block.sync
                def _(sp):
                    sp.dma_start(out.rearrange("b c h w -> c b (h w)"), images(X)).then_inc(stored, 16)
                    sp.wait_ge(stored, 16)


def _pack(given):
    import numpy as np
    f = np.float32
    groups = lambda n: np.kron(np.eye(128 // n, dtype=f), np.ones((n, n), f))
    head_of = np.kron(np.eye(NH, dtype=f), np.ones((DH, 1), f))
    tap5, tap3 = np.zeros((4, 32, 10), f), np.zeros((4, 32, 10), f)
    tap5[:, :, 0:5] = 1
    tap5[0, :, 5:10] = 1
    for row in (0, 2, 4):
        tap3[0, :, row] = tap3[2, :, row] = tap3[0, :, 5 + row] = 1

    def column(a):
        return np.asarray(a).reshape(-1, 1)

    def every(a):
        return np.repeat(np.asarray(a).reshape(1, -1), 128, axis=0)

    def below(a, *at):
        out = np.zeros((128, np.asarray(a).reshape(np.shape(a)[0], -1).shape[1]), f)
        for row in at:
            out[row:row + np.shape(a)[0]] = np.asarray(a).reshape(np.shape(a)[0], -1)
        return out

    def taps5(a):
        a = np.asarray(a).reshape(5, 5)
        out = np.zeros((4, 32, 10), f)
        for j in range(4):
            out[j, :, 0:5] = a[:, j]
        out[:, :, 5:10] = a[:, 4]
        return out.reshape(128, 10)

    def taps3(a):
        a = np.asarray(a).reshape(3, 3)
        out = np.zeros((5, 5), f)
        for r in range(3):
            for c in range(3):
                out[2 * r, 2 * c] = a[r, c]
        return taps5(out)

    g = given
    four = (0, 32, 64, 96)
    fuse = np.asarray(g["L2_conv_fuse_w"])[:, :, 0, 0].T
    front = np.zeros((128, 1), f)
    front[0:2] = 1
    values = {
        "identity": np.eye(128, dtype=f), "ones": np.ones((128, 128), f),
        "group_mean": groups(8) / 8, "head_of": head_of,
        "same_query": np.tile(np.eye(QB * QB, dtype=f), (2, 1)),
        "earlier": np.triu(np.ones((128, 128), f), 1),
        "token_code": np.concatenate([np.arange(1, NTOK // 2 + 1), -np.arange(1, NTOK // 2 + 1)]).astype(f).reshape(NC, 128).T,
        "tile_number": every(np.arange(TILES[2], dtype=f)), "lane": every(np.arange(128, dtype=f)),
        "unused_target": 2 * NTOK + 1 + (np.arange(TILES[2]) % (2 * GROUP)) * 128 + np.arange(128).reshape(128, 1),
        "tap5": tap5.reshape(128, 10), "tap3": tap3.reshape(128, 10),
        "gn_w": column(g["L0_conv_gn_w"]), "gn_b": column(g["L0_conv_gn_b"]), "qkv_b": np.asarray(g["L0_conv_qkv_b"]).reshape(3, C).T,
        "scale": every(g["L0_conv_scale"]), "out_b": column(g["L0_conv_out_b"]),
        "ln_g": column(g["L0_ffn_ln_g"]), "ln_b": column(g["L0_ffn_ln_b"]),
        "gate_0": g["L0_ffn_gate_w"],
        "bv": column(g["L1_conv_bv"]), "bq": below(g["L1_conv_bq"], 32, 64, 96), "bk": below(g["L1_conv_bk"], 32, 64, 96) + front,
        "wq": below(g["L1_conv_Wq"], 32, 64, 96).T, "wk": below(g["L1_conv_Wk"], 32, 64, 96).T, "wv": np.asarray(g["L1_conv_Wv"]).T,
        "gate_1": g["L1_ffn_Wr"], "br": every(g["L1_ffn_br"]),
        "conv_w": np.tile(np.asarray(g["L2_conv_conv_w"])[:, :, 0, 0].T, (1, 4)), "conv_b": below(g["L2_conv_conv_b"], *four),
        "k_w": every(g["L2_conv_conv_k_w"]), "k_b": every(g["L2_conv_conv_k_b"]),
        "k2_w": every(g["L2_conv_conv_k2_w"]), "k2_b": every(g["L2_conv_conv_k2_b"]),
        "kernel_w": taps5(g["L2_conv_conv_kernel_w"]), "kernel_b": taps5(g["L2_conv_conv_kernel_b"]),
        "kernel2_w": taps3(g["L2_conv_conv_kernel2_w"]), "kernel2_b": taps3(g["L2_conv_conv_kernel2_b"]),
        "fuse1": below(fuse[0:32], *four), "fuse2": below(fuse[32:64], *four),
        "adap_b": below(g["L2_conv_adap_bias"], 0), "atrous_b": below(g["L2_conv_atrous_bias"], 0), "fuse_b": column(g["L2_conv_fuse_b"]),
        "w2f": g["L2_ffn_weight"], "b2f": column(g["L2_ffn_bias"]),
        "dw_w": np.asarray(g["L3_conv_dw_w"]).reshape(128, 9), "dw_b": column(g["L3_conv_dw_b"]),
        "pw": np.asarray(g["L3_conv_pw_w"])[:, :, 0, 0].T, "pw_b": column(g["L3_conv_pw_b"]), "gate_3": g["L3_ffn_router_w"],
    }
    for n in (1, 2):
        for part in "gbmv":
            values[f"bn{n}_{part}"] = column(g[f"L3_conv_bn{n}_{part}"])
    packed = np.zeros((128, PARAMS.width), f)
    for name, (at, width) in PARAMS.at.items():
        packed[:, at:at + width] = np.asarray(values[name])
    return packed


def _window_masks():
    import numpy as np
    outside = np.zeros((NBLK, QB, WIN), np.float32)
    for block in range(NBLK):
        for y in range(QB):
            start = min(max(block * QB + y - 3, 0), H - 7) - (block * QB - 3)
            outside[block, y] = MASKED
            outside[block, y, start:start + 7] = 0
    keys = np.zeros((1 + 2 * QB, NBLK, NBLK, WIN, WIN), np.float32)
    keys[0] = 1
    for y in range(QB):
        keys[1 + y] = outside[:, y][:, None, :, None]
        keys[1 + QB + y] = outside[:, y][None, :, None, :]
    queries = np.zeros((1 + 2 * QB, NH, QB, QB), np.float32)
    for y in range(QB):
        queries[1 + y, :, y, :] = 1
        queries[1 + QB + y, :, :, y] = 1
    return (keys.reshape(1 + 2 * QB, NBLK * NBLK, WIN * WIN).astype("bfloat16"), queries.reshape(1 + 2 * QB, NH, QB * QB).astype("bfloat16"))


def _inputs(given):
    import numpy as np
    g = {name: np.asarray(a) for name, a in given.items()}

    def conv(a):
        return a.transpose(1, 2, 3, 0).reshape(C, -1)

    def into(a):
        return a.transpose(1, 0, 2).reshape(C, -1)

    def out_of(a):
        return a.reshape(E, -1, 128, C).transpose(2, 0, 1, 3).reshape(128, -1)

    masks, query_side = _window_masks()
    def bias(b1, b2):
        return np.repeat(np.concatenate([b1.reshape(1, -1), b2.reshape(1, -1)], axis=1), 128, axis=0)

    arrays = {
        "x": g["x"], "params": _pack(g),
        "masks": masks, "query_side": query_side,
        "wqkv": conv(g["L0_conv_qkv_w"]), "wout": conv(g["L0_conv_out_w"]),
        "w1_0": into(g["L0_ffn_w1"]), "w2_0": out_of(g["L0_ffn_w2"]), "bias_0": bias(g["L0_ffn_b1"], g["L0_ffn_b2"]),
        "w1_1": into(g["L1_ffn_W1"]), "w2_1": out_of(g["L1_ffn_W2"]), "bias_1": bias(g["L1_ffn_b1"], g["L1_ffn_b2"]),
        "w13_3": into(np.concatenate([g["L3_ffn_w1"], g["L3_ffn_w3"]], axis=2)), "w2_3": out_of(g["L3_ffn_w2"]),
    }
    return {f"in_{name}": np.ascontiguousarray(a) for name, a in arrays.items()}


def kernel(**given):
    import concourse.bacc as bacc
    from concourse.bass_utils import run_bass_kernel_spmd

    arrays = _inputs(given)
    nc = bacc.Bacc("TRN2", target_bir_lowering=False, num_devices=1)
    tensors = [nc.dram_tensor(name, a.shape, mybir.dt.from_np(a.dtype), kind="ExternalInput").ap() for name, a in arrays.items()]
    out = nc.dram_tensor("out", arrays["in_x"].shape, F32, kind="ExternalOutput").ap()
    build(nc, *tensors, out)
    return run_bass_kernel_spmd(nc, [arrays], core_ids=[0]).results[0]["out"]
```
